# Optimizing a Trainium2 kernel written in Bass

```python
import numpy as np
import jax
import jax.numpy as jnp

def _softmax(x, axis=-1):
    return jax.nn.softmax(x, axis=axis)

def _gelu(x):
    return jax.nn.gelu(x, approximate=True)

def _silu(x):
    return jax.nn.silu(x)

def _sigmoid(x):
    return jax.nn.sigmoid(x)

def _layernorm(x, axis=-1, eps=1e-05):
    m = jnp.mean(x, axis=axis, keepdims=True)
    v = jnp.var(x, axis=axis, keepdims=True)
    return (x - m) / jnp.sqrt(v + eps)

def _scatter_add(tgt, idx, src, axis=0):
    return tgt.at[idx].add(src)

def _segment_sum(src, seg, n):
    return jax.ops.segment_sum(src, seg, n)
kernel_name = 'mk_gps_d1_gnn_r8_1631fa'

def setup_inputs(seed: int=0):
    np.random.seed(seed)
    _w = jnp.asarray

    def _rec_inputs():
        import jax
        import jax.numpy as jnp
        _gk = jax.random.key(seed)
        x = -8.776e-05 + 1 * jax.random.normal(jax.random.fold_in(_gk, 1), (2500, 256), jnp.float32)
        src = jax.random.randint(jax.random.fold_in(_gk, 2), (80000,), 0, 2500, jnp.int32)
        dst = jax.random.randint(jax.random.fold_in(_gk, 3), (80000,), 0, 2500, jnp.int32)
        _o = jnp.argsort(dst, stable=True)
        src = src[_o]
        dst = dst[_o]
        return (x, src, dst)
    x, src, dst = _rec_inputs()

    def _L0_gnn_setup():
        import jax, jax.numpy as jnp
        import numpy as np
        N_NODES = 2500
        key = jax.random.key(seed)
        k1, k2, k3, k4 = jax.random.split(key, 4)
        d = 256
        E = 40000
        x = jax.random.normal(k1, (N_NODES, d), dtype=jnp.float32)
        edge_index = jax.random.randint(k2, (2, E), 0, N_NODES, dtype=jnp.int64)
        limit = float(np.sqrt(6.0 / (d + d)))
        W_l = jax.random.uniform(k3, (d, d), dtype=jnp.float32, minval=-limit, maxval=limit)
        W_r = jax.random.uniform(k4, (d, d), dtype=jnp.float32, minval=-limit, maxval=limit)
        b_r = jnp.zeros((d,), dtype=jnp.float32)
        return {'x': x, 'edge_index': edge_index, 'W_l': W_l, 'W_r': W_r, 'b_r': b_r}
    _L0_gnn_all = _L0_gnn_setup()
    _L0_gnn_in = {k: v for k, v in _L0_gnn_all.items() if k in ('W_l', 'W_r', 'b_r')}
    del _L0_gnn_all

    def _L0_mix_setup():
        import jax, jax.numpy as jnp
        import numpy as np
        D_MODEL = 256
        NHEAD = 8
        D_HEAD = D_MODEL // NHEAD
        DIM_FF = 1024
        B, L = (4, 2048)
        LN_EPS = 1e-05

        def _layernorm(x, g, b):
            mu = jnp.mean(x, axis=-1, keepdims=True)
            var = jnp.mean((x - mu) ** 2, axis=-1, keepdims=True)
            return (x - mu) * jax.lax.rsqrt(var + LN_EPS) * g + b

        def _phi(x):
            return jnp.where(x > 0, x + 1.0, jnp.exp(x))
        key = jax.random.key(seed)
        ks = jax.random.split(key, 16)
        s_in = 1.0 / np.sqrt(D_MODEL)
        s_ff = 1.0 / np.sqrt(DIM_FF)
        inp = {'x': jax.random.normal(ks[0], (B, L, D_MODEL), dtype=jnp.float32), 'Wq': jax.random.normal(ks[1], (D_MODEL, D_MODEL), dtype=jnp.float32) * s_in, 'bq': jnp.zeros((D_MODEL,), jnp.float32), 'Wk': jax.random.normal(ks[2], (D_MODEL, D_MODEL), dtype=jnp.float32) * s_in, 'bk': jnp.zeros((D_MODEL,), jnp.float32), 'Wv': jax.random.normal(ks[3], (D_MODEL, D_MODEL), dtype=jnp.float32) * s_in, 'bv': jnp.zeros((D_MODEL,), jnp.float32), 'Wo': jax.random.normal(ks[4], (D_MODEL, D_MODEL), dtype=jnp.float32) * s_in, 'bo': jnp.zeros((D_MODEL,), jnp.float32), 'W1': jax.random.normal(ks[5], (D_MODEL, DIM_FF), dtype=jnp.float32) * s_in, 'b1': jnp.zeros((DIM_FF,), jnp.float32), 'W2': jax.random.normal(ks[6], (DIM_FF, D_MODEL), dtype=jnp.float32) * s_ff, 'b2': jnp.zeros((D_MODEL,), jnp.float32), 'ln1_g': jnp.ones((D_MODEL,), jnp.float32), 'ln1_b': jnp.zeros((D_MODEL,), jnp.float32), 'ln2_g': jnp.ones((D_MODEL,), jnp.float32), 'ln2_b': jnp.zeros((D_MODEL,), jnp.float32)}
        return inp
    _L0_mix_all = _L0_mix_setup()
    _L0_mix_in = {k: v for k, v in _L0_mix_all.items() if k in ('Wq', 'bq', 'Wk', 'bk', 'Wv', 'bv', 'Wo', 'bo', 'W1', 'b1', 'W2', 'b2', 'ln1_g', 'ln1_b', 'ln2_g', 'ln2_b')}
    del _L0_mix_all

    def _L0_ffn_setup():
        import jax, jax.numpy as jnp
        import numpy as np
        B, S, D = (8, 512, 256)
        H = 4 * D
        CAPACITY = 0.5
        key = jax.random.key(seed)
        ks = jax.random.split(key, 6)
        x = jax.random.normal(ks[0], (B, S, D), dtype=jnp.float32)
        attention_mask = jnp.zeros((B, 1, 1, S), dtype=jnp.float32)
        wr = jax.random.normal(ks[1], (D, 1), dtype=jnp.float32) * 0.02
        br = jnp.zeros((1,), dtype=jnp.float32)
        w1 = jax.random.normal(ks[2], (D, H), dtype=jnp.float32) * 0.02
        b1 = jnp.zeros((H,), dtype=jnp.float32)
        w2 = jax.random.normal(ks[3], (H, D), dtype=jnp.float32) * 0.02
        b2 = jnp.zeros((D,), dtype=jnp.float32)
        return {'x': x, 'attention_mask': attention_mask, 'wr': wr, 'br': br, 'w1': w1, 'b1': b1, 'w2': w2, 'b2': b2}
    _L0_ffn_all = _L0_ffn_setup()
    _L0_ffn_in = {k: v for k, v in _L0_ffn_all.items() if k in ('attention_mask', 'wr', 'br', 'w1', 'b1', 'w2', 'b2')}
    del _L0_ffn_all
    return {'x': x, 'src': src, 'dst': dst, 'L0_gnn_W_l': _L0_gnn_in['W_l'], 'L0_gnn_W_r': _L0_gnn_in['W_r'], 'L0_gnn_b_r': _L0_gnn_in['b_r'], 'L0_mix_Wq': _L0_mix_in['Wq'], 'L0_mix_bq': _L0_mix_in['bq'], 'L0_mix_Wk': _L0_mix_in['Wk'], 'L0_mix_bk': _L0_mix_in['bk'], 'L0_mix_Wv': _L0_mix_in['Wv'], 'L0_mix_bv': _L0_mix_in['bv'], 'L0_mix_Wo': _L0_mix_in['Wo'], 'L0_mix_bo': _L0_mix_in['bo'], 'L0_mix_W1': _L0_mix_in['W1'], 'L0_mix_b1': _L0_mix_in['b1'], 'L0_mix_W2': _L0_mix_in['W2'], 'L0_mix_b2': _L0_mix_in['b2'], 'L0_mix_ln1_g': _L0_mix_in['ln1_g'], 'L0_mix_ln1_b': _L0_mix_in['ln1_b'], 'L0_mix_ln2_g': _L0_mix_in['ln2_g'], 'L0_mix_ln2_b': _L0_mix_in['ln2_b'], 'L0_ffn_attention_mask': _L0_ffn_in['attention_mask'], 'L0_ffn_wr': _L0_ffn_in['wr'], 'L0_ffn_br': _L0_ffn_in['br'], 'L0_ffn_w1': _L0_ffn_in['w1'], 'L0_ffn_b1': _L0_ffn_in['b1'], 'L0_ffn_w2': _L0_ffn_in['w2'], 'L0_ffn_b2': _L0_ffn_in['b2']}

def reference(x, src, dst, L0_gnn_W_l, L0_gnn_W_r, L0_gnn_b_r, L0_mix_Wq, L0_mix_bq, L0_mix_Wk, L0_mix_bk, L0_mix_Wv, L0_mix_bv, L0_mix_Wo, L0_mix_bo, L0_mix_W1, L0_mix_b1, L0_mix_W2, L0_mix_b2, L0_mix_ln1_g, L0_mix_ln1_b, L0_mix_ln2_g, L0_mix_ln2_b, L0_ffn_attention_mask, L0_ffn_wr, L0_ffn_br, L0_ffn_w1, L0_ffn_b1, L0_ffn_w2, L0_ffn_b2):
    import jax
    import jax.numpy as jnp

    def _L0_gnn_ref(x, edge_index, W_l, W_r, b_r):
        import jax, jax.numpy as jnp
        import numpy as np
        N_NODES = 2500
        src, dst = (edge_index[0], edge_index[1])
        messages = x[src]
        sums = jax.ops.segment_sum(messages, dst, num_segments=N_NODES)
        counts = jax.ops.segment_sum(jnp.ones_like(dst, dtype=x.dtype), dst, num_segments=N_NODES)
        aggr = sums / jnp.maximum(counts, 1.0)[:, None]
        out = aggr @ W_l.T + x @ W_r.T + b_r
        return out

    def _L0_mix_ref(x, Wq, bq, Wk, bk, Wv, bv, Wo, bo, W1, b1, W2, b2, ln1_g, ln1_b, ln2_g, ln2_b):
        import jax, jax.numpy as jnp
        import numpy as np
        D_MODEL = 256
        NHEAD = 8
        D_HEAD = D_MODEL // NHEAD
        DIM_FF = 1024
        B, L = (4, 2048)
        LN_EPS = 1e-05

        def _layernorm(x, g, b):
            mu = jnp.mean(x, axis=-1, keepdims=True)
            var = jnp.mean((x - mu) ** 2, axis=-1, keepdims=True)
            return (x - mu) * jax.lax.rsqrt(var + LN_EPS) * g + b

        def _phi(x):
            return jnp.where(x > 0, x + 1.0, jnp.exp(x))
        Bq, Lq, _ = x.shape
        q = (x @ Wq + bq).reshape(Bq, Lq, NHEAD, D_HEAD)
        k = (x @ Wk + bk).reshape(Bq, Lq, NHEAD, D_HEAD)
        v = (x @ Wv + bv).reshape(Bq, Lq, NHEAD, D_HEAD)
        q_phi = _phi(q)
        k_phi = _phi(k)
        kv = jnp.einsum('blhd,blhe->bhde', k_phi, v)
        k_sum = k_phi.sum(axis=1)
        z = 1.0 / (jnp.einsum('blhd,bhd->blh', q_phi, k_sum) + 1e-06)
        out = jnp.einsum('blhd,bhde,blh->blhe', q_phi, kv, z)
        out = out.reshape(Bq, Lq, D_MODEL) @ Wo + bo
        x = _layernorm(x + out, ln1_g, ln1_b)
        ff = jax.nn.relu(x @ W1 + b1) @ W2 + b2
        x = _layernorm(x + ff, ln2_g, ln2_b)
        return x

    def _L0_ffn_ref(x, attention_mask, wr, br, w1, b1, w2, b2):
        import jax, jax.numpy as jnp
        import numpy as np
        B, S, D = (8, 512, 256)
        H = 4 * D
        CAPACITY = 0.5
        b, s, d = x.shape
        weights = (jnp.einsum('bsd,do->bso', x, wr) + br)[..., 0]
        k = max(1, int(CAPACITY * s))
        kk = k - 1 if k > 1 else 1
        _, idx = jax.lax.top_k(weights, k)
        sel_idx = idx[:, :kk]
        sel = jnp.take_along_axis(x, sel_idx[:, :, None], axis=1)
        h = jax.nn.gelu(jnp.einsum('bkd,dh->bkh', sel, w1) + b1)
        y = jnp.einsum('bkh,hd->bkd', h, w2) + b2
        w_sel = jnp.take_along_axis(weights, sel_idx, axis=1)
        y = y * w_sel[..., None]
        batch_idx = jnp.arange(b)[:, None]
        processed = jnp.zeros_like(x).at[batch_idx, sel_idx].set(y)
        return processed + x
    edge_index = jnp.stack([src, dst])
    xn = _layernorm(x, axis=-1)
    x = x + _L0_gnn_ref(xn, edge_index, L0_gnn_W_l, L0_gnn_W_r, L0_gnn_b_r) + _L0_mix_ref(xn[None], L0_mix_Wq, L0_mix_bq, L0_mix_Wk, L0_mix_bk, L0_mix_Wv, L0_mix_bv, L0_mix_Wo, L0_mix_bo, L0_mix_W1, L0_mix_b1, L0_mix_W2, L0_mix_b2, L0_mix_ln1_g, L0_mix_ln1_b, L0_mix_ln2_g, L0_mix_ln2_b)[0]
    x = x + _L0_ffn_ref(_layernorm(x, axis=-1)[None], L0_ffn_attention_mask, L0_ffn_wr, L0_ffn_br, L0_ffn_w1, L0_ffn_b1, L0_ffn_w2, L0_ffn_b2)[0]
    return x

_drawn_inputs = setup_inputs


def setup_inputs(seed=0):
    import zlib

    import numpy as np

    out = dict(_drawn_inputs(seed))
    spreads = {'L0_gnn_b_r': (0.0, 0.1),
     'L0_mix_bq': (0.0, 0.8),
     'L0_mix_bk': (0.0, 0.8),
     'L0_mix_bv': (0.0, 0.1),
     'L0_mix_bo': (0.0, 0.1),
     'L0_mix_b1': (0.0, 0.295),
     'L0_mix_b2': (0.0, 0.1),
     'L0_mix_ln1_g': (1.0, 0.2),
     'L0_mix_ln1_b': (0.0, 0.1),
     'L0_mix_ln2_g': (1.0, 0.2),
     'L0_mix_ln2_b': (0.0, 0.1),
     'L0_ffn_b1': (0.0, 0.8),
     'L0_ffn_b2': (0.0, 0.8)}
    factors = {'L0_mix_Wq': 8.0,
     'L0_mix_Wk': 8.0,
     'L0_mix_Wv': 5.86,
     'L0_ffn_wr': 6.62,
     'L0_ffn_w1': 7.356,
     'L0_ffn_w2': 6.913}
    for name, (base, spread) in spreads.items():
        noise = np.random.default_rng([zlib.crc32(name.encode()), seed]).standard_normal(out[name].shape)
        drawn = base * np.exp(spread * noise) if base else spread * noise
        out[name] = jnp.asarray(drawn.astype(out[name].dtype))
    for name, factor in factors.items():
        out[name] = (out[name] * factor).astype(out[name].dtype)
    return out
```

```python
import concourse.bass as bass
from concourse import mybir
from contextlib import ExitStack

P = 128
N = 2500
D = 256
DK = D // P
H = 1024
HK = H // P
HEADS = 8
DH = D // HEADS
HPC = P // DH
E = 80000
NT = -(-N // P)
LAST = N - (NT - 1) * P
ET = E // P
W = 8
WPB = P // W
NW = NT * WPB
WG = 4
GW = NW // WG
TPW = 3
RUN = TPW * P
ER = 32
KEYS = W * NT
PPB = WPB // 2
TPP = 2 * TPW
EP = 125
EK = E // ER // EP
EPS = 1e-5
LO = 2.0 ** 11
KEEP = int(0.5 * N) - 1
ROWS = ["bk", "bv", "bo", "g1", "c1", "b2", "g2", "c2", "bg", "wr", "fb2"]
CW = P + HPC


class Tile:

    def __init__(self, n, j=None):
        self.n, self.j, self.par = n, j, n % 2
        self.i = n if j is None else j * 2 + n
        self.half = n // 2 if j is None else j + n // 2

    def back(self, k):
        return Tile(self.n - k, self.j)

    def real(self):
        return self.j is not None or 0 <= self.n < NT

    def done(self, per=1):
        if self.j is None:
            return per * max(0, min(self.n + 1, NT))
        return self.i * per + per


def steps(eng, total, body):
    for n in range(3):
        body(Tile(n))
    with eng.Fori(0, 8) as j:
        body(Tile(3, j))
        body(Tile(4, j))
    for n in range(19, total):
        body(Tile(n))


def wait(eng, sem, value):
    if not isinstance(value, int) or value > 0:
        eng.wait_ge(sem, value)


def wait_apart(eng, sem, value, met):
    if not isinstance(value, int):
        value = eng.snap(eng.to_reg(value))
    eng.wait_ge(*met)
    eng.wait_ge(sem, value)


class Chain:

    def __init__(self, eng, sem, per, tile=0):
        self.eng, self.sem, self.per, self.base, self.n = eng, sem, per, tile * per, 0

    def __call__(self, ins, met=None):
        self.n += 1
        assert self.n <= self.per
        ins.then_inc(self.sem, 1)
        if met:
            wait_apart(self.eng, self.sem, self.base + self.n, met)
        else:
            self.eng.wait_ge(self.sem, self.base + self.n)


def gps_layer(nc, x, src, dst, w_l, w_r, w_q, w_k, w_v, w_o, w_1, w_2, f_1, f_2, rows, cols, out,
              xq_d, xg_d, w_d):
    f32, f16, i32 = mybir.dt.float32, mybir.dt.float16, mybir.dt.int32
    ALU, ACT = mybir.AluOpType, mybir.ActivationFunctionType
    V, G, A, T = nc.vector, nc.gpsimd, nc.scalar, nc.tensor
    NR = len(ROWS)
    ctx = ExitStack()
    with ctx:
        def sb(name, shape, dt=f32):
            return ctx.enter_context(nc.sbuf_tensor(name, shape, dt))

        def over(held, at, shape, dt=f32):
            size, n = {f32: 4, i32: 4, f16: 2}[dt], 1
            for k in shape[1:]:
                n *= k
            end = at + -(-n * size // 4)
            v = held[0:shape[0], at:end].bitcast(dt)[:, 0:n] if dt != f32 else held[0:shape[0], at:end]
            if len(shape) == 3:
                v = v.rearrange("p (a b) -> p a b", a=shape[1])
            if len(shape) == 4:
                v = v.rearrange("p (a b c) -> p a b c", a=shape[1], b=shape[2])
            return v, end

        def sem(name):
            return ctx.enter_context(nc.semaphore(name))

        xn = sb("xn", [P, NT, D])
        xn16 = sb("xn16", [P, NT, 2 * D], f16)
        acc = sb("acc", [P, NT, D])
        dacc = sb("dacc", [P, NT])
        yw_m = sb("yw", [P, NT * D])
        yw = yw_m[:, :].rearrange("p (c f) -> p c f", c=NT)
        wo = sb("wo", [P, DK, D])
        wl = sb("wl", [P, DK, D])
        wrr = sb("wrr", [P, DK, D])
        w1 = sb("w1", [P, DK, H])
        w2 = sb("w2", [P, HK, D])
        f1 = sb("f1", [P, DK, H])
        f2 = sb("f2", [P, HK, D])
        rowt = sb("rowt", [P, NR * D + 1])
        colt = sb("colt", [P, DK + 2 * HK])
        ident = sb("ident", [P, P])
        same_head = sb("same_head", [P, P])
        head_of = sb("head_of", [P, HPC])
        before = sb("before", [P, P])
        iota = sb("iota", [P, KEYS, TPP], f16)
        one16 = sb("one16", [P, 1], f16)
        ones = sb("ones", [P, P])
        scale_lo = sb("scale_lo", [P, 1])
        minus_half = sb("minus_half", [P, NT])
        win0 = sb("win0", [EP, NW], f16)
        key0 = sb("key0", [GW, WG])
        row = {n: rowt[:, i * D:(i + 1) * D] for i, n in enumerate(ROWS)}
        br = rowt[:, NR * D:NR * D + 1]
        bq, b1c, fb1c = colt[:, 0:DK], colt[:, DK:DK + HK], colt[:, DK + HK:DK + 2 * HK]

        adj_m = sb("adj", [P, NT * P])
        adj = adj_m[:, :].bitcast(f16).rearrange("p (u c d) -> p u c d", u=2, c=NT)
        dlast, at = over(adj_m, 0, [EP, EK, ER], i32)
        e_d, at = over(adj_m, at, [GW, WG, RUN], i32)
        passed, at = over(yw_m, 0, [EP, EK, NW], f16)
        e_a, at = over(yw_m, 0, [GW, WG, RUN], i32)
        e_b, at = over(yw_m, at, [GW, WG, RUN], i32)
        e_c, at = over(yw_m, at, [GW, WG, RUN], i32)
        dlastf = sb("dlastf", [EP, EK])
        gidx = sb("gidx", [GW, WG], i32)
        cov = sb("cov", [GW, 1])
        covered = sb("covered", [P, 1])
        covered_m1 = sb("covered_m1", [P, 1])
        flag = sb("flag", [P, 1], i32)
        scol = sb("scol", [P, NW * TPW], f16)
        kcol = sb("kcol", [P, NW * TPW], f16)
        blk = sb("blk", [P, 2, 2, WPB * TPW], f16)
        oh_m = sb("oh", [P, 2688])
        oh_s, at = over(oh_m, 0, [P, 2, P, TPP], f16)
        oh_k, at = over(oh_m, at, [P, 2, KEYS, TPP], f16)
        oh_e, _ = over(oh_m, 0, [P, P], f16)

        sidx = sb("sidx", [P, 1], i32)
        didx = sb("didx", [P, 1], i32)
        dcol = sb("dcol", [P, 1])
        msg = sb("msg", [P, 2 * D], f16)

        stats = sb("stats", [P, NT, 6])
        mv = sb("mv", [P, NT, 2])
        ve = sb("ve", [P, NT])
        rstd = sb("rstd", [P, NT])
        hid_m = sb("hid", [P, 2 * H])
        xs, at = over(hid_m, 0, [P, 2, D])
        lo32, at = over(hid_m, at, [P, D])
        xq, at = over(hid_m, at, [P, 2, 2, D])
        kb, at = over(oh_m, 0, [P, D])
        kmin, at = over(oh_m, at, [P, D])
        kexp, at = over(oh_m, at, [P, D])
        qb, at = over(oh_m, at, [P, D])
        qmin, at = over(oh_m, at, [P, D])
        qexp, at = over(oh_m, at, [P, D])
        kphi, at = over(oh_m, at, [P, 2, D])
        vv, at = over(oh_m, at, [P, 2, DK, P + 1])
        io_m = sb("io", [P, 6 * D])
        wkv, at = over(io_m, 0, [P, DK, 2 * D])
        wq, at = over(io_m, at, [P, DK, D])
        ksum = sb("ksum", [P, DK])
        kvm = sb("kvm", [P, DK, CW])

        qs, at = over(io_m, 0, [P, 2, D])
        xts, at = over(io_m, at, [P, 2, D])
        xin, at = over(io_m, at, [P, 2, D])
        deg = sb("deg", [P, 3])
        den = sb("den", [P, 2, HEADS])
        at_in = sb("at_in", [P, 4, P])
        at_t = sb("at_t", [P, 4, P])
        agg1 = sb("agg1", [P, D])
        r1 = sb("r1", [P, D])
        gx = sb("gx", [P, D])
        gxb = sb("gxb", [P, 2, D])
        x1 = sb("x1", [P, 2, D])
        x1a = sb("x1a", [P, D])
        x1t = sb("x1t", [P, DK, P])
        ht, at = over(hid_m, 0, [P, HK, P])
        gt, at = over(hid_m, at, [P, HK, P])
        r2 = sb("r2", [P, D])
        z1 = sb("z1", [P, D])
        x2 = sb("x2", [P, D])
        xn2 = sb("xn2", [P, 2, D])
        x2t = sb("x2t", [P, DK, P])
        yb = sb("yb", [P, D])
        bn = sb("bn", [P, 3, 6])
        mvs = sb("mvs", [P, 3, 2])
        ves = sb("ves", [P, 3])
        rs = sb("rs", [P, 3])
        cgb = sb("cgb", [P, D])
        wraw = sb("wraw", [P, 1])
        wall = sb("wall", [P, NT])

        wrow = xn16[:, :, :].rearrange("p c f -> p (c f)").bitcast(f32)[:, 0:N]
        scrap = acc[:, :, :].rearrange("p c f -> p (c f)")
        wt = sb("wt", [NT, P])
        cnt = sb("cnt", [P, 4, NT])
        cnt2 = sb("cnt2", [P, 2, NT])
        sel = sb("sel", [P, NT])

        bank = [ctx.enter_context(nc.psum_tensor(f"bank{i}", [P, 512], f32)) for i in range(8)]
        pT, pKV, pQ, pAcc = bank[0:2], bank[2:4], bank[4:6], bank[6:8]
        pW, pG, pX, pN, pH, pY = bank[0:2], bank[2], bank[3], bank[4], bank[5:7], bank[7]

        names = """const rows_in cols_in wkv_in wq_in w_in dst_in pad vset eset epass cnt idx gat
            var rstd ln xs_ready xn_ready x16 x16c xT xTc KV kvb kc kmin kexp kphi Q qb qmin qexp
            qphi acc kvm cov flag etr ecol tot blkc oh win Aev agg num att atc aggr aggn T1 T1c OG
            og ogc ve1 r1 x1c x1p x1 gxb T2 T2c W1 rel W2 y1 ln2c ve2 r2 z1 x2c x2 ve3 r3 ln3c
            xn2 wsum w base T3 T3c F1 gel F2 y2 yc yw wt wtc wd wrow rankc outs cgb
            sx ssrc sdst sg soh smm sc sacc""".split()
        s = {n: sem("s_" + n) for n in names}
        s_x = [sem(f"s_xload{i}") for i in range(4)]
        s_st = [sem(f"s_store{i}") for i in range(2)]
        s_q = [sem(f"s_qload{i}") for i in range(2)]
        s_xt = [sem(f"s_xtload{i}") for i in range(2)]
        s_xi = [sem(f"s_xiload{i}") for i in range(2)]
        CH = NT // 4

        x_t = x[0:(NT - 1) * P, :].rearrange("(c p) f -> p c f", p=P)
        out_t = out[0:(NT - 1) * P, :].rearrange("(c p) f -> p c f", p=P)
        dst_r = dst.rearrange("(t e) -> t e", e=ER)
        src_r = src.rearrange("(t e) -> t e", e=ER)
        src_c = src.rearrange("(n a) -> n a", a=1)
        dst_c = dst.rearrange("(n a) -> n a", a=1)
        NCONST = 23
        block = ctx.enter_context(nc.Block())

        @block.sync
        def _(sp):
            sp.dma_start(dlast[:, :, :], dst.rearrange("(p k e) -> p k e", p=EP, e=ER)).then_inc(s["dst_in"], 16)
            for i in range(4):
                n = min(CH * (i + 1), NT - 1)
                sp.dma_start(xn[:, CH * i:n, :], x_t[:, CH * i:n, :]).then_inc(s_x[i], 16)
            sp.wait_ge(s["pad"], 1)
            sp.dma_start(xn[0:LAST, NT - 1, :], x[N - LAST:N, :]).then_inc(s_x[3], 16)
            for w_sb, w_in in ((wo, w_o), (wl, w_l), (wrr, w_r), (w1, w_1), (w2, w_2), (f1, f_1), (f2, f_2)):
                sp.dma_start(w_sb[:, :, :], w_in.rearrange("(k p) n -> p k n", p=P)).then_inc(s["w_in"], 16)

            def store(st):
                t = st.back(1)
                if t.real():
                    sp.wait_ge(s["qphi"], t.done())
                    sp.dma_start(xq_d[t.i, :, :], xq[:, t.par, :, :].rearrange("p a f -> p (a f)")).then_inc(s_st[t.par], 16)
            steps(sp, NT + 1, store)
            for u in range(2):
                sp.wait_ge(s_st[u], 16 * NT // 2)

            sp.wait_ge(s["flag"], 1)
            fast = sp.value_load(flag[0:1, 0:1], min_val=0, max_val=1)
            with sp.If(fast == 0):
                sp.wait_ge(s["x16"], NT)
                sp.dma_start(xg_d.rearrange("(c p) f -> p c f", p=P), xn16[:, :, :]).then_inc(s["sx"], 16)
                with sp.Fori(0, ET) as e:
                    wait_apart(sp, s["sacc"], e + 1, (s["flag"], 1))
                    sp.dma_start(sidx[:, :], src_c[bass.ds(e * P, P), :]).then_inc(s["ssrc"], 16)
                    sp.dma_start(didx[:, :], dst_c[bass.ds(e * P, P), :]).then_inc(s["sdst"], 16)

            def load(st):
                t = st.back(-1) if st.n >= 0 else st
                def q_of(t):
                    if t.real():
                        wait(sp, s["num"], t.back(2).done())
                        sp.dma_start(qs[:, t.par, :], xq_d[t.i, :, D:2 * D]).then_inc(s_q[t.par], 16)
                if st.j is None and st.n == 0:
                    q_of(st)
                q_of(t)
                if st.real():
                    if st.back(2).real():
                        wait_apart(sp, s["OG"], st.back(2).done(), (s["flag"], 1))
                        wait_apart(sp, s["og"], st.back(2).done(), (s["flag"], 1))
                    sp.dma_start(xts[:, st.par, :], xq_d[st.i, :, 0:D]).then_inc(s_xt[st.par], 16)
                    if st.j is None and st.n == NT - 1:
                        sp.dma_start(xin[0:LAST, st.par, :], x[N - LAST:N, :]).then_inc(s_xi[st.par], 16)
                    else:
                        sp.dma_start(xin[:, st.par, :], x[bass.ds(st.i * P, P), :]).then_inc(s_xi[st.par], 16)
            steps(sp, NT, load)

            sp.wait_ge(s["wtc"], 1)
            sp.dma_start(w_d.rearrange("(c p) -> c p", p=P), wt[:, :]).then_inc(s["wd"], 16)
            sp.wait_ge(s["wd"], 16)
            sp.wait_ge(s["agg"], NT)
            sp.dma_start(wrow, w_d[0:N].partition_broadcast(P)).then_inc(s["wrow"], 16)
            for c in range(NT):
                sp.wait_ge(s["outs"], c + 1)
                if c < NT - 1:
                    sp.dma_start(out_t[:, c, :], xn[:, c, :]).then_inc(s["w_in"], 16)
                else:
                    sp.dma_start(out[N - LAST:N, :], xn[0:LAST, c, :]).then_inc(s["w_in"], 16)
            sp.wait_ge(s["w_in"], 16 * (7 + NT))

        @block.gpsimd
        def _(pool):
            link = Chain(pool, s["const"], NCONST)
            G.iota(win0[:, :], pattern=[[W, NW]], base=0, channel_multiplier=0,
                   allow_small_or_imprecise_dtypes=True).then_inc(s["eset"], 1)
            G.iota(key0[:, :], pattern=[[-KEYS * GW, WG]], base=0, channel_multiplier=-KEYS,
                   allow_small_or_imprecise_dtypes=True).then_inc(s["eset"], 1)
            G.memset(one16[:, :], 1.0).then_inc(s["eset"], 1)
            link(G.memset(minus_half[:, :], -0.5))
            link(G.memset(ident[:, :], 0.0))
            link(G.affine_select(out=ident[:, :], in_=ident[:, :], compare_op=ALU.not_equal, fill=1.0, base=0,
                                 pattern=[[-1, P]], channel_multiplier=1))
            for u in range(2):
                link(G.memset(vv[:, u, :, P:P + 1], 1.0))
            pool.wait_ge(s["idx"], 1)
            for g in range(WG):
                for buf, tab in ((e_a, src_r), (e_b, dst_r)):
                    G.indirect_dma_start(buf[:, g, :], None, tab[:, :],
                                         bass.IndirectOffsetOnAxis(ap=gidx[:, g:g + 1], axis=0)).then_inc(s["gat"], 16)
            link(G.memset(ones[:, :], 1.0))
            link(G.memset(scale_lo[:, :], LO))
            link(G.iota(iota[:, :, :], pattern=[[1, KEYS], [0, TPP]], base=0, channel_multiplier=0,
                        allow_small_or_imprecise_dtypes=True))
            link(G.memset(same_head[:, :], 0.0))
            link(G.memset(head_of[:, :], 0.0))
            link(G.memset(before[:, :], 0.0))
            link(G.affine_select(out=before[:, :], in_=before[:, :], compare_op=ALU.is_ge, fill=1.0, base=0,
                                 pattern=[[1, P]], channel_multiplier=-1))
            for h in range(HPC):
                r = slice(h * DH, (h + 1) * DH)
                link(G.memset(same_head[r, r], 1.0))
                link(G.memset(head_of[r, h:h + 1], 1.0))
            link(G.memset(acc[:, :, :], 0.0))
            link(G.memset(dacc[:, :], 0.0))
            pool.wait_ge(s["rows_in"], 16)
            link(G.tensor_tensor(cgb[:, :], row["bg"], row["c2"], ALU.add))
            assert link.n == link.per

            pool.wait_ge(s["var"], 1)
            G.tensor_tensor(rstd[:, :], ve[:, :], minus_half[:, :], ALU.pow).then_inc(s["rstd"], 1)

            with pool.Fori(0, NT) as t:
                c16 = Chain(pool, s["x16c"], 2, t)
                wait_apart(pool, s["xn_ready"], t + 1, (s["var"], 1))
                xt = xn[:, bass.ds(t, 1), :].rearrange("p a f -> p (a f)")
                hi = xn16[:, bass.ds(t, 1), 0:D].rearrange("p a f -> p (a f)")
                lo = xn16[:, bass.ds(t, 1), D:2 * D].rearrange("p a f -> p (a f)")
                c16(G.tensor_copy(hi, xt), met=(s["var"], 1))
                c16(G.tensor_tensor(lo32[:, :], xt, hi, ALU.subtract), met=(s["var"], 1))
                G.tensor_tensor(lo, lo32[:, :], scale_lo[:, :].broadcast_to([P, D]), ALU.mult).then_inc(s["x16"], 1)

            pool.wait_ge(s["flag"], 1)
            fast = pool.value_load(flag[0:1, 0:1], min_val=0, max_val=1)
            with pool.If(fast == 0):
                pool.wait_ge(s["sx"], 16)
                with pool.Fori(0, ET) as e:
                    wait_apart(pool, s["ssrc"], (e + 1) * 16, (s["flag"], 1))
                    G.indirect_dma_start(msg[:, :], None, xg_d[:, :],
                                         bass.IndirectOffsetOnAxis(ap=sidx[:, 0:1], axis=0)).then_inc(s["sg"], 16)

            def norm_tail(st):
                t1, t2 = st.back(1), st.back(2)
                if t1.real():
                    pool.wait_ge(s["ve1"], t1.done())
                    G.tensor_tensor(rs[:, 0:1], ves[:, 0:1], minus_half[:, 0:1], ALU.pow).then_inc(s["r1"], 1)
                    pool.wait_ge(s["og"], t1.done())
                    wait(pool, s["x2"], t1.back(2).done())
                    G.tensor_tensor(gxb[:, t1.par, :], gx[:, :], cgb[:, :], ALU.add).then_inc(s["gxb"], 1)
                    pool.wait_ge(s["x1c"], t1.done())
                    G.tensor_tensor(x1a[:, :], x1a[:, :], row["g1"], ALU.mult).then_inc(s["x1p"], 1)
                    pool.wait_ge(s["x1p"], t1.done())
                    wait(pool, s["T2"], t1.back(2).done())
                    wait(pool, s["ve2"], t1.back(2).done())
                    G.tensor_tensor(x1[:, t1.par, :], x1a[:, :], row["c1"], ALU.add).then_inc(s["x1"], 1)
                if t2.real():
                    pool.wait_ge(s["ve2"], t2.done())
                    G.tensor_tensor(rs[:, 1:2], ves[:, 1:2], minus_half[:, 0:1], ALU.pow).then_inc(s["r2"], 1)
                    pool.wait_ge(s["z1"], t2.done())
                    G.tensor_tensor(z1[:, :], z1[:, :], row["g2"], ALU.mult).then_inc(s["x2c"], 1)
                    pool.wait_ge(s["x2c"], t2.done())
                    G.tensor_tensor(x2[:, :], z1[:, :], gxb[:, t2.par, :], ALU.add).then_inc(s["x2"], 1)
                    pool.wait_ge(s["ve3"], t2.done())
                    G.tensor_tensor(rs[:, 2:3], ves[:, 2:3], minus_half[:, 0:1], ALU.pow).then_inc(s["r3"], 1)
                    wait_apart(pool, s["xn2"], t2.done(), (s["flag"], 1))
                    G.tensor_tensor(xn[:, bass.ds(t2.i, 1), :].rearrange("p a f -> p (a f)"), x2[:, :],
                                    xn2[:, t2.par, :], ALU.add).then_inc(s["base"], 1)
            pool.wait_ge(s["const"], NCONST)
            steps(pool, NT + 2, norm_tail)

        @block.scalar
        def _(act):
            act.dma_start(wkv[:, :, 0:D], w_k.rearrange("(k p) n -> p k n", p=P)).then_inc(s["wkv_in"], 16)
            act.dma_start(wkv[:, :, D:2 * D], w_v.rearrange("(k p) n -> p k n", p=P)).then_inc(s["wkv_in"], 16)
            act.dma_start(wq[:, :, :], w_q.rearrange("(k p) n -> p k n", p=P)).then_inc(s["wq_in"], 16)
            act.dma_start(colt[:, :], cols).then_inc(s["cols_in"], 16)
            act.dma_start(rowt[:, :], rows.partition_broadcast(P)).then_inc(s["rows_in"], 16)
            act.wait_ge(s["cols_in"], 16)

            def qkv(st):
                if st.real():
                    t = st
                    act.wait_ge(s["xT"], t.done())
                    wait(act, s["Q"], t.back(2).done())
                    if t.j is not None or t.n >= 2:
                        act.wait_ge(s_st[t.par], t.half * 16)
                    A.activation(xq[:, t.par, 0, :], pT[t.par][:, 0:D], ACT.Copy).then_inc(s["xTc"], 1)
                t = st.back(1)
                if t.real():
                    act.wait_ge(s["Q"], t.done())
                    wait(act, s["qphi"], t.back(1).done())
                    for m in range(DK):
                        i = A.activation(qb[:, m * P:(m + 1) * P], pQ[t.par][:, m * P:(m + 1) * P], ACT.Identity,
                                         bias=bq[:, m:m + 1])
                    i.then_inc(s["qb"], 1)
                    act.wait_ge(s["kmin"], t.done())
                    A.activation(kexp[:, :], kmin[:, :], ACT.Exp).then_inc(s["kexp"], 1)
                    act.wait_ge(s["qmin"], t.done())
                    A.activation(qexp[:, :], qmin[:, :], ACT.Exp).then_inc(s["qexp"], 1)
            steps(act, NT + 1, qkv)

            def adj_out(a, w):
                act.wait_ge(s["win"], a.i * PPB + w + 1)
                if w == 0:
                    wait(act, s["num"], a.back(2).done())
                A.activation(adj[:, a.par, :, w * 2 * W:(w + 1) * 2 * W],
                             pW[w % 2][:, 0:2 * KEYS].rearrange("p (d c) -> p c d", c=NT), ACT.Copy).then_inc(s["Aev"], 1)

            def mix(st):
                a, t1, t2, t3 = st, st.back(1), st.back(2), st.back(3)
                if a.real():
                    adj_out(a, 0)
                if t2.real():
                    act.wait_ge(s["T2"], t2.done())
                    wait(act, s["W1"], t2.back(1).done(2))
                    A.activation(x1t[:, :, :].rearrange("p k q -> p (k q)"), pX[:, 0:D], ACT.Copy).then_inc(s["T2c"], 1)
                if a.real():
                    adj_out(a, 1)
                if t1.real():
                    act.wait_ge(s["T1"], t1.done())
                    wait(act, s["OG"], t1.back(1).done())
                    A.activation(at_t[:, :, :].rearrange("p k q -> p (k q)"), pX[:, :], ACT.Copy).then_inc(s["T1c"], 1)
                if t2.real():
                    wait(act, s["W2"], t2.back(1).done())
                    for m in range(HK):
                        act.wait_ge(s["W1"], t2.i * 2 + m // 4 + 1)
                        i = A.activation(ht[:, m, :], pH[m // 4][:, (m % 4) * P:(m % 4 + 1) * P], ACT.Relu,
                                         bias=b1c[:, m:m + 1])
                        if m % 4 == 3:
                            i.then_inc(s["rel"], 1)
                if a.real():
                    adj_out(a, 2)
                if t3.real():
                    act.wait_ge(s["T3"], t3.done())
                    wait(act, s["F1"], t3.back(1).done(2))
                    A.activation(x2t[:, :, :].rearrange("p k q -> p (k q)"), pX[:, 0:D], ACT.Copy).then_inc(s["T3c"], 1)
                if a.real():
                    adj_out(a, 3)
                    adj_out(a, 4)
                if t3.real():
                    wait(act, s["F2"], t3.back(1).done())
                    for m in range(HK):
                        act.wait_ge(s["F1"], t3.i * 2 + m // 4 + 1)
                        i = A.activation(gt[:, m, :], pH[m // 4][:, (m % 4) * P:(m % 4 + 1) * P],
                                         ACT.Gelu_apprx_tanh, bias=fb1c[:, m:m + 1])
                        if m % 4 == 3:
                            i.then_inc(s["gel"], 1)
                if a.real():
                    for w in (5, 6, 7):
                        adj_out(a, w)
            steps(act, NT + 3, mix)

        @block.vector
        def _(dve):
            link = Chain(dve, s["vset"], 40)
            V.memset(xn[LAST // 32 * 32:P, NT - 1, :], 0.0).then_inc(s["pad"], 1)
            dve.wait_ge(s["dst_in"], 16)
            link(V.tensor_copy(dlastf[:, :], dlast[:, :, ER - 1]))
            dve.wait_ge(s["eset"], 3)
            for k in range(EK):
                i = V.tensor_scalar(passed[:, k, :], win0[:, :], dlastf[:, k:k + 1], None, ALU.is_gt)
            i.then_inc(s["epass"], 1)
            dve.wait_ge(s["cnt"], 1)
            V.tensor_scalar(gidx[:, :], pT[0][0:GW, 0:WG], float((E - RUN) // ER), None, ALU.min).then_inc(s["idx"], 1)

            for q in range(4):
                dve.wait_ge(s_x[q], 16 if q < 3 else 32)
                for c in range(CH * q, CH * (q + 1)):
                    i = V.bn_stats(stats[:, c, :], xn[:, c, :])
            link(i)
            for c in range(NT):
                i = V.bn_aggr(mv[:, c, :], stats[:, c, :])
            link(i)
            V.tensor_scalar(ve[:, :], mv[:, :, 1], EPS, None, ALU.add).then_inc(s["var"], 1)
            dve.wait_ge(s["rstd"], 1)
            dve.wait_ge(s["rows_in"], 16)

            def qkv(st):
                if st.real():
                    t = st
                    xt = xn[:, bass.ds(t.i, 1), :].rearrange("p a f -> p (a f)")
                    m = mv[:, bass.ds(t.i, 1), 0:1].rearrange("p a f -> p (a f)")
                    r = rstd[:, bass.ds(t.i, 1)]
                    wait(dve, s["xT"], t.back(2).done())
                    V.tensor_scalar(xs[:, t.par, :], xt, m, r, ALU.subtract, ALU.mult).then_inc(s["xs_ready"], 1)
                    V.tensor_scalar(xt, xt, m, r, ALU.subtract, ALU.mult).then_inc(s["xn_ready"], 1)
                t = st.back(1)
                if t.real():
                    dve.wait_ge(s["KV"], t.done())
                    wait(dve, s["kphi"], t.back(1).done())
                    V.tensor_tensor(kb[:, :], pKV[t.par][:, 0:D], row["bk"], ALU.add).then_inc(s["kc"], 1)
                    wait(dve, s["acc"], t.back(2).done())
                    V.tensor_tensor(vv[:, t.par, :, 0:P], pKV[t.par][:, D:2 * D].rearrange("p (k f) -> p k f", k=DK),
                                    row["bv"].rearrange("p (k f) -> p k f", k=DK), ALU.add).then_inc(s["kvb"], 1)
                    dve.wait_ge(s["kc"], t.done())
                    V.tensor_scalar(kmin[:, :], kb[:, :], 0.0, None, ALU.min).then_inc(s["kmin"], 1)
                    dve.wait_ge(s["qb"], t.done())
                    wait(dve, s["qphi"], t.back(1).done())
                    V.tensor_scalar(qmin[:, :], qb[:, :], 0.0, None, ALU.min).then_inc(s["qmin"], 1)
                    dve.wait_ge(s["kexp"], t.done())
                    V.scalar_tensor_tensor(out=kphi[:, t.par, :], in0=kb[:, :], scalar=0.0, in1=kexp[:, :],
                                           op0=ALU.max, op1=ALU.add).then_inc(s["kphi"], 1)
                    dve.wait_ge(s["qexp"], t.done())
                    if t.j is not None or t.n >= 2:
                        dve.wait_ge(s_st[t.par], t.half * 16)
                    V.scalar_tensor_tensor(out=xq[:, t.par, 1, :], in0=qb[:, :], scalar=0.0, in1=qexp[:, :],
                                           op0=ALU.max, op1=ALU.add).then_inc(s["qphi"], 1)
            steps(dve, NT + 1, qkv)

            dve.wait_ge(s["acc"], NT)
            dve.wait_ge(s["const"], NCONST)
            for k in range(DK):
                V.tensor_tensor(kvm[:, k, 0:P], pAcc[k][:, 0:P], same_head[:, :], ALU.mult)
                i = V.tensor_copy(ksum[:, k:k + 1], pAcc[k][:, P:P + 1])
            link(i)
            for k in range(DK):
                i = V.tensor_scalar(kvm[:, k, P:CW], head_of[:, :], ksum[:, k:k + 1], None, ALU.mult)
            i.then_inc(s["kvm"], 1)

            dve.wait_ge(s["gat"], 16 * 2 * WG)
            e_f = [e[:, :, :].bitcast(f32) for e in (e_a, e_b, e_c, e_d)]
            link(V.tensor_scalar(e_c[:, :, :], e_a[:, :, :], 7, None, ALU.logical_shift_right))
            link(V.tensor_scalar(e_d[:, :, :], e_a[:, :, :], P - 1, None, ALU.bitwise_and))
            link(V.tensor_copy(e_f[0], e_d[:, :, :]))
            for g in range(WG):
                i = V.tensor_scalar(e_f[3][:, g, :], e_b[:, g, :], float(NT), key0[:, g:g + 1], ALU.mult, ALU.add)
            link(i)
            link(V.tensor_tensor(e_f[3], e_f[3], e_c[:, :, :], ALU.add))
            link(V.tensor_scalar(e_f[1], e_f[3], 0.0, None, ALU.is_ge))
            V.scalar_tensor_tensor(out=e_f[2].rearrange("p a b -> p (a b)"),
                                   in0=e_f[3].rearrange("p a b -> p (a b)"), scalar=float(KEYS),
                                   in1=e_f[1].rearrange("p a b -> p (a b)"),
                                   op0=ALU.is_lt, op1=ALU.mult, accum_out=cov[:, :]).then_inc(s["cov"], 1)
            dve.wait_ge(s["tot"], 1)
            link(V.tensor_scalar(covered[:, :], pQ[0][:, 0:1], float(E), None, ALU.is_equal))
            link(V.tensor_scalar(covered_m1[:, :], covered[:, :], -1.0, None, ALU.add))
            V.tensor_copy(flag[:, :], covered[:, :]).then_inc(s["flag"], 1)
            dve.wait_ge(s["etr"], 1)
            for h in range(2):
                half = slice(h * 2 * GW * TPW, (h + 1) * 2 * GW * TPW)
                o = [c[:, half].rearrange("p (g w j) -> p g j w", g=2, j=TPW) for c in (scol, kcol)]
                in_ = [b[h][:, 0:2 * GW * TPW].rearrange("p (g j w) -> p g j w", g=2, j=TPW) for b in (pT, pKV)]
                V.tensor_copy(o[0], in_[0])
                i = V.tensor_scalar(o[1], in_[1], covered[:, :], covered_m1[:, :], ALU.mult, ALU.add)
            link(i)
            i_last = i

            dve.wait_ge(s["flag"], 1)
            fast = dve.value_load(flag[0:1, 0:1], min_val=0, max_val=1)
            with dve.If(fast == 0):
                V.memset(dcol[:, :], 0.0).then_inc(s["sacc"], 1)
                dve.wait_ge(s["sacc"], 1)
                with dve.Fori(0, ET) as e:
                    dve.wait_ge(s["sdst"], (e + 1) * 16)
                    V.tensor_copy(dcol[:, :], didx[:, :]).then_inc(s["sc"], 1)
                    with dve.Fori(0, NT) as b:
                        n = e * (4 * NT + 1) + b * 4 + 1
                        dve.wait_ge(s["sc"], n)
                        V.tensor_scalar(oh_e[:, :], iota[:, 0:P, 0], dcol[:, :], None, ALU.is_equal).then_inc(s["soh"], 1)
                        dve.wait_ge(s["smm"], e * NT + b + 1)
                        ab = acc[:, bass.ds(b, 1), :].rearrange("p a f -> p (a f)")
                        db = dacc[:, bass.ds(b, 1)]
                        V.tensor_tensor(ab, pG[:, 0:D], ab, ALU.add).then_inc(s["sc"], 1)
                        dve.wait_ge(s["sc"], n + 1)
                        V.scalar_tensor_tensor(out=ab, in0=pG[:, D:2 * D], scalar=1 / LO, in1=ab, op0=ALU.mult,
                                               op1=ALU.add).then_inc(s["sc"], 1)
                        V.tensor_tensor(db, pN[:, 0:1], db, ALU.add).then_inc(s["sc"], 1)
                        V.tensor_scalar(dcol[:, :], dcol[:, :], -float(P), None, ALU.add).then_inc(s["sc"], 1)
                    dve.wait_ge(s["sc"], (e + 1) * (4 * NT + 1))
                    V.tensor_copy(dcol[:, :], didx[:, :]).then_inc(s["sacc"], 1)

            def one_hots(a, w):
                if w == 0:
                    bc = Chain(dve, s["blkc"], 1, a.i)
                    for n, c in enumerate((scol, kcol)):
                        i = V.tensor_copy(blk[:, a.par, n, :], c[:, bass.ds(a.i * (WPB * TPW), WPB * TPW)])
                    bc(i)
                if w >= 2 or a.j is not None or a.n > 0:
                    dve.wait_ge(s["win"], a.i * PPB + w - 1)
                for c, (oh, n) in enumerate(((oh_s, P), (oh_k, KEYS))):
                    of_pair = blk[:, a.par, c, w * TPP:(w + 1) * TPP].unsqueeze(1).broadcast_to([P, n, TPP])
                    i = V.tensor_tensor(oh[:, w % 2, :, :], iota[:, 0:n, :], of_pair, ALU.is_equal)
                i.then_inc(s["oh"], 1)

            def heads_and_mean(t):
                lk = Chain(dve, s["atc"], 5, t.i)
                dve.wait_ge(s["num"], t.done())
                state = pN[:, 0:DK * CW].rearrange("p (k c) -> p k c", k=DK)
                V.tensor_tensor(deg[:, 0:1], pN[:, DK * CW:DK * CW + 1], dacc[:, bass.ds(t.i, 1)], ALU.add)
                lk(V.tensor_scalar(den[:, 0, :].rearrange("p (k h) -> p k h", k=DK), state[:, :, P:CW], 1e-6, None,
                                   ALU.add))
                V.tensor_scalar(deg[:, 1:2], deg[:, 0:1], 1.0, None, ALU.max)
                lk(V.reciprocal(den[:, 1, :], den[:, 0, :]))
                lk(V.reciprocal(deg[:, 2:3], deg[:, 1:2]))
                wait(dve, s["T1"], t.back(1).done())
                V.tensor_tensor(at_in[:, 2:4, :].rearrange("p k (h f) -> p k h f", h=HPC),
                                state[:, :, 0:P].rearrange("p k (h f) -> p k h f", h=HPC),
                                den[:, 1, :].rearrange("p (k h) -> p k h", k=DK).unsqueeze(3).broadcast_to(
                                    [P, DK, HPC, DH]), ALU.mult).then_inc(s["att"], 1)
                dve.wait_ge(s["agg"], t.done())
                lk(V.tensor_tensor(agg1[:, :], pG[:, 0:D], acc[:, bass.ds(t.i, 1), :].rearrange("p a f -> p (a f)"),
                                   ALU.add))
                V.scalar_tensor_tensor(out=agg1[:, :], in0=pG[:, D:2 * D], scalar=1 / LO, in1=agg1[:, :],
                                       op0=ALU.mult, op1=ALU.add).then_inc(s["aggr"], 1)
                dve.wait_ge(s["aggr"], t.done())
                lk(V.tensor_scalar(at_in[:, 0:2, :].rearrange("p k f -> p (k f)"), agg1[:, :], deg[:, 2:3], None,
                                   ALU.mult))

            def statistics(lk, n, r, out_sem):
                lk(V.bn_stats(bn[:, n, :], r), met=(s["kvm"], 1))
                lk(V.bn_aggr(mvs[:, n, :], bn[:, n, :]))
                V.tensor_scalar(ves[:, n:n + 1], mvs[:, n, 1:2], EPS, None, ALU.add).then_inc(out_sem, 1)

            def after_attention(t):
                lk = Chain(dve, s["ogc"], 4, t.i)
                dve.wait_ge(s["OG"], t.done())
                V.tensor_tensor(r1[:, :], pN[:, 0:D], row["bo"], ALU.add).then_inc(s["ogc"], 1)
                dve.wait_ge(s_xi[t.par], (t.half + 1) * 16)
                wait(dve, s["gxb"], t.back(1).done())
                V.tensor_tensor(gx[:, :], pN[:, D:2 * D], xin[:, t.par, :], ALU.add).then_inc(s["og"], 1)
                lk.n = 1
                dve.wait_ge(s["ogc"], lk.base + 1)
                lk(V.tensor_tensor(r1[:, :], r1[:, :], xn[:, bass.ds(t.i, 1), :].rearrange("p a f -> p (a f)"), ALU.add))
                statistics(lk, 0, r1[:, :], s["ve1"])

            def norm1(t):
                dve.wait_ge(s["r1"], t.done())
                wait(dve, s["x1"], t.back(1).done())
                V.tensor_scalar(x1a[:, :], r1[:, :], mvs[:, 0, 0:1], rs[:, 0:1], ALU.subtract, ALU.mult).then_inc(s["x1c"], 1)

            def after_ff(t):
                lk = Chain(dve, s["ln2c"], 3, t.i)
                dve.wait_ge(s["W2"], t.done())
                V.tensor_tensor(r2[:, :], pY[:, 0:D], row["b2"], ALU.add).then_inc(s["y1"], 1)
                dve.wait_ge(s["y1"], t.done())
                dve.wait_ge(s["x1"], t.done())
                lk(V.tensor_tensor(r2[:, :], r2[:, :], x1[:, t.par, :], ALU.add))
                lk(V.bn_stats(bn[:, 1, :], r2[:, :]), met=(s["kvm"], 1))
                lk(V.bn_aggr(mvs[:, 1, :], bn[:, 1, :]))
                V.tensor_scalar(ves[:, 1:2], mvs[:, 1, 1:2], EPS, None, ALU.add).then_inc(s["ve2"], 1)

            def norm2(t):
                dve.wait_ge(s["r2"], t.done())
                wait(dve, s["x2"], t.back(1).done())
                V.tensor_scalar(z1[:, :], r2[:, :], mvs[:, 1, 0:1], rs[:, 1:2], ALU.subtract, ALU.mult).then_inc(s["z1"], 1)

            def stats3(t):
                lk = Chain(dve, s["ln3c"], 2, t.i)
                dve.wait_ge(s["x2"], t.done())
                statistics(lk, 2, x2[:, :], s["ve3"])

            def norm3(t):
                dve.wait_ge(s["r3"], t.done())
                wait(dve, s["T3"], t.back(2).done())
                wait(dve, s["base"], t.back(2).done())
                V.tensor_scalar(xn2[:, t.par, :], x2[:, :], mvs[:, 2, 0:1], rs[:, 2:3], ALU.subtract, ALU.mult).then_inc(s["xn2"], 1)
                dve.wait_ge(s["xn2"], t.done())
                wait(dve, s["yw"], t.back(2).done())
                V.tensor_tensor_reduce(out=yb[:, :], in0=xn2[:, t.par, :], in1=row["wr"], scale=1.0, scalar=0.0,
                                       op0=ALU.mult, op1=ALU.add, accum_out=wraw[:, :]).then_inc(s["wsum"], 1)
                dve.wait_ge(s["wsum"], t.done())
                V.tensor_tensor(wall[:, bass.ds(t.i, 1)], wraw[:, :], br, ALU.add).then_inc(s["w"], 1)

            def routed(t):
                dve.wait_ge(s["F2"], t.done())
                wait(dve, s["yw"], t.back(1).done())
                V.tensor_tensor(yb[:, :], pY[:, 0:D], row["fb2"], ALU.add).then_inc(s["y2"], 1)
                dve.wait_ge(s["y2"], t.done())
                dve.wait_ge(s["w"], t.done())
                V.tensor_scalar(yw[:, bass.ds(t.i, 1), :].rearrange("p a f -> p (a f)"), yb[:, :],
                                wall[:, bass.ds(t.i, 1)], None, ALU.mult).then_inc(s["yw"], 1)

            def mix(st):
                a, t1, t2, t3 = st, st.back(1), st.back(2), st.back(3)
                if t1.real():
                    heads_and_mean(t1)
                if a.real():
                    one_hots(a, 2)
                    one_hots(a, 3)
                if t1.real():
                    after_attention(t1)
                if a.real():
                    one_hots(a, 4)
                if t1.real():
                    norm1(t1)
                if t2.real():
                    after_ff(t2)
                if a.real():
                    one_hots(a, 5)
                if t2.real():
                    norm2(t2)
                if a.real():
                    one_hots(a, 6)
                if t2.real():
                    stats3(t2)
                if a.real():
                    one_hots(a, 7)
                if t2.real():
                    norm3(t2)
                if t3.real():
                    routed(t3)
                b = st.back(-1)
                if b.real():
                    one_hots(b, 0)
                    one_hots(b, 1)
            first_block = Tile(0)
            one_hots(first_block, 0)
            one_hots(first_block, 1)
            steps(dve, NT + 3, mix)

            dve.wait_ge(s["wt"], 1)
            V.tensor_copy(wt[:, :], pX[0:NT, 0:P]).then_inc(s["wtc"], 1)
            dve.wait_ge(s["wrow"], 16)
            dve.wait_ge(s["base"], NT)
            rl = Chain(dve, s["rankc"], 5 * NT)
            rl(V.memset(cnt[:, :, :], 0.0))
            for c in range(NT):
                me = wall[:, c:c + 1]
                lo, hi = c * P, min(c * P + P, N)
                if c:
                    V.tensor_scalar(scrap[:, 0:lo], wrow[:, 0:lo], me, None, ALU.is_ge, ALU.add,
                                    accum_out=cnt[:, 0, c:c + 1])
                V.tensor_scalar(scrap[:, lo:N], wrow[:, lo:N], me, None, ALU.is_gt, ALU.add,
                                accum_out=cnt[:, 1, c:c + 1])
                rl(V.scalar_tensor_tensor(out=scrap[:, N:N + hi - lo], in0=wrow[:, lo:hi], scalar=me,
                                          in1=before[:, 0:hi - lo], op0=ALU.is_equal, op1=ALU.mult,
                                          accum_out=cnt[:, 2, c:c + 1]))
                rl(V.tensor_tensor(cnt2[:, 0, c:c + 1], cnt[:, 0, c:c + 1], cnt[:, 1, c:c + 1], ALU.add))
                rl(V.tensor_tensor(cnt2[:, 1, c:c + 1], cnt2[:, 0, c:c + 1], cnt[:, 2, c:c + 1], ALU.add))
                rl(V.tensor_scalar(sel[:, c:c + 1], cnt2[:, 1, c:c + 1], float(KEEP), None, ALU.is_lt))
                V.scalar_tensor_tensor(out=xn[:, c, :], in0=yw[:, c, :], scalar=sel[:, c:c + 1], in1=xn[:, c, :],
                                       op0=ALU.mult, op1=ALU.add).then_inc(s["outs"], 1)

        @block.tensor
        def _(pe):
            pe.wait_ge(s["epass"], 1)
            for g in range(WG):
                for k in range(EK):
                    i = T.matmul(pT[0][0:GW, g:g + 1], passed[:, k, g * GW:(g + 1) * GW], one16[0:EP, :],
                                 start=(k == 0), stop=(k == EK - 1))
            i.then_inc(s["cnt"], 1)
            pe.wait_ge(s["idx"], 1)
            pe.wait_ge(s["const"], 5)
            pe.wait_ge(s["wkv_in"], 32)
            pe.wait_ge(s["wq_in"], 16)

            def qkv(st):
                if st.real():
                    t = st
                    pe.wait_ge(s["xs_ready"], t.done())
                    wait(pe, s["xTc"], t.back(2).done())
                    for k in range(DK):
                        i = T.transpose(pT[t.par][:, k * P:(k + 1) * P], xs[:, t.par, k * P:(k + 1) * P], ident[:, :])
                    i.then_inc(s["xT"], 1)
                t = st.back(1)
                if t.real():
                    pe.wait_ge(s["xTc"], t.done())
                    wait(pe, s["kvb"], t.back(2).done())
                    for k in range(DK):
                        i = T.matmul(pKV[t.par][:, :], xq[:, t.par, 0, k * P:(k + 1) * P], wkv[:, k, :],
                                     start=(k == 0), stop=(k == DK - 1))
                    i.then_inc(s["KV"], 1)
                    wait(pe, s["qb"], t.back(2).done())
                    for m in range(DK):
                        for k in range(DK):
                            i = T.matmul(pQ[t.par][:, m * P:(m + 1) * P], wq[:, k, m * P:(m + 1) * P],
                                         xq[:, t.par, 0, k * P:(k + 1) * P], start=(k == 0), stop=(k == DK - 1))
                    i.then_inc(s["Q"], 1)
                t = st.back(2)
                if t.real():
                    r = LAST if t.j is None and t.n == NT - 1 else P
                    pe.wait_ge(s["kphi"], t.done())
                    for k in range(DK):
                        i = T.matmul(pAcc[k][:, 0:P + 1], kphi[0:r, t.par, k * P:(k + 1) * P], vv[0:r, t.par, k, :],
                                     start=(t.j is None and t.n == 0), stop=(t.j is None and t.n == NT - 1))
                    i.then_inc(s["acc"], 1)
            steps(pe, NT + 2, qkv)

            pe.wait_ge(s["cov"], 1)
            pe.wait_ge(s["const"], NCONST)
            T.matmul(pQ[0][:, 0:1], ones[0:GW, :], cov[:, :], start=True, stop=True).then_inc(s["tot"], 1)
            for g in range(WG):
                for j in range(TPW):
                    for bk, e in ((pT[g // 2], e_a), (pKV[g // 2], e_d)):
                        col = (g % 2 * TPW + j) * GW
                        i = T.transpose(bk[:, col:col + GW], e[:, g, j * P:(j + 1) * P].bitcast(f32),
                                        ident[0:GW, 0:GW])
            i.then_inc(s["etr"], 1)

            pe.wait_ge(s["flag"], 1)
            fast = pe.value_load(flag[0:1, 0:1], min_val=0, max_val=1)
            with pe.If(fast == 0):
                with pe.Fori(0, ET) as e:
                    wait_apart(pe, s["sg"], (e + 1) * 16, (s["flag"], 1))
                    with pe.Fori(0, NT) as b:
                        pe.wait_ge(s["soh"], e * NT + b + 1)
                        T.matmul(pG[:, :], oh_e[:, :], msg[:, :], start=True, stop=True)
                        T.matmul(pN[:, 0:1], oh_e[:, :], one16[:, :], start=True, stop=True).then_inc(s["smm"], 1)

            pe.wait_ge(s["w_in"], 16 * 7)
            pe.wait_ge(s["kvm"], 1)
            pe.wait_ge(s["x16"], NT)
            pe.wait_ge(s["vset"], 13)

            def window(a, w):
                pe.wait_ge(s["oh"], a.i * PPB + w + 1)
                if w >= 2 or a.j is not None or a.n > 0:
                    pe.wait_ge(s["Aev"], a.i * PPB + w - 1)
                for h in range(2):
                    for j in range(TPW):
                        i = T.matmul(pW[w % 2][:, h * KEYS:(h + 1) * KEYS], oh_s[:, w % 2, :, h * TPW + j],
                                     oh_k[:, w % 2, :, h * TPW + j], start=(j == 0), stop=(j == TPW - 1))
                i.then_inc(s["win"], 1)

            def to_hidden(w_sb, xt, out_sem):
                for m in range(HK):
                    for k in range(DK):
                        i = T.matmul(pH[m // 4][:, (m % 4) * P:(m % 4 + 1) * P], w_sb[:, k, m * P:(m + 1) * P],
                                     xt[:, k, :], start=(k == 0), stop=(k == DK - 1))
                    if m % 4 == 3:
                        i.then_inc(out_sem, 1)

            def from_hidden(w_sb, h, in_sem, t, out_sem):
                for m in range(HK):
                    pe.wait_ge(in_sem, t.i * 2 + m // 4 + 1)
                    i = T.matmul(pY[:, 0:D], h[:, m, :], w_sb[:, m, :], start=(m == 0), stop=(m == HK - 1))
                i.then_inc(out_sem, 1)

            def mix(st):
                a, t1, t2, t3 = st, st.back(1), st.back(2), st.back(3)
                if a.real():
                    window(a, 0)
                if t2.real():
                    pe.wait_ge(s["x1"], t2.done())
                    wait(pe, s["T3c"], t2.back(2).done())
                    wait(pe, s["T1c"], t2.done())
                    for k in range(DK):
                        i = T.transpose(pX[:, k * P:(k + 1) * P], x1[:, t2.par, k * P:(k + 1) * P], ident[:, :])
                    i.then_inc(s["T2"], 1)
                if a.real():
                    window(a, 1)
                if t1.real():
                    pe.wait_ge(s["att"], t1.done())
                    pe.wait_ge(s["atc"], t1.done(5))
                    wait(pe, s["T2c"], t1.back(1).done())
                    for k in range(4):
                        i = T.transpose(pX[:, k * P:(k + 1) * P], at_in[:, k, :], ident[:, :])
                    i.then_inc(s["T1"], 1)
                if t2.real():
                    pe.wait_ge(s["T2c"], t2.done())
                    wait(pe, s["gel"], t2.back(2).done(2))
                    to_hidden(w1, x1t, s["W1"])
                if a.real():
                    window(a, 2)
                if t3.real():
                    pe.wait_ge(s["xn2"], t3.done())
                    wait(pe, s["T1c"], st.back(1).done())
                    wait(pe, s["T2c"], st.back(2).done())
                    wait(pe, s["T3c"], t3.back(1).done())
                    for k in range(DK):
                        i = T.transpose(pX[:, k * P:(k + 1) * P], xn2[:, t3.par, k * P:(k + 1) * P], ident[:, :])
                    i.then_inc(s["T3"], 1)
                if t1.real():
                    pe.wait_ge(s["T1c"], t1.done())
                    pe.wait_ge(s_xt[t1.par], (t1.half + 1) * 16)
                    for k in range(DK):
                        T.matmul(pN[:, 0:D], at_t[:, 2 + k, :], wo[:, k, :], start=(k == 0), stop=(k == DK - 1))
                    for k in range(DK):
                        T.matmul(pN[:, D:2 * D], at_t[:, k, :], wl[:, k, :], start=(k == 0), stop=False)
                    for k in range(DK):
                        i = T.matmul(pN[:, D:2 * D], xts[:, t1.par, k * P:(k + 1) * P], wrr[:, k, :], start=False,
                                     stop=(k == DK - 1))
                    i.then_inc(s["OG"], 1)
                if a.real():
                    window(a, 3)
                if t2.real():
                    wait(pe, s["y2"], t2.back(2).done())
                    from_hidden(w2, ht, s["rel"], t2, s["W2"])
                if a.real():
                    window(a, 4)
                if t3.real():
                    pe.wait_ge(s["T3c"], t3.done())
                    wait(pe, s["rel"], st.back(2).done(2))
                    wait(pe, s["gel"], t3.back(1).done(2))
                    to_hidden(f1, x2t, s["F1"])
                if a.real():
                    window(a, 5)
                    window(a, 6)
                if t3.real():
                    wait(pe, s["y1"], st.back(2).done())
                    wait(pe, s["y2"], t3.back(1).done())
                    from_hidden(f2, gt, s["gel"], t3, s["F2"])
                if a.real():
                    window(a, 7)
                    pe.wait_ge(s["Aev"], a.i * PPB + PPB)
                    wait(pe, s["aggr"], a.back(1).done())
                    for c in range(NT):
                        i = T.matmul(pG[:, :], adj[:, a.par, c, :], xn16[:, c, :], start=(c == 0), stop=(c == NT - 1))
                    i.then_inc(s["agg"], 1)
                    wait(pe, s["og"], a.back(1).done())
                    for c in range(NT):
                        T.matmul(pN[:, DK * CW:DK * CW + 1], adj[:, a.par, c, :], one16[:, :], start=(c == 0),
                                 stop=(c == NT - 1))
                    pe.wait_ge(s_q[a.par], (a.half + 1) * 16)
                    for k in range(DK):
                        i = T.matmul(pN[:, k * CW:(k + 1) * CW], qs[:, a.par, k * P:(k + 1) * P], kvm[:, k, :],
                                     start=True, stop=True)
                    i.then_inc(s["num"], 1)
            steps(pe, NT + 3, mix)
            pe.wait_ge(s["w"], NT)
            pe.wait_ge(s["T3c"], NT)
            T.transpose(pX[0:NT, 0:P], wall[:, :], ident[:, :]).then_inc(s["wt"], 1)


def kernel(**inputs):
    import numpy as np
    import concourse.bacc as bacc
    from concourse.bass_utils import run_bass_kernel_spmd

    a = {k: np.asarray(v) for k, v in inputs.items()}
    m = {k[7:]: v for k, v in a.items() if k.startswith("L0_mix_")}
    g = {k[7:]: v for k, v in a.items() if k.startswith("L0_gnn_")}
    f = {k[7:]: v for k, v in a.items() if k.startswith("L0_ffn_")}
    rows = [m["bk"], m["bv"], m["bo"], m["ln1_g"], m["ln1_b"], m["b2"], m["ln2_g"], m["ln2_b"], g["b_r"],
            f["wr"].reshape(-1), f["b2"], f["br"].reshape(-1)]
    cols = [m["bq"].reshape(-1, P).T, m["b1"].reshape(-1, P).T, f["b1"].reshape(-1, P).T]
    given = [
        ("x", a["x"]), ("src", a["src"]), ("dst", a["dst"]), ("w_l", g["W_l"].T), ("w_r", g["W_r"].T),
        ("w_q", m["Wq"]), ("w_k", m["Wk"]), ("w_v", m["Wv"]), ("w_o", m["Wo"]), ("w_1", m["W1"]), ("w_2", m["W2"]),
        ("f_1", f["w1"]), ("f_2", f["w2"]), ("rows", np.concatenate(rows)), ("cols", np.concatenate(cols, axis=1)),
    ]
    nc = bacc.Bacc("TRN2", target_bir_lowering=False, num_devices=1)
    arrays, args = {}, []
    for name, v in given:
        v = np.ascontiguousarray(v)
        arrays["in_" + name] = v
        args.append(nc.dram_tensor("in_" + name, v.shape, mybir.dt.from_np(v.dtype), kind="ExternalInput").ap())
    args.append(nc.dram_tensor("out_0", (N, D), mybir.dt.float32, kind="ExternalOutput").ap())
    args.append(nc.dram_tensor("xq_d", (NT, P, 2 * D), mybir.dt.float32, kind="Internal").ap())
    args.append(nc.dram_tensor("xg_d", (NT * P, 2 * D), mybir.dt.float16, kind="Internal").ap())
    args.append(nc.dram_tensor("w_d", (NT * P,), mybir.dt.float32, kind="Internal").ap())
    gps_layer(nc, *args)
    r = run_bass_kernel_spmd(nc, [arrays], core_ids=[0])
    return r.results[0]["out_0"]
```

```python
import concourse.bass as bass
from concourse import mybir
from contextlib import ExitStack

P = 128
N = 2500
D = 256
DK = D // P
H = 1024
HK = H // P
HEADS = 8
DH = D // HEADS
HPC = P // DH
E = 80000
NT = -(-N // P)
LAST = N - (NT - 1) * P
ET = E // P
W = 8
WPB = P // W
NW = NT * WPB
WG = 4
GW = NW // WG
TPW = 3
RUN = TPW * P
ER = 32
KEYS = W * NT
PPB = WPB // 2
TPP = 2 * TPW
OH = 4
EP = 125
EK = E // ER // EP
EPS = 1e-5
LO = 2.0 ** 11
KEEP = int(0.5 * N) - 1
NS = -(-KEEP // (2 * P))
SLOTS = 2 * P * NS
ROWS = ["bk", "bv", "bo", "g1", "c1", "b2", "g2", "c2", "bg", "wr", "fb2"]
CW = P + HPC


class Tile:

    def __init__(self, n, j=None):
        self.n, self.j, self.par = n, j, n % 2
        self.i = n if j is None else j * 2 + n
        self.half = n // 2 if j is None else j + n // 2

    def back(self, k):
        return Tile(self.n - k, self.j)

    def real(self):
        return self.j is not None or 0 <= self.n < NT

    def done(self, per=1):
        if self.j is None:
            return per * max(0, min(self.n + 1, NT))
        return self.i * per + per


def steps(eng, total, body, first=3):
    for n in range(first):
        body(Tile(n))
    with eng.Fori(0, (19 - first) // 2) as j:
        body(Tile(first, j))
        body(Tile(first + 1, j))
    for n in range(19, total):
        body(Tile(n))


def wait(eng, sem, value):
    if not isinstance(value, int) or value > 0:
        eng.wait_ge(sem, value)


def wait_apart(eng, sem, value, met):
    if not isinstance(value, int):
        value = eng.snap(eng.to_reg(value))
    eng.wait_ge(*met)
    eng.wait_ge(sem, value)


class Chain:

    def __init__(self, eng, sem, per, tile=0):
        self.eng, self.sem, self.per, self.base, self.n = eng, sem, per, tile * per, 0

    def __call__(self, ins, met=None):
        self.n += 1
        assert self.n <= self.per
        ins.then_inc(self.sem, 1)
        if met:
            wait_apart(self.eng, self.sem, self.base + self.n, met)
        else:
            self.eng.wait_ge(self.sem, self.base + self.n)


def gps_layer(nc, x, src, dst, w_l, w_r, w_q, w_k, w_v, w_o, w_1, w_2, f_1, f_2, rows, cols, out,
              xq_d, xg_d, w_d, xb_d):
    f32, f16, i32 = mybir.dt.float32, mybir.dt.float16, mybir.dt.int32
    ALU, ACT = mybir.AluOpType, mybir.ActivationFunctionType
    V, G, A, T = nc.vector, nc.gpsimd, nc.scalar, nc.tensor
    NR = len(ROWS)
    ctx = ExitStack()
    with ctx:
        def sb(name, shape, dt=f32):
            return ctx.enter_context(nc.sbuf_tensor(name, shape, dt))

        def over(held, at, shape, dt=f32):
            size, n = {f32: 4, i32: 4, f16: 2}[dt], 1
            for k in shape[1:]:
                n *= k
            end = at + -(-n * size // 4)
            v = held[0:shape[0], at:end].bitcast(dt)[:, 0:n] if dt != f32 else held[0:shape[0], at:end]
            if len(shape) == 3:
                v = v.rearrange("p (a b) -> p a b", a=shape[1])
            if len(shape) == 4:
                v = v.rearrange("p (a b c) -> p a b c", a=shape[1], b=shape[2])
            return v, end

        def sem(name):
            return ctx.enter_context(nc.semaphore(name))

        xn = sb("xn", [P, NT, D])
        xn16 = sb("xn16", [P, NT, 2 * D], f16)
        acc_m = sb("acc", [P, NT * D])
        acc = acc_m[:, :].rearrange("p (c f) -> p c f", c=NT)
        dacc = sb("dacc", [P, NT])
        e_m = sb("e", [P, 3 * WG * RUN])
        wo = sb("wo", [P, DK, D])
        wl = sb("wl", [P, DK, D])
        wrr = sb("wrr", [P, DK, D])
        w1 = sb("w1", [P, DK, H])
        w2 = sb("w2", [P, HK, D])
        f1 = sb("f1", [P, DK, H])
        f2 = sb("f2", [P, HK, D])
        rowt = sb("rowt", [P, NR * D + 1])
        colt = sb("colt", [P, DK + 2 * HK])
        ident = sb("ident", [P, P])
        same_head = sb("same_head", [P, P])
        head_of = sb("head_of", [P, HPC])
        later = sb("later", [P, P])
        iota = sb("iota", [P, KEYS, TPP], f16)
        one16 = sb("one16", [P, 1], f16)
        ones = sb("ones", [P, P])
        scale_lo = sb("scale_lo", [P, 1])
        minus_half = sb("minus_half", [P, NT])
        win0 = sb("win0", [EP, NW], f16)
        key0 = sb("key0", [GW, WG])
        row = {n: rowt[:, i * D:(i + 1) * D] for i, n in enumerate(ROWS)}
        br = rowt[:, NR * D:NR * D + 1]
        bq, b1c, fb1c = colt[:, 0:DK], colt[:, DK:DK + HK], colt[:, DK + HK:DK + 2 * HK]

        adj_m = sb("adj", [P, NT * P])
        adj = adj_m[:, :].bitcast(f16).rearrange("p (u c d) -> p u c d", u=2, c=NT)
        dlast, at = over(adj_m, 0, [EP, EK, ER], i32)
        e_d, at = over(adj_m, at, [GW, WG, RUN], i32)
        passed, at = over(e_m, 0, [EP, EK, NW], f16)
        e_a, at = over(e_m, 0, [GW, WG, RUN], i32)
        e_b, at = over(e_m, at, [GW, WG, RUN], i32)
        e_c, at = over(e_m, at, [GW, WG, RUN], i32)
        dlastf = sb("dlastf", [EP, EK])
        gidx = sb("gidx", [GW, WG], i32)
        cov = sb("cov", [GW, 1])
        covered = sb("covered", [P, 1])
        covered_m1 = sb("covered_m1", [P, 1])
        flag = sb("flag", [P, 1], i32)
        scol = sb("scol", [P, NW * TPW], f16)
        kcol = sb("kcol", [P, NW * TPW], f16)
        blk = sb("blk", [P, 2, 2, WPB * TPW], f16)
        oh_m = sb("oh", [P, OH * (P + KEYS) * TPP // 2])
        oh_s, at = over(oh_m, 0, [P, OH, P, TPP], f16)
        oh_k, at = over(oh_m, at, [P, OH, KEYS, TPP], f16)
        oh_e, _ = over(oh_m, 0, [P, P], f16)

        sidx = sb("sidx", [P, 1], i32)
        didx = sb("didx", [P, 1], i32)
        dcol = sb("dcol", [P, 1])
        msg = sb("msg", [P, 2 * D], f16)

        stats = sb("stats", [P, NT, 6])
        mv = sb("mv", [P, NT, 2])
        ve = sb("ve", [P, NT])
        rstd = sb("rstd", [P, NT])
        hid_m = sb("hid", [P, 2 * H])
        xs, at = over(hid_m, 0, [P, 2, D])
        lo32, at = over(hid_m, at, [P, D])
        xt_s, at = over(hid_m, at, [P, 2, D])
        qp_s, at = over(hid_m, at, [P, 2, D])
        kb, at = over(oh_m, 0, [P, D])
        kmin, at = over(oh_m, at, [P, D])
        kexp, at = over(oh_m, at, [P, D])
        qb, at = over(oh_m, at, [P, D])
        qmin, at = over(oh_m, at, [P, D])
        qexp, at = over(oh_m, at, [P, D])
        kphi, at = over(oh_m, at, [P, 2, D])
        vv, at = over(oh_m, at, [P, 2, DK, P + 1])
        io_m = sb("io", [P, 6 * D])
        wkv, at = over(io_m, 0, [P, DK, 2 * D])
        wq, at = over(io_m, at, [P, DK, D])
        ksum = sb("ksum", [P, DK])
        kvm = sb("kvm", [P, DK, CW])

        qs, at = over(io_m, 0, [P, 2, D])
        xts, at = over(io_m, at, [P, 2, D])
        xin, at = over(io_m, at, [P, 2, D])
        deg = sb("deg", [P, 3])
        den = sb("den", [P, 2, HEADS])
        at_in = sb("at_in", [P, 4, P])
        at_t = sb("at_t", [P, 4, P])
        agg1 = sb("agg1", [P, D])
        r1 = sb("r1", [P, D])
        gx = sb("gx", [P, D])
        gxb = sb("gxb", [P, 2, D])
        x1 = sb("x1", [P, 2, D])
        x1a = sb("x1a", [P, D])
        x1t = sb("x1t", [P, DK, P])
        ht, at = over(hid_m, 0, [P, HK, P])
        r2 = sb("r2", [P, D])
        z1 = sb("z1", [P, D])
        x2 = sb("x2", [P, D])
        xb = sb("xb", [P, 2, 2 * D])
        yb = sb("yb", [P, D])
        bn = sb("bn", [P, 3, 6])
        mvs = sb("mvs", [P, 3, 2])
        ves = sb("ves", [P, 3])
        rs = sb("rs", [P, 3])
        cgb = sb("cgb", [P, D])
        wraw = sb("wraw", [P, 1])
        wall = sb("wall", [P, NT])

        xn16_m = xn16[:, :, :].rearrange("p c f -> p (c f)").bitcast(f32)
        wrow, at = over(xn16_m, 0, [P, N])
        beats, at = over(xn16_m, at, [P, 2, NT * P], f16)
        scrap, _ = over(e_m, 0, [P, 2, N], f16)
        tok = sb("tok", [P, NT, 2], f16)
        places, at = over(adj_m, 0, [P, SLOTS], f16)
        oh_r, at = over(adj_m, at, [P, 2, SLOTS], f16)
        ahead = sb("ahead", [P, NT])
        n_later = sb("n_later", [P, NT])
        rank = sb("rank", [P, NT])
        stok = sb("stok", [P, 2 * NS, 2])
        sid = sb("sid", [P, 2 * NS], i32)
        gx2, _ = over(acc_m, 0, [P, 2 * NS, 2 * D])
        x2t, at = over(e_m, 0, [P, DK, 2 * P])
        gt, at = over(e_m, at, [P, 2, HK * 2 * P])
        gt = gt.rearrange("p u (m t) -> p u m t", m=HK)
        yo, at = over(hid_m, 0, [P, 2, D])
        ws = sb("ws", [P, 2, 2])
        wt = sb("wt", [NT, P])

        bank = [ctx.enter_context(nc.psum_tensor(f"bank{i}", [P, 512], f32)) for i in range(8)]
        pT, pKV, pQ, pAcc = bank[0:2], bank[2:4], bank[4:6], bank[6:8]
        pW, pG, pX, pN, pH, pY = bank[0:2], bank[2], bank[3], bank[4], bank[5:7], bank[7]
        pF, pR = bank[0:2] + bank[5:7], (bank[7], bank[2])

        names = """const rows_in cols_in wkv_in wq_in w_in dst_in pad vset eset epass cnt idx gat
            var rstd ln xs_ready xn_ready x16 x16c xT xTc KV kvb kc kmin kexp kphi Q qb qmin qexp
            qphi acc kvm cov flag etr ecol tot blkc oh win Aev agg num att atc aggr aggn T1 T1c OG
            og ogc ve1 r1 x1c x1p x1 gxb T2 T2c W1 rel W2 y1 ln2c ve2 r2 z1 x2c x2 ve3 r3 ln3c
            xn2 wsum w base wt wtc wd wrow tail beats beaten rank ohr sids sidc wsc ybj ranked picked T3 T3c F1 gel F2 yoc yo
            sx ssrc sdst sg soh smm sc sacc""".split()
        s = {n: sem("s_" + n) for n in names}
        s_x = [sem(f"s_xload{i}") for i in range(4)]
        s_st = [sem(f"s_xtstore{i}") for i in range(2)]
        s_sq = [sem(f"s_qstore{i}") for i in range(2)]
        s_q = [sem(f"s_qload{i}") for i in range(2)]
        s_xt = [sem(f"s_xtload{i}") for i in range(2)]
        s_xi = [sem(f"s_xiload{i}") for i in range(2)]
        s_bs = [sem(f"s_xbstore{i}") for i in range(2)]
        s_os = [sem(f"s_outstore{i}") for i in range(2)]
        s_gx = [sem(f"s_gather{i}") for i in range(NS)]
        s_sc = [sem(f"s_scatter{i}") for i in range(2)]
        CH = NT // 4

        x_t = x[0:(NT - 1) * P, :].rearrange("(c p) f -> p c f", p=P)
        dst_r = dst.rearrange("(t e) -> t e", e=ER)
        src_r = src.rearrange("(t e) -> t e", e=ER)
        src_c = src.rearrange("(n a) -> n a", a=1)
        dst_c = dst.rearrange("(n a) -> n a", a=1)
        NCONST = 27
        VSET = 15
        block = ctx.enter_context(nc.Block())

        @block.sync
        def _(sp):
            sp.dma_start(dlast[:, :, :], dst.rearrange("(p k e) -> p k e", p=EP, e=ER)).then_inc(s["dst_in"], 16)
            for i in range(4):
                n = min(CH * (i + 1), NT - 1)
                sp.dma_start(xn[:, CH * i:n, :], x_t[:, CH * i:n, :]).then_inc(s_x[i], 16)
            sp.wait_ge(s["pad"], 1)
            sp.dma_start(xn[0:LAST, NT - 1, :], x[N - LAST:N, :]).then_inc(s_x[3], 16)
            for w_sb, w_in in ((wo, w_o), (wl, w_l), (wrr, w_r), (w1, w_1), (w2, w_2), (f1, f_1), (f2, f_2)):
                sp.dma_start(w_sb[:, :, :], w_in.rearrange("(k p) n -> p k n", p=P)).then_inc(s["w_in"], 16)

            def store(st):
                t = st.back(1)
                if t.real():
                    sp.wait_ge(s["xTc"], t.done())
                    sp.dma_start(xq_d[t.i, :, 0:D], xt_s[:, t.par, :]).then_inc(s_st[t.par], 16)
                t = st.back(3)
                if t.real():
                    sp.wait_ge(s["qphi"], t.done())
                    sp.dma_start(xq_d[t.i, :, D:2 * D], qp_s[:, t.par, :]).then_inc(s_sq[t.par], 16)
            steps(sp, NT + 3, store, 5)
            for u in range(2):
                sp.wait_ge(s_st[u], 16 * NT // 2)
                sp.wait_ge(s_sq[u], 16 * NT // 2)

            sp.wait_ge(s["flag"], 1)
            fast = sp.value_load(flag[0:1, 0:1], min_val=0, max_val=1)
            with sp.If(fast == 0):
                sp.wait_ge(s["x16"], NT)
                sp.dma_start(xg_d.rearrange("(c p) f -> p c f", p=P), xn16[:, :, :]).then_inc(s["sx"], 16)
                with sp.Fori(0, ET) as e:
                    wait_apart(sp, s["sacc"], e + 1, (s["flag"], 1))
                    sp.dma_start(sidx[:, :], src_c[bass.ds(e * P, P), :]).then_inc(s["ssrc"], 16)
                    sp.dma_start(didx[:, :], dst_c[bass.ds(e * P, P), :]).then_inc(s["sdst"], 16)

            def load_store(st):
                t3 = st.back(3)
                if t3.real():
                    pair = (xb[:, t3.par, :], xb[:, t3.par, D:2 * D])
                    wait_apart(sp, s["base"], t3.done(), (s["flag"], 1))
                    sp.dma_start(xb_d[bass.ds(t3.i * P, P), :], pair[0]).then_inc(s_bs[t3.par], 16)
                    if t3.j is None and t3.n == NT - 1:
                        sp.dma_start(out[N - LAST:N, :], pair[1][0:LAST, :]).then_inc(s_os[t3.par], 16)
                    else:
                        sp.dma_start(out[bass.ds(t3.i * P, P), :], pair[1]).then_inc(s_os[t3.par], 16)
                t = st.back(-1)

                def q_of(t):
                    if t.real():
                        wait(sp, s["num"], t.back(2).done())
                        sp.dma_start(qs[:, t.par, :], xq_d[t.i, :, D:2 * D]).then_inc(s_q[t.par], 16)
                if st.j is None and st.n == 0:
                    q_of(st)
                q_of(t)
                if st.real():
                    if st.back(2).real():
                        wait_apart(sp, s["OG"], st.back(2).done(), (s["flag"], 1))
                        wait_apart(sp, s["og"], st.back(2).done(), (s["flag"], 1))
                    sp.dma_start(xts[:, st.par, :], xq_d[st.i, :, 0:D]).then_inc(s_xt[st.par], 16)
                    if st.j is None and st.n == NT - 1:
                        sp.dma_start(xin[0:LAST, st.par, :], x[N - LAST:N, :]).then_inc(s_xi[st.par], 16)
                    else:
                        sp.dma_start(xin[:, st.par, :], x[bass.ds(st.i * P, P), :]).then_inc(s_xi[st.par], 16)
            steps(sp, NT + 3, load_store)

            sp.wait_ge(s["wtc"], 1)
            sp.dma_start(w_d.rearrange("(c p) -> c p", p=P), wt[:, :]).then_inc(s["wd"], 16)
            sp.wait_ge(s["wd"], 16)
            sp.wait_ge(s["agg"], NT)
            sp.dma_start(wrow, w_d[0:N].partition_broadcast(P)).then_inc(s["wrow"], 16)
            sp.wait_ge(s["w_in"], 16 * 7)
            for u in range(2):
                sp.wait_ge(s_bs[u], 16 * NT // 2)
                sp.wait_ge(s_os[u], 16 * NT // 2)
                sp.wait_ge(s_sc[u], 16 * NS)

        @block.gpsimd
        def _(pool):
            link = Chain(pool, s["const"], NCONST)
            G.iota(win0[:, :], pattern=[[W, NW]], base=0, channel_multiplier=0,
                   allow_small_or_imprecise_dtypes=True).then_inc(s["eset"], 1)
            G.iota(key0[:, :], pattern=[[-KEYS * GW, WG]], base=0, channel_multiplier=-KEYS,
                   allow_small_or_imprecise_dtypes=True).then_inc(s["eset"], 1)
            G.memset(one16[:, :], 1.0).then_inc(s["eset"], 1)
            link(G.memset(minus_half[:, :], -0.5))
            link(G.memset(ident[:, :], 0.0))
            link(G.affine_select(out=ident[:, :], in_=ident[:, :], compare_op=ALU.not_equal, fill=1.0, base=0,
                                 pattern=[[-1, P]], channel_multiplier=1))
            for u in range(2):
                link(G.memset(vv[:, u, :, P:P + 1], 1.0))
            pool.wait_ge(s["var"], 1)
            G.tensor_tensor(rstd[:, 0:CH], ve[:, 0:CH], minus_half[:, 0:CH], ALU.pow).then_inc(s["rstd"], 1)
            pool.wait_ge(s["idx"], 1)
            for g in range(WG):
                for buf, tab in ((e_a, src_r), (e_b, dst_r)):
                    G.indirect_dma_start(buf[:, g, :], None, tab[:, :],
                                         bass.IndirectOffsetOnAxis(ap=gidx[:, g:g + 1], axis=0)).then_inc(s["gat"], 16)
            pool.wait_ge(s["var"], 2)
            G.tensor_tensor(rstd[:, CH:NT], ve[:, CH:NT], minus_half[:, CH:NT], ALU.pow).then_inc(s["rstd"], 1)
            link(G.memset(ones[:, :], 1.0))
            link(G.memset(scale_lo[:, :], LO))
            link(G.iota(iota[:, :, :], pattern=[[1, KEYS], [0, TPP]], base=0, channel_multiplier=0,
                        allow_small_or_imprecise_dtypes=True))
            link(G.memset(same_head[:, :], 0.0))
            link(G.memset(head_of[:, :], 0.0))
            link(G.memset(later[:, :], 1.0))
            link(G.affine_select(out=later[:, :], in_=later[:, :], compare_op=ALU.is_gt, fill=0.0, base=0,
                                 pattern=[[1, P]], channel_multiplier=-1))
            link(G.iota(tok[:, :, 0], pattern=[[0, NT]], base=0, channel_multiplier=1,
                        allow_small_or_imprecise_dtypes=True))
            link(G.iota(tok[:, :, 1], pattern=[[1, NT]], base=0, channel_multiplier=0,
                        allow_small_or_imprecise_dtypes=True))
            link(G.iota(n_later[:, :], pattern=[[-P, NT]], base=N - 1, channel_multiplier=-1,
                        allow_small_or_imprecise_dtypes=True))
            link(G.memset(ahead[:, :], 0.0))
            for h in range(HPC):
                r = slice(h * DH, (h + 1) * DH)
                link(G.memset(same_head[r, r], 1.0))
                link(G.memset(head_of[r, h:h + 1], 1.0))
            link(G.memset(acc[:, :, :], 0.0))
            link(G.memset(dacc[:, :], 0.0))
            pool.wait_ge(s["rows_in"], 16)
            link(G.tensor_tensor(cgb[:, :], row["bg"], row["c2"], ALU.add))
            assert link.n == link.per

            with pool.Fori(0, NT) as t:
                c16 = Chain(pool, s["x16c"], 2, t)
                wait_apart(pool, s["xn_ready"], t + 1, (s["var"], 1))
                xt = xn[:, bass.ds(t, 1), :].rearrange("p a f -> p (a f)")
                hi = xn16[:, bass.ds(t, 1), 0:D].rearrange("p a f -> p (a f)")
                lo = xn16[:, bass.ds(t, 1), D:2 * D].rearrange("p a f -> p (a f)")
                c16(G.tensor_copy(hi, xt), met=(s["var"], 1))
                c16(G.tensor_tensor(lo32[:, :], xt, hi, ALU.subtract), met=(s["var"], 1))
                G.tensor_tensor(lo, lo32[:, :], scale_lo[:, :].broadcast_to([P, D]), ALU.mult).then_inc(s["x16"], 1)

            pool.wait_ge(s["flag"], 1)
            fast = pool.value_load(flag[0:1, 0:1], min_val=0, max_val=1)
            with pool.If(fast == 0):
                pool.wait_ge(s["sx"], 16)
                with pool.Fori(0, ET) as e:
                    wait_apart(pool, s["ssrc"], (e + 1) * 16, (s["flag"], 1))
                    G.indirect_dma_start(msg[:, :], None, xg_d[:, :],
                                         bass.IndirectOffsetOnAxis(ap=sidx[:, 0:1], axis=0)).then_inc(s["sg"], 16)

            def norm_tail(st):
                t1, t2 = st.back(1), st.back(2)
                if t1.real():
                    pool.wait_ge(s["ve1"], t1.done())
                    G.tensor_tensor(rs[:, 0:1], ves[:, 0:1], minus_half[:, 0:1], ALU.pow).then_inc(s["r1"], 1)
                    pool.wait_ge(s["og"], t1.done())
                    wait(pool, s["x2"], t1.back(2).done())
                    G.tensor_tensor(gxb[:, t1.par, :], gx[:, :], cgb[:, :], ALU.add).then_inc(s["gxb"], 1)
                    pool.wait_ge(s["x1c"], t1.done())
                    G.tensor_tensor(x1a[:, :], x1a[:, :], row["g1"], ALU.mult).then_inc(s["x1p"], 1)
                    pool.wait_ge(s["x1p"], t1.done())
                    wait(pool, s["T2"], t1.back(2).done())
                    wait(pool, s["ve2"], t1.back(2).done())
                    G.tensor_tensor(x1[:, t1.par, :], x1a[:, :], row["c1"], ALU.add).then_inc(s["x1"], 1)
                if t2.real():
                    pool.wait_ge(s["ve2"], t2.done())
                    G.tensor_tensor(rs[:, 1:2], ves[:, 1:2], minus_half[:, 0:1], ALU.pow).then_inc(s["r2"], 1)
                    pool.wait_ge(s["z1"], t2.done())
                    G.tensor_tensor(z1[:, :], z1[:, :], row["g2"], ALU.mult).then_inc(s["x2c"], 1)
                    pool.wait_ge(s["x2c"], t2.done())
                    G.tensor_tensor(x2[:, :], z1[:, :], gxb[:, t2.par, :], ALU.add).then_inc(s["x2"], 1)
                    pool.wait_ge(s["ve3"], t2.done())
                    G.tensor_tensor(rs[:, 2:3], ves[:, 2:3], minus_half[:, 0:1], ALU.pow).then_inc(s["r3"], 1)
                    wait_apart(pool, s["xn2"], t2.done(), (s["flag"], 1))
                    G.tensor_tensor(xb[:, t2.par, D:2 * D], x2[:, :], xb[:, t2.par, 0:D], ALU.add).then_inc(s["base"], 1)
            pool.wait_ge(s["const"], NCONST)
            steps(pool, NT + 2, norm_tail)

            pool.wait_ge(s["agg"], NT)
            pool.wait_ge(s["num"], NT)
            G.iota(places[:, :], pattern=[[1, SLOTS]], base=0, channel_multiplier=0,
                   allow_small_or_imprecise_dtypes=True).then_inc(s["tail"], 1)
            pool.wait_ge(s["sids"], 1)
            pool.wait_ge(s["aggr"], NT)
            for u in range(2):
                pool.wait_ge(s_bs[u], 16 * NT // 2)
            for c in range(2 * NS):
                G.indirect_dma_start(gx2[:, c, :], None, xb_d[:, :],
                                     bass.IndirectOffsetOnAxis(ap=sid[:, c:c + 1], axis=0)).then_inc(s_gx[c // 2], 16)
            for u in range(2):
                pool.wait_ge(s_os[u], 16 * NT // 2)
            for c in range(2 * NS):
                r = min(P, KEEP - c * P)
                pool.wait_ge(s["yo"], c + 1)
                G.indirect_dma_start(out[:, :], bass.IndirectOffsetOnAxis(ap=sid[0:r, c:c + 1], axis=0),
                                     yo[0:r, c % 2, :], None).then_inc(s_sc[c % 2], 16)

        @block.scalar
        def _(act):
            act.dma_start(wkv[:, :, 0:D], w_k.rearrange("(k p) n -> p k n", p=P)).then_inc(s["wkv_in"], 16)
            act.dma_start(wkv[:, :, D:2 * D], w_v.rearrange("(k p) n -> p k n", p=P)).then_inc(s["wkv_in"], 16)
            act.dma_start(wq[:, :, :], w_q.rearrange("(k p) n -> p k n", p=P)).then_inc(s["wq_in"], 16)
            act.dma_start(colt[:, :], cols).then_inc(s["cols_in"], 16)
            act.dma_start(rowt[:, :], rows.partition_broadcast(P)).then_inc(s["rows_in"], 16)
            act.wait_ge(s["cols_in"], 16)

            def qkv(st):
                t = st.back(1)
                if t.real():
                    act.wait_ge(s["xT"], t.done())
                    wait(act, s["Q"], t.back(2).done())
                    if t.j is not None or t.n >= 2:
                        act.wait_ge(s_st[t.par], t.half * 16)
                    A.activation(xt_s[:, t.par, :], pT[t.par][:, 0:D], ACT.Copy).then_inc(s["xTc"], 1)
                t = st.back(2)
                if t.real():
                    act.wait_ge(s["Q"], t.done())
                    wait(act, s["qphi"], t.back(1).done())
                    for m in range(DK):
                        i = A.activation(qb[:, m * P:(m + 1) * P], pQ[t.par][:, m * P:(m + 1) * P], ACT.Identity,
                                         bias=bq[:, m:m + 1])
                    i.then_inc(s["qb"], 1)
                    act.wait_ge(s["kmin"], t.done())
                    wait(act, s["kphi"], t.back(1).done())
                    A.activation(kexp[:, :], kmin[:, :], ACT.Exp).then_inc(s["kexp"], 1)
                    act.wait_ge(s["qmin"], t.done())
                    A.activation(qexp[:, :], qmin[:, :], ACT.Exp).then_inc(s["qexp"], 1)
            steps(act, NT + 2, qkv, 5)

            def adj_out(a, w):
                act.wait_ge(s["win"], a.i * PPB + w + 1)
                if w == 0:
                    wait(act, s["num"], a.back(2).done())
                A.activation(adj[:, a.par, :, w * 2 * W:(w + 1) * 2 * W],
                             pW[w % 2][:, 0:2 * KEYS].rearrange("p (d c) -> p c d", c=NT), ACT.Copy).then_inc(s["Aev"], 1)

            def mix(st):
                a, t1, t2 = st, st.back(1), st.back(2)
                if a.real():
                    adj_out(a, 0)
                if t2.real():
                    act.wait_ge(s["T2"], t2.done())
                    wait(act, s["W1"], t2.back(1).done(2))
                    A.activation(x1t[:, :, :].rearrange("p k q -> p (k q)"), pX[:, 0:D], ACT.Copy).then_inc(s["T2c"], 1)
                if a.real():
                    adj_out(a, 1)
                if t2.real():
                    wait(act, s["W2"], t2.back(1).done())
                    for m in range(HK):
                        act.wait_ge(s["W1"], t2.i * 2 + m // 4 + 1)
                        i = A.activation(ht[:, m, :], pH[m // 4][:, (m % 4) * P:(m % 4 + 1) * P], ACT.Relu,
                                         bias=b1c[:, m:m + 1])
                        if m % 4 == 3:
                            i.then_inc(s["rel"], 1)
                if t1.real():
                    act.wait_ge(s["T1"], t1.done())
                    wait(act, s["OG"], t1.back(1).done())
                    A.activation(at_t[:, :, :].rearrange("p k q -> p (k q)"), pX[:, :], ACT.Copy).then_inc(s["T1c"], 1)
                if a.real():
                    adj_out(a, 2)
                if a.real():
                    for w in range(3, PPB):
                        adj_out(a, w)
            steps(act, NT + 2, mix)

            for c in range(NT):
                r = min(P, N - c * P)
                act.wait_ge(s["beats"], c + 1)
                wait(act, s["beaten"], c - 1)
                A.activation(scrap[0:r, c % 2, 0:N - c * P],
                             beats[0:r, c % 2, c * P:N], ACT.Copy, accum_out=ahead[0:r, c:c + 1]).then_inc(s["beaten"], 1)

            for q in range(NS):
                act.wait_ge(s["T3"], q + 1)
                A.activation(x2t[:, :, :].rearrange("p k q -> p (k q)"), pX[:, :], ACT.Copy).then_inc(s["T3c"], 1)
                for m in range(HK):
                    if m % 2 == 0:
                        act.wait_ge(s["F1"], q * HK // 2 + m // 2 + 1)
                    if m == 0:
                        wait(act, s["F2"], (q - 1) * 2)
                    i = A.activation(gt[:, q % 2, m, :], pF[m // 2][:, m % 2 * 2 * P:(m % 2 + 1) * 2 * P],
                                     ACT.Gelu_apprx_tanh, bias=fb1c[:, m:m + 1])
                    if m % 2 == 1:
                        i.then_inc(s["gel"], 1)

        @block.vector
        def _(dve):
            link = Chain(dve, s["vset"], 40)
            V.memset(xn[LAST // 32 * 32:P, NT - 1, :], 0.0).then_inc(s["pad"], 1)
            dve.wait_ge(s["dst_in"], 16)
            link(V.tensor_copy(dlastf[:, :], dlast[:, :, ER - 1]))
            dve.wait_ge(s["eset"], 3)
            for k in range(EK):
                i = V.tensor_scalar(passed[:, k, :], win0[:, :], dlastf[:, k:k + 1], None, ALU.is_gt)
            i.then_inc(s["epass"], 1)

            for q in range(4):
                dve.wait_ge(s_x[q], 16 if q < 3 else 32)
                for c in range(CH * q, CH * (q + 1)):
                    i = V.bn_stats(stats[:, c, :], xn[:, c, :])
                if q in (0, 3):
                    lot = slice(0, CH) if q == 0 else slice(CH, NT)
                    link(i)
                    for c in range(lot.start, lot.stop):
                        i = V.bn_aggr(mv[:, c, :], stats[:, c, :])
                    link(i)
                    V.tensor_scalar(ve[:, lot], mv[:, lot, 1], EPS, None, ALU.add).then_inc(s["var"], 1)
                if q == 0:
                    dve.wait_ge(s["cnt"], 1)
                    V.tensor_scalar(gidx[:, :], pT[0][0:GW, 0:WG], float((E - RUN) // ER), None,
                                    ALU.min).then_inc(s["idx"], 1)
            dve.wait_ge(s["rstd"], 1)

            e_f = [e[:, :, :].bitcast(f32) for e in (e_a, e_b, e_c, e_d)]

            def sources():
                dve.wait_ge(s["gat"], 16 * 2 * WG)
                link(V.tensor_scalar(e_c[:, :, :], e_a[:, :, :], 7, None, ALU.logical_shift_right))
                link(V.tensor_scalar(e_d[:, :, :], e_a[:, :, :], P - 1, None, ALU.bitwise_and))

            def edge_keys():
                link(V.tensor_copy(e_f[0], e_d[:, :, :]))
                for g in range(WG):
                    i = V.tensor_scalar(e_f[3][:, g, :], e_b[:, g, :], float(NT), key0[:, g:g + 1], ALU.mult, ALU.add)
                link(i)

            def count_found():
                link(V.tensor_tensor(e_f[3], e_f[3], e_c[:, :, :], ALU.add))
                link(V.tensor_scalar(e_f[1], e_f[3], 0.0, None, ALU.is_ge))
                V.scalar_tensor_tensor(out=e_f[2].rearrange("p a b -> p (a b)"),
                                       in0=e_f[3].rearrange("p a b -> p (a b)"), scalar=float(KEYS),
                                       in1=e_f[1].rearrange("p a b -> p (a b)"),
                                       op0=ALU.is_lt, op1=ALU.mult, accum_out=cov[:, :]).then_inc(s["cov"], 1)
            edge_work = {2: sources, NT: edge_keys, NT + 1: count_found}

            def qkv(st):
                if st.real():
                    t = st
                    xt = xn[:, bass.ds(t.i, 1), :].rearrange("p a f -> p (a f)")
                    m = mv[:, bass.ds(t.i, 1), 0:1].rearrange("p a f -> p (a f)")
                    r = rstd[:, bass.ds(t.i, 1)]
                    wait(dve, s["xT"], t.back(2).done())
                    V.tensor_scalar(xs[:, t.par, :], xt, m, r, ALU.subtract, ALU.mult).then_inc(s["xs_ready"], 1)
                    V.tensor_scalar(xt, xt, m, r, ALU.subtract, ALU.mult).then_inc(s["xn_ready"], 1)
                    if t.j is None and t.n == 0:
                        dve.wait_ge(s["rows_in"], 16)
                    if t.j is None and t.n == 2:
                        dve.wait_ge(s["rstd"], 2)
                t = st.back(3)
                if t.real():
                    dve.wait_ge(s["kexp"], t.done())
                    wait(dve, s["acc"], t.back(2).done())
                    V.scalar_tensor_tensor(out=kphi[:, t.par, :], in0=kb[:, :], scalar=0.0, in1=kexp[:, :],
                                           op0=ALU.max, op1=ALU.add).then_inc(s["kphi"], 1)
                    dve.wait_ge(s["qexp"], t.done())
                    if t.j is not None or t.n >= 2:
                        dve.wait_ge(s_sq[t.par], t.half * 16)
                    V.scalar_tensor_tensor(out=qp_s[:, t.par, :], in0=qb[:, :], scalar=0.0, in1=qexp[:, :],
                                           op0=ALU.max, op1=ALU.add).then_inc(s["qphi"], 1)
                t = st.back(2)
                if t.real():
                    dve.wait_ge(s["KV"], t.done())
                    wait(dve, s["kphi"], t.back(1).done())
                    V.tensor_tensor(kb[:, :], pKV[t.par][:, 0:D], row["bk"], ALU.add).then_inc(s["kc"], 1)
                    wait(dve, s["acc"], t.back(2).done())
                    V.tensor_tensor(vv[:, t.par, :, 0:P], pKV[t.par][:, D:2 * D].rearrange("p (k f) -> p k f", k=DK),
                                    row["bv"].rearrange("p (k f) -> p k f", k=DK), ALU.add).then_inc(s["kvb"], 1)
                    dve.wait_ge(s["kc"], t.done())
                    wait(dve, s["kexp"], t.back(1).done())
                    V.tensor_scalar(kmin[:, :], kb[:, :], 0.0, None, ALU.min).then_inc(s["kmin"], 1)
                    dve.wait_ge(s["qb"], t.done())
                    wait(dve, s["qexp"], t.back(1).done())
                    V.tensor_scalar(qmin[:, :], qb[:, :], 0.0, None, ALU.min).then_inc(s["qmin"], 1)
                if st.j is None and st.n in edge_work:
                    edge_work[st.n]()
            steps(dve, NT + 3, qkv, 5)

            dve.wait_ge(s["acc"], NT)
            dve.wait_ge(s["const"], NCONST)
            for k in range(DK):
                V.tensor_tensor(kvm[:, k, 0:P], pAcc[k][:, 0:P], same_head[:, :], ALU.mult)
                i = V.tensor_copy(ksum[:, k:k + 1], pAcc[k][:, P:P + 1])
            link(i)
            for k in range(DK):
                i = V.tensor_scalar(kvm[:, k, P:CW], head_of[:, :], ksum[:, k:k + 1], None, ALU.mult)
            i.then_inc(s["kvm"], 1)

            dve.wait_ge(s["tot"], 1)
            link(V.tensor_scalar(covered[:, :], pQ[0][:, 0:1], float(E), None, ALU.is_equal))
            link(V.tensor_scalar(covered_m1[:, :], covered[:, :], -1.0, None, ALU.add))
            V.tensor_copy(flag[:, :], covered[:, :]).then_inc(s["flag"], 1)
            dve.wait_ge(s["etr"], 1)
            for h in range(2):
                half = slice(h * 2 * GW * TPW, (h + 1) * 2 * GW * TPW)
                o = [c[:, half].rearrange("p (g w j) -> p g j w", g=2, j=TPW) for c in (scol, kcol)]
                in_ = [b[h][:, 0:2 * GW * TPW].rearrange("p (g j w) -> p g j w", g=2, j=TPW) for b in (pT, pKV)]
                V.tensor_copy(o[0], in_[0])
                i = V.tensor_scalar(o[1], in_[1], covered[:, :], covered_m1[:, :], ALU.mult, ALU.add)
            link(i)
            assert link.n == VSET, link.n

            dve.wait_ge(s["flag"], 1)
            fast = dve.value_load(flag[0:1, 0:1], min_val=0, max_val=1)
            with dve.If(fast == 0):
                V.memset(dcol[:, :], 0.0).then_inc(s["sacc"], 1)
                dve.wait_ge(s["sacc"], 1)
                with dve.Fori(0, ET) as e:
                    dve.wait_ge(s["sdst"], (e + 1) * 16)
                    V.tensor_copy(dcol[:, :], didx[:, :]).then_inc(s["sc"], 1)
                    with dve.Fori(0, NT) as b:
                        n = e * (4 * NT + 1) + b * 4 + 1
                        dve.wait_ge(s["sc"], n)
                        V.tensor_scalar(oh_e[:, :], iota[:, 0:P, 0], dcol[:, :], None, ALU.is_equal).then_inc(s["soh"], 1)
                        dve.wait_ge(s["smm"], e * NT + b + 1)
                        ab = acc[:, bass.ds(b, 1), :].rearrange("p a f -> p (a f)")
                        db = dacc[:, bass.ds(b, 1)]
                        V.tensor_tensor(ab, pG[:, 0:D], ab, ALU.add).then_inc(s["sc"], 1)
                        dve.wait_ge(s["sc"], n + 1)
                        V.scalar_tensor_tensor(out=ab, in0=pG[:, D:2 * D], scalar=1 / LO, in1=ab, op0=ALU.mult,
                                               op1=ALU.add).then_inc(s["sc"], 1)
                        V.tensor_tensor(db, pN[:, 0:1], db, ALU.add).then_inc(s["sc"], 1)
                        V.tensor_scalar(dcol[:, :], dcol[:, :], -float(P), None, ALU.add).then_inc(s["sc"], 1)
                    dve.wait_ge(s["sc"], (e + 1) * (4 * NT + 1))
                    V.tensor_copy(dcol[:, :], didx[:, :]).then_inc(s["sacc"], 1)

            def one_hots(a, w):
                if w == 0:
                    bc = Chain(dve, s["blkc"], 1, a.i)
                    for n, c in enumerate((scol, kcol)):
                        i = V.tensor_copy(blk[:, a.par, n, :], c[:, bass.ds(a.i * (WPB * TPW), WPB * TPW)])
                    bc(i)
                if w >= OH or a.j is not None or a.n > 0:
                    dve.wait_ge(s["win"], a.i * PPB + w + 1 - OH)
                for c, (oh, n) in enumerate(((oh_s, P), (oh_k, KEYS))):
                    of_pair = blk[:, a.par, c, w * TPP:(w + 1) * TPP].unsqueeze(1).broadcast_to([P, n, TPP])
                    i = V.tensor_tensor(oh[:, w % OH, :, :], iota[:, 0:n, :], of_pair, ALU.is_equal)
                i.then_inc(s["oh"], 1)

            def heads_and_mean(t):
                lk = Chain(dve, s["atc"], 5, t.i)
                dve.wait_ge(s["num"], t.done())
                state = pN[:, 0:DK * CW].rearrange("p (k c) -> p k c", k=DK)
                V.tensor_tensor(deg[:, 0:1], pN[:, DK * CW:DK * CW + 1], dacc[:, bass.ds(t.i, 1)], ALU.add)
                lk(V.tensor_scalar(den[:, 0, :].rearrange("p (k h) -> p k h", k=DK), state[:, :, P:CW], 1e-6, None,
                                   ALU.add))
                V.tensor_scalar(deg[:, 1:2], deg[:, 0:1], 1.0, None, ALU.max)
                lk(V.reciprocal(den[:, 1, :], den[:, 0, :]))
                lk(V.reciprocal(deg[:, 2:3], deg[:, 1:2]))
                wait(dve, s["T1"], t.back(1).done())
                V.tensor_tensor(at_in[:, 2:4, :].rearrange("p k (h f) -> p k h f", h=HPC),
                                state[:, :, 0:P].rearrange("p k (h f) -> p k h f", h=HPC),
                                den[:, 1, :].rearrange("p (k h) -> p k h", k=DK).unsqueeze(3).broadcast_to(
                                    [P, DK, HPC, DH]), ALU.mult).then_inc(s["att"], 1)
                dve.wait_ge(s["agg"], t.done())
                lk(V.tensor_tensor(agg1[:, :], pG[:, 0:D], acc[:, bass.ds(t.i, 1), :].rearrange("p a f -> p (a f)"),
                                   ALU.add))
                V.scalar_tensor_tensor(out=agg1[:, :], in0=pG[:, D:2 * D], scalar=1 / LO, in1=agg1[:, :],
                                       op0=ALU.mult, op1=ALU.add).then_inc(s["aggr"], 1)
                dve.wait_ge(s["aggr"], t.done())
                lk(V.tensor_scalar(at_in[:, 0:2, :].rearrange("p k f -> p (k f)"), agg1[:, :], deg[:, 2:3], None,
                                   ALU.mult))

            def statistics(lk, n, r, out_sem):
                lk(V.bn_stats(bn[:, n, :], r), met=(s["kvm"], 1))
                lk(V.bn_aggr(mvs[:, n, :], bn[:, n, :]))
                V.tensor_scalar(ves[:, n:n + 1], mvs[:, n, 1:2], EPS, None, ALU.add).then_inc(out_sem, 1)

            def after_attention(t):
                lk = Chain(dve, s["ogc"], 4, t.i)
                dve.wait_ge(s["OG"], t.done())
                V.tensor_tensor(r1[:, :], pN[:, 0:D], row["bo"], ALU.add).then_inc(s["ogc"], 1)
                dve.wait_ge(s_xi[t.par], (t.half + 1) * 16)
                wait(dve, s["gxb"], t.back(1).done())
                V.tensor_tensor(gx[:, :], pN[:, D:2 * D], xin[:, t.par, :], ALU.add).then_inc(s["og"], 1)
                lk.n = 1
                dve.wait_ge(s["ogc"], lk.base + 1)
                lk(V.tensor_tensor(r1[:, :], r1[:, :], xn[:, bass.ds(t.i, 1), :].rearrange("p a f -> p (a f)"), ALU.add))
                statistics(lk, 0, r1[:, :], s["ve1"])

            def norm1(t):
                dve.wait_ge(s["r1"], t.done())
                wait(dve, s["x1"], t.back(1).done())
                V.tensor_scalar(x1a[:, :], r1[:, :], mvs[:, 0, 0:1], rs[:, 0:1], ALU.subtract, ALU.mult).then_inc(s["x1c"], 1)

            def after_ff(t):
                lk = Chain(dve, s["ln2c"], 3, t.i)
                dve.wait_ge(s["W2"], t.done())
                V.tensor_tensor(r2[:, :], pY[:, 0:D], row["b2"], ALU.add).then_inc(s["y1"], 1)
                dve.wait_ge(s["y1"], t.done())
                dve.wait_ge(s["x1"], t.done())
                lk(V.tensor_tensor(r2[:, :], r2[:, :], x1[:, t.par, :], ALU.add))
                lk(V.bn_stats(bn[:, 1, :], r2[:, :]), met=(s["kvm"], 1))
                lk(V.bn_aggr(mvs[:, 1, :], bn[:, 1, :]))
                V.tensor_scalar(ves[:, 1:2], mvs[:, 1, 1:2], EPS, None, ALU.add).then_inc(s["ve2"], 1)

            def norm2(t):
                dve.wait_ge(s["r2"], t.done())
                wait(dve, s["x2"], t.back(1).done())
                V.tensor_scalar(z1[:, :], r2[:, :], mvs[:, 1, 0:1], rs[:, 1:2], ALU.subtract, ALU.mult).then_inc(s["z1"], 1)

            def stats3(t):
                lk = Chain(dve, s["ln3c"], 2, t.i)
                dve.wait_ge(s["x2"], t.done())
                statistics(lk, 2, x2[:, :], s["ve3"])

            def norm3(t):
                dve.wait_ge(s["r3"], t.done())
                wait(dve, s["base"], t.back(2).done())
                if t.j is not None or t.n >= 2:
                    dve.wait_ge(s_bs[t.par], t.half * 16)
                    dve.wait_ge(s_os[t.par], t.half * 16)
                V.tensor_scalar(xb[:, t.par, 0:D], x2[:, :], mvs[:, 2, 0:1], rs[:, 2:3], ALU.subtract, ALU.mult).then_inc(s["xn2"], 1)
                dve.wait_ge(s["xn2"], t.done())
                V.tensor_tensor_reduce(out=yb[:, :], in0=xb[:, t.par, 0:D], in1=row["wr"], scale=1.0, scalar=0.0,
                                       op0=ALU.mult, op1=ALU.add, accum_out=wraw[:, :]).then_inc(s["wsum"], 1)
                dve.wait_ge(s["wsum"], t.done())
                V.tensor_tensor(wall[:, bass.ds(t.i, 1)], wraw[:, :], br, ALU.add).then_inc(s["w"], 1)

            def mix(st):
                a, t1, t2 = st, st.back(1), st.back(2)
                if t1.real():
                    heads_and_mean(t1)
                if a.real():
                    for w in range(OH, PPB):
                        one_hots(a, w)
                if t1.real():
                    after_attention(t1)
                    norm1(t1)
                if t2.real():
                    after_ff(t2)
                b = st.back(-1)
                if b.real():
                    one_hots(b, 0)
                if t2.real():
                    norm2(t2)
                if b.real():
                    one_hots(b, 1)
                if t2.real():
                    stats3(t2)
                if b.real():
                    one_hots(b, 2)
                if t2.real():
                    norm3(t2)
                if b.real():
                    one_hots(b, 3)
            first_block = Tile(0)
            for w in range(OH):
                one_hots(first_block, w)
            steps(dve, NT + 2, mix)

            dve.wait_ge(s["wt"], 1)
            V.tensor_copy(wt[:, :], pX[0:NT, 0:P]).then_inc(s["wtc"], 1)
            dve.wait_ge(s["agg"], NT)
            V.memset(beats[:, :, N:NT * P], 0.0)
            dve.wait_ge(s["wrow"], 16)
            for c in range(NT):
                r = min(P, N - c * P)
                lo, hi = c * P, c * P + r
                wait(dve, s["beaten"], c - 1)
                wait(dve, s["ranked"], c - 1)
                me = wall[0:r, c:c + 1]
                i = V.scalar_tensor_tensor(out=beats[0:r, c % 2, lo:hi], in0=wrow[0:r, lo:hi], scalar=me,
                                           in1=later[0:r, 0:r], op0=ALU.is_le, op1=ALU.mult)
                if hi < N:
                    i = V.tensor_scalar(beats[0:r, c % 2, hi:N], wrow[0:r, hi:N], me, None, ALU.is_le)
                i.then_inc(s["beats"], 1)
            rl = Chain(dve, s["rank"], 2)
            dve.wait_ge(s["beaten"], NT)
            rl(V.tensor_tensor(rank[:, :], n_later[:, :], ahead[:, :], ALU.subtract))
            dve.wait_ge(s["ranked"], NT)
            rl(V.tensor_tensor(rank[:, :], rank[:, :], pN[:, 0:NT], ALU.add))
            dve.wait_ge(s["tail"], 1)
            for c in range(NT):
                r = min(P, N - c * P)
                wait(dve, s["picked"], c - 1)
                V.tensor_scalar(oh_r[0:r, c % 2, :], places[0:r, :], rank[0:r, c:c + 1], None,
                                ALU.is_equal).then_inc(s["ohr"], 1)
            dve.wait_ge(s["picked"], NT)
            V.tensor_copy(stok[:, :, :].rearrange("p c a -> p (c a)"), pY[:, 0:4 * NS]).then_inc(s["sidc"], 1)
            dve.wait_ge(s["sidc"], 1)
            V.scalar_tensor_tensor(out=sid[:, :], in0=stok[:, :, 1], scalar=float(P), in1=stok[:, :, 0],
                                   op0=ALU.mult, op1=ALU.add).then_inc(s["sids"], 1)

            for q in range(NS):
                wk = Chain(dve, s["wsc"], 1, q)
                dve.wait_ge(s_gx[q], 32)
                wait(dve, s["yo"], 2 * q)
                for u in range(2):
                    if u:
                        dve.wait_ge(s["ybj"], 2 * q + 1)
                    i = V.tensor_tensor_reduce(out=yb[:, :], in0=gx2[:, 2 * q + u, 0:D], in1=row["wr"], scale=1.0,
                                               scalar=0.0, op0=ALU.mult, op1=ALU.add, accum_out=ws[:, 0, u:u + 1])
                    i.then_inc(s["ybj"], 1)
                dve.wait_ge(s["ybj"], 2 * q + 2)
                wk(V.tensor_scalar(ws[:, 1, :], ws[:, 0, :], br, None, ALU.add))
                for u in range(2):
                    c = 2 * q + u
                    dve.wait_ge(s["F2"], c + 1)
                    wait(dve, s_sc[u], 16 * q)
                    V.tensor_tensor(yo[:, u, :], pR[u][:, 0:D], row["fb2"], ALU.add).then_inc(s["yoc"], 1)
                    dve.wait_ge(s["yoc"], c + 1)
                    V.scalar_tensor_tensor(out=yo[:, u, :], in0=yo[:, u, :], scalar=ws[:, 1, u:u + 1],
                                           in1=gx2[:, c, D:2 * D], op0=ALU.mult, op1=ALU.add).then_inc(s["yo"], 1)

        @block.tensor
        def _(pe):
            pe.wait_ge(s["epass"], 1)
            for g in range(WG):
                for k in range(EK):
                    i = T.matmul(pT[0][0:GW, g:g + 1], passed[:, k, g * GW:(g + 1) * GW], one16[0:EP, :],
                                 start=(k == 0), stop=(k == EK - 1))
            i.then_inc(s["cnt"], 1)
            pe.wait_ge(s["idx"], 1)
            pe.wait_ge(s["const"], 5)
            pe.wait_ge(s["wkv_in"], 32)
            pe.wait_ge(s["wq_in"], 16)

            def qkv(st):
                t = st.back(1)
                if t.real():
                    pe.wait_ge(s["xs_ready"], t.done())
                    wait(pe, s["xTc"], t.back(2).done())
                    for k in range(DK):
                        i = T.transpose(pT[t.par][:, k * P:(k + 1) * P], xs[:, t.par, k * P:(k + 1) * P], ident[:, :])
                    i.then_inc(s["xT"], 1)
                t = st.back(2)
                if t.real():
                    pe.wait_ge(s["xTc"], t.done())
                    wait(pe, s["kvb"], t.back(2).done())
                    for k in range(DK):
                        i = T.matmul(pKV[t.par][:, :], xt_s[:, t.par, k * P:(k + 1) * P], wkv[:, k, :],
                                     start=(k == 0), stop=(k == DK - 1))
                    i.then_inc(s["KV"], 1)
                    wait(pe, s["qb"], t.back(2).done())
                    for m in range(DK):
                        for k in range(DK):
                            i = T.matmul(pQ[t.par][:, m * P:(m + 1) * P], wq[:, k, m * P:(m + 1) * P],
                                         xt_s[:, t.par, k * P:(k + 1) * P], start=(k == 0), stop=(k == DK - 1))
                    i.then_inc(s["Q"], 1)
                t = st.back(3)
                if t.real():
                    r = LAST if t.j is None and t.n == NT - 1 else P
                    pe.wait_ge(s["kphi"], t.done())
                    for k in range(DK):
                        i = T.matmul(pAcc[k][:, 0:P + 1], kphi[0:r, t.par, k * P:(k + 1) * P], vv[0:r, t.par, k, :],
                                     start=(t.j is None and t.n == 0), stop=(t.j is None and t.n == NT - 1))
                    i.then_inc(s["acc"], 1)
            steps(pe, NT + 3, qkv, 5)

            pe.wait_ge(s["cov"], 1)
            pe.wait_ge(s["const"], NCONST)
            T.matmul(pQ[0][:, 0:1], ones[0:GW, :], cov[:, :], start=True, stop=True).then_inc(s["tot"], 1)
            for g in range(WG):
                for j in range(TPW):
                    for bk, e in ((pT[g // 2], e_a), (pKV[g // 2], e_d)):
                        col = (g % 2 * TPW + j) * GW
                        i = T.transpose(bk[:, col:col + GW], e[:, g, j * P:(j + 1) * P].bitcast(f32),
                                        ident[0:GW, 0:GW])
            i.then_inc(s["etr"], 1)

            pe.wait_ge(s["flag"], 1)
            fast = pe.value_load(flag[0:1, 0:1], min_val=0, max_val=1)
            with pe.If(fast == 0):
                with pe.Fori(0, ET) as e:
                    wait_apart(pe, s["sg"], (e + 1) * 16, (s["flag"], 1))
                    with pe.Fori(0, NT) as b:
                        pe.wait_ge(s["soh"], e * NT + b + 1)
                        T.matmul(pG[:, :], oh_e[:, :], msg[:, :], start=True, stop=True)
                        T.matmul(pN[:, 0:1], oh_e[:, :], one16[:, :], start=True, stop=True).then_inc(s["smm"], 1)

            pe.wait_ge(s["w_in"], 16 * 7)
            pe.wait_ge(s["kvm"], 1)
            pe.wait_ge(s["x16"], NT)
            pe.wait_ge(s["vset"], VSET)

            def window(a, w):
                pe.wait_ge(s["oh"], a.i * PPB + w + 1)
                if w >= 2 or a.j is not None or a.n > 0:
                    pe.wait_ge(s["Aev"], a.i * PPB + w - 1)
                for h in range(2):
                    for j in range(TPW):
                        i = T.matmul(pW[w % 2][:, h * KEYS:(h + 1) * KEYS], oh_s[:, w % OH, :, h * TPW + j],
                                     oh_k[:, w % OH, :, h * TPW + j], start=(j == 0), stop=(j == TPW - 1))
                i.then_inc(s["win"], 1)

            def to_hidden(w_sb, xt, out_sem):
                for m in range(HK):
                    for k in range(DK):
                        i = T.matmul(pH[m // 4][:, (m % 4) * P:(m % 4 + 1) * P], w_sb[:, k, m * P:(m + 1) * P],
                                     xt[:, k, :], start=(k == 0), stop=(k == DK - 1))
                    if m % 4 == 3:
                        i.then_inc(out_sem, 1)

            def from_hidden(w_sb, h, in_sem, t, out_sem):
                for m in range(HK):
                    pe.wait_ge(in_sem, t.i * 2 + m // 4 + 1)
                    i = T.matmul(pY[:, 0:D], h[:, m, :], w_sb[:, m, :], start=(m == 0), stop=(m == HK - 1))
                i.then_inc(out_sem, 1)

            def mix(st):
                a, t1, t2 = st, st.back(1), st.back(2)
                if a.real():
                    window(a, 0)
                if t2.real():
                    pe.wait_ge(s["x1"], t2.done())
                    wait(pe, s["T1c"], t2.done())
                    for k in range(DK):
                        i = T.transpose(pX[:, k * P:(k + 1) * P], x1[:, t2.par, k * P:(k + 1) * P], ident[:, :])
                    i.then_inc(s["T2"], 1)
                if a.real():
                    window(a, 1)
                if t2.real():
                    pe.wait_ge(s["T2c"], t2.done())
                    wait(pe, s["rel"], t2.back(1).done(2))
                    to_hidden(w1, x1t, s["W1"])
                if t1.real():
                    pe.wait_ge(s["att"], t1.done())
                    pe.wait_ge(s["atc"], t1.done(5))
                    wait(pe, s["T2c"], t1.back(1).done())
                    for k in range(4):
                        i = T.transpose(pX[:, k * P:(k + 1) * P], at_in[:, k, :], ident[:, :])
                    i.then_inc(s["T1"], 1)
                if a.real():
                    window(a, 2)
                    window(a, 3)
                if t1.real():
                    pe.wait_ge(s["T1c"], t1.done())
                    pe.wait_ge(s_xt[t1.par], (t1.half + 1) * 16)
                    for k in range(DK):
                        T.matmul(pN[:, 0:D], at_t[:, 2 + k, :], wo[:, k, :], start=(k == 0), stop=(k == DK - 1))
                    for k in range(DK):
                        T.matmul(pN[:, D:2 * D], at_t[:, k, :], wl[:, k, :], start=(k == 0), stop=False)
                    for k in range(DK):
                        i = T.matmul(pN[:, D:2 * D], xts[:, t1.par, k * P:(k + 1) * P], wrr[:, k, :], start=False,
                                     stop=(k == DK - 1))
                    i.then_inc(s["OG"], 1)
                if t2.real():
                    wait(pe, s["y1"], t2.back(1).done())
                    from_hidden(w2, ht, s["rel"], t2, s["W2"])
                if a.real():
                    for w in range(4, PPB):
                        window(a, w)
                    pe.wait_ge(s["Aev"], a.i * PPB + PPB)
                    wait(pe, s["aggr"], a.back(1).done())
                    for c in range(NT):
                        i = T.matmul(pG[:, :], adj[:, a.par, c, :], xn16[:, c, :], start=(c == 0), stop=(c == NT - 1))
                    i.then_inc(s["agg"], 1)
                    wait(pe, s["og"], a.back(1).done())
                    for c in range(NT):
                        T.matmul(pN[:, DK * CW:DK * CW + 1], adj[:, a.par, c, :], one16[:, :], start=(c == 0),
                                 stop=(c == NT - 1))
                    pe.wait_ge(s_q[a.par], (a.half + 1) * 16)
                    for k in range(DK):
                        i = T.matmul(pN[:, k * CW:(k + 1) * CW], qs[:, a.par, k * P:(k + 1) * P], kvm[:, k, :],
                                     start=True, stop=True)
                    i.then_inc(s["num"], 1)
            steps(pe, NT + 2, mix)
            pe.wait_ge(s["w"], NT)
            pe.wait_ge(s["T1c"], NT)
            pe.wait_ge(s["T2c"], NT)
            T.transpose(pX[0:NT, 0:P], wall[:, :], ident[:, :]).then_inc(s["wt"], 1)

            pe.wait_ge(s["og"], NT)
            for c in range(NT):
                r = min(P, N - c * P)
                pe.wait_ge(s["beats"], c + 1)
                for b in range(c, NT):
                    i = T.matmul(pN[:, b:b + 1], beats[0:r, c % 2, b * P:(b + 1) * P], one16[0:r, :],
                                 start=(c == 0 and b == 0), stop=(c == NT - 1))
                i.then_inc(s["ranked"], 1)
            pe.wait_ge(s["y1"], NT)
            for c in range(NT):
                r = min(P, N - c * P)
                pe.wait_ge(s["ohr"], c + 1)
                for b in range(2 * NS):
                    i = T.matmul(pY[:, 2 * b:2 * b + 2], oh_r[0:r, c % 2, b * P:(b + 1) * P], tok[0:r, c, :],
                                 start=(c == 0 and b == 0), stop=(c == NT - 1 and b == 2 * NS - 1))
                i.then_inc(s["picked"], 1)

            pe.wait_ge(s["wtc"], 1)
            pe.wait_ge(s["sidc"], 1)
            pe.wait_ge(s["Aev"], NT * PPB)
            pe.wait_ge(s["rel"], NT * 2)
            pe.wait_ge(s["aggr"], NT)

            def second_layer(q):
                for u in range(2):
                    wait(pe, s["yoc"], 2 * (q - 1) + u + 1)
                    for m in range(HK):
                        if u == 0 and m % 2 == 0:
                            pe.wait_ge(s["gel"], q * HK // 2 + m // 2 + 1)
                        i = T.matmul(pR[u][:, 0:D], gt[:, q % 2, m, u * P:(u + 1) * P], f2[:, m, :],
                                     start=(m == 0), stop=(m == HK - 1))
                    i.then_inc(s["F2"], 1)

            for q in range(NS):
                pe.wait_ge(s_gx[q], 32)
                wait(pe, s["T3c"], q)
                for k in range(DK):
                    for u in range(2):
                        i = T.transpose(pX[:, (k * 2 + u) * P:(k * 2 + u + 1) * P],
                                        gx2[:, 2 * q + u, k * P:(k + 1) * P], ident[:, :])
                i.then_inc(s["T3"], 1)
                if q:
                    second_layer(q - 1)
                pe.wait_ge(s["T3c"], q + 1)
                for m in range(HK):
                    if m % 2 == 0:
                        wait(pe, s["gel"], (q - 1) * HK // 2 + m // 2 + 1)
                    for k in range(DK):
                        i = T.matmul(pF[m // 2][:, m % 2 * 2 * P:(m % 2 + 1) * 2 * P], f1[:, k, m * P:(m + 1) * P],
                                     x2t[:, k, :], start=(k == 0), stop=(k == DK - 1))
                    if m % 2 == 1:
                        i.then_inc(s["F1"], 1)
            second_layer(NS - 1)


def kernel(**inputs):
    import numpy as np
    import concourse.bacc as bacc
    from concourse.bass_utils import run_bass_kernel_spmd

    a = {k: np.asarray(v) for k, v in inputs.items()}
    m = {k[7:]: v for k, v in a.items() if k.startswith("L0_mix_")}
    g = {k[7:]: v for k, v in a.items() if k.startswith("L0_gnn_")}
    f = {k[7:]: v for k, v in a.items() if k.startswith("L0_ffn_")}
    rows = [m["bk"], m["bv"], m["bo"], m["ln1_g"], m["ln1_b"], m["b2"], m["ln2_g"], m["ln2_b"], g["b_r"],
            f["wr"].reshape(-1), f["b2"], f["br"].reshape(-1)]
    cols = [m["bq"].reshape(-1, P).T, m["b1"].reshape(-1, P).T, f["b1"].reshape(-1, P).T]
    given = [
        ("x", a["x"]), ("src", a["src"]), ("dst", a["dst"]), ("w_l", g["W_l"].T), ("w_r", g["W_r"].T),
        ("w_q", m["Wq"]), ("w_k", m["Wk"]), ("w_v", m["Wv"]), ("w_o", m["Wo"]), ("w_1", m["W1"]), ("w_2", m["W2"]),
        ("f_1", f["w1"]), ("f_2", f["w2"]), ("rows", np.concatenate(rows)), ("cols", np.concatenate(cols, axis=1)),
    ]
    nc = bacc.Bacc("TRN2", target_bir_lowering=False, num_devices=1)
    arrays, args = {}, []
    for name, v in given:
        v = np.ascontiguousarray(v)
        arrays["in_" + name] = v
        args.append(nc.dram_tensor("in_" + name, v.shape, mybir.dt.from_np(v.dtype), kind="ExternalInput").ap())
    args.append(nc.dram_tensor("out_0", (N, D), mybir.dt.float32, kind="ExternalOutput").ap())
    args.append(nc.dram_tensor("xq_d", (NT, P, 2 * D), mybir.dt.float32, kind="Internal").ap())
    args.append(nc.dram_tensor("xg_d", (NT * P, 2 * D), mybir.dt.float16, kind="Internal").ap())
    args.append(nc.dram_tensor("w_d", (NT * P,), mybir.dt.float32, kind="Internal").ap())
    args.append(nc.dram_tensor("xb_d", (NT * P, 2 * D), mybir.dt.float32, kind="Internal").ap())
    gps_layer(nc, *args)
    r = run_bass_kernel_spmd(nc, [arrays], core_ids=[0])
    return r.results[0]["out_0"]
```

```python
import concourse.bass as bass
from concourse import mybir
from contextlib import ExitStack

P = 128
N = 2500
D = 256
DK = D // P
H = 1024
HK = H // P
HEADS = 8
DH = D // HEADS
HPC = P // DH
E = 80000
NT = -(-N // P)
LAST = N - (NT - 1) * P
ET = E // P
W = 4
WPB = P // W
NW = NT * WPB
WG = 5
GW = NW // WG
TPW = 2
RUN = TPW * P
ER = 64
KEYS = W * NT
WPU = 4
UPB = WPB // WPU
TPU = WPU * TPW
TPH = TPU // 2
OH = 4
EP = 125
EK = E // ER // EP
EPS = 1e-5
LO = 2.0 ** 11
KEEP = int(0.5 * N) - 1
NS = -(-KEEP // (2 * P))
ET1 = 16
EN = ET1 * P
BY_ACT = 13
ROWS = ["bk", "bv", "bo", "g1", "c1", "b2", "g2", "c2", "bg", "wr", "fb2"]
CW = P + HPC


class Tile:

    def __init__(self, n, j=None):
        self.n, self.j, self.par = n, j, n % 2
        self.i = n if j is None else j * 2 + n
        self.half = n // 2 if j is None else j + n // 2

    def back(self, k):
        return Tile(self.n - k, self.j)

    def real(self):
        return self.j is not None or 0 <= self.n < NT

    def done(self, per=1):
        if self.j is None:
            return per * max(0, min(self.n + 1, NT))
        return self.i * per + per


def steps(eng, total, body):
    for n in range(5):
        body(Tile(n))
    with eng.Fori(0, 7) as j:
        body(Tile(5, j))
        body(Tile(6, j))
    for n in range(19, total):
        body(Tile(n))


def wait(eng, sem, value):
    if not isinstance(value, int) or value > 0:
        eng.wait_ge(sem, value)


def wait_apart(eng, sem, value, met):
    if not isinstance(value, int):
        value = eng.snap(eng.to_reg(value))
    eng.wait_ge(*met)
    eng.wait_ge(sem, value)


class Chain:

    def __init__(self, eng, sem, per, tile=0):
        self.eng, self.sem, self.per, self.base, self.n = eng, sem, per, tile * per, 0

    def __call__(self, ins, met=None):
        self.n += 1
        assert self.n <= self.per
        ins.then_inc(self.sem, 1)
        if met:
            wait_apart(self.eng, self.sem, self.base + self.n, met)
        else:
            self.eng.wait_ge(self.sem, self.base + self.n)


def gps_layer(nc, x, src, dst, w_l, w_r, w_q, w_k, w_v, w_o, w_1, w_2, f_1, f_2, rows, cols, out,
              xq_d, xg_d, w_d, xb_d):
    f32, f16, i32, fr = mybir.dt.float32, mybir.dt.float16, mybir.dt.int32, mybir.dt.float32r
    ALU, ACT = mybir.AluOpType, mybir.ActivationFunctionType
    V, G, A, T = nc.vector, nc.gpsimd, nc.scalar, nc.tensor
    NR = len(ROWS)
    ctx = ExitStack()
    with ctx:
        def sb(name, shape, dt=f32):
            return ctx.enter_context(nc.sbuf_tensor(name, shape, dt))

        def over(held, at, shape, dt=f32):
            size, n = {f32: 4, i32: 4, f16: 2}[dt], 1
            for k in shape[1:]:
                n *= k
            end = at + -(-n * size // 4)
            v = held[0:shape[0], at:end].bitcast(dt)[:, 0:n] if dt != f32 else held[0:shape[0], at:end]
            if len(shape) == 3:
                v = v.rearrange("p (a b) -> p a b", a=shape[1])
            if len(shape) == 4:
                v = v.rearrange("p (a b c) -> p a b c", a=shape[1], b=shape[2])
            return v, end

        def sem(name):
            return ctx.enter_context(nc.semaphore(name))

        xn_m = sb("xn", [P, NT * D])
        xn = xn_m[:, :].rearrange("p (c f) -> p c f", c=NT)
        xn16 = sb("xn16", [P, NT, 2 * D], f16)
        acc_m = sb("acc", [P, NT * D])
        acc = acc_m[:, :].rearrange("p (c f) -> p c f", c=NT)
        dacc = sb("dacc", [P, NT])
        e_m = sb("e", [P, (DK + 2 * HK) * 2 * P])
        wo = sb("wo", [P, DK, D])
        wl = sb("wl", [P, DK, D])
        wrr = sb("wrr", [P, DK, D])
        w1 = sb("w1", [P, DK, H])
        w2_hi = sb("w2_hi", [P, HK, D], fr)
        w2_lo = sb("w2_lo", [P, HK, D], fr)
        ht_hi = sb("ht_hi", [P, HK, P], fr)
        ht_lo = sb("ht_lo", [P, HK, P], fr)
        rowt = sb("rowt", [P, NR * D + 1])
        colt = sb("colt", [P, DK + 2 * HK])
        ident = sb("ident", [P, P])
        same_head = sb("same_head", [P, P])
        head_of = sb("head_of", [P, HPC])
        later = sb("later", [P, P])
        iota = sb("iota", [P, P, TPH], f16)
        one16 = sb("one16", [P, 1], f16)
        ones = sb("ones", [P, P])
        scale_lo = sb("scale_lo", [P, 1])
        minus_half = sb("minus_half", [P, NT])
        win0 = sb("win0", [EP, NW], f16)
        key0 = sb("key0", [GW, WG])
        row = {n: rowt[:, i * D:(i + 1) * D] for i, n in enumerate(ROWS)}
        br = rowt[:, NR * D:NR * D + 1]
        bq, b1c, fb1c = colt[:, 0:DK], colt[:, DK:DK + HK], colt[:, DK + HK:DK + 2 * HK]

        adj_m = sb("adj", [P, NT * P])
        adj = adj_m[:, :].bitcast(f16).rearrange("p (u c d) -> p u c d", u=2, c=NT)
        dlast, at = over(adj_m, 0, [EP, EK, ER], i32)
        e_d, at = over(adj_m, at, [GW, WG, RUN], i32)
        passed, at = over(e_m, 0, [EP, EK, NW], f16)
        e_a, at = over(e_m, 0, [GW, WG, RUN], i32)
        e_b, at = over(e_m, at, [GW, WG, RUN], i32)
        e_c, at = over(e_m, at, [GW, WG, RUN], i32)
        dlastf = sb("dlastf", [EP, EK])
        gidx = sb("gidx", [GW, WG], i32)
        cov = sb("cov", [GW, 1])
        covered = sb("covered", [P, 1])
        covered_m1 = sb("covered_m1", [P, 1])
        flag = sb("flag", [P, 1], i32)
        scol = sb("scol", [P, NW * TPW], f16)
        kcol = sb("kcol", [P, NW * TPW], f16)
        blk = sb("blk", [P, 2, 2, WPB * TPW], f16)
        oh_m = sb("oh", [P, OH * (P + KEYS) * TPU // 2])
        oh_s, at = over(oh_m, 0, [P, OH, 2, P * TPH], f16)
        oh_k, at = over(oh_m, at, [P, OH, 2, KEYS * TPH], f16)
        oh_s, oh_k = (oh.rearrange("p u h (n j) -> p u h n j", j=TPH) for oh in (oh_s, oh_k))
        oh_e, _ = over(oh_m, 0, [P, P], f16)

        sidx = sb("sidx", [P, 1], i32)
        didx = sb("didx", [P, 1], i32)
        dcol = sb("dcol", [P, 1])
        msg = sb("msg", [P, 2 * D], f16)

        stats = sb("stats", [P, NT, 6])
        mv = sb("mv", [P, NT, 2])
        ve = sb("ve", [P, NT])
        rstd = sb("rstd", [P, NT])
        hid_m = sb("hid", [P, 2 * H])
        xs, at = over(hid_m, 0, [P, 2, D])
        lo32, at = over(hid_m, at, [P, D])
        xt_s, at = over(hid_m, at, [P, 2, D])
        qp_s, at = over(hid_m, at, [P, 2, D])
        kb, at = over(oh_m, 0, [P, D])
        kmin, at = over(oh_m, at, [P, D])
        kexp, at = over(oh_m, at, [P, D])
        qb, at = over(oh_m, at, [P, D])
        qmin, at = over(oh_m, at, [P, D])
        qexp, at = over(oh_m, at, [P, D])
        kphi, at = over(oh_m, at, [P, 2, D])
        vv, at = over(oh_m, at, [P, 2, DK, P + 1])
        io_m = sb("io", [P, 6 * D])
        wkv, at = over(io_m, 0, [P, DK, 2 * D])
        wq, at = over(io_m, at, [P, DK, D])
        ksum = sb("ksum", [P, DK])
        kvm = sb("kvm", [P, DK, CW])

        qs, at = over(io_m, 0, [P, 2, D])
        xts, at = over(io_m, at, [P, 2, D])
        xin, at = over(io_m, at, [P, 2, D])
        deg = sb("deg", [P, 3])
        den = sb("den", [P, 2, HEADS])
        at_in = sb("at_in", [P, 4, P])
        at_t = sb("at_t", [P, 4, P])
        agg1 = sb("agg1", [P, D])
        r1 = sb("r1", [P, D])
        gx = sb("gx", [P, D])
        gxb = sb("gxb", [P, 2, D])
        x1 = sb("x1", [P, 2, D])
        x1a = sb("x1a", [P, D])
        x1b = sb("x1b", [P, D])
        x1t = sb("x1t", [P, DK, P])
        ht, at = over(hid_m, 0, [P, HK, P])
        w2, _ = over(e_m, 0, [P, HK, D])
        r2 = sb("r2", [P, D])
        z1 = sb("z1", [P, D])
        x2 = sb("x2", [P, D])
        xb = sb("xb", [P, 2, 2 * D])
        yb = sb("yb", [P, D])
        bn = sb("bn", [P, 3, 6])
        mvs = sb("mvs", [P, 3, 2])
        ves = sb("ves", [P, 3])
        rs = sb("rs", [P, 3])
        cgb = sb("cgb", [P, D])
        wraw = sb("wraw", [P, 1])
        wall = sb("wall", [P, NT])

        xn16_m = xn16[:, :, :].rearrange("p c f -> p (c f)").bitcast(f32)
        wrow, at = over(e_m, 0, [P, N])
        beats1, at = over(e_m, at, [P, 2, EN], f16)
        beats2, at = over(xn16_m, 0, [P, 4, NT * P - EN], f16)
        scrap, _ = over(oh_m, 0, [P, 2, EN], f16)
        tok = sb("tok", [P, NT, 2], f16)
        oh_r, at = over(adj_m, 0, [P, NT // TPH, P * TPH], f16)
        oh_r = oh_r.rearrange("p g (n j) -> p g n j", j=TPH)
        oh_b, at = over(adj_m, at, [P, NT, 2 * NS], f16)
        tok_b, at = over(adj_m, at, [P, NT, 2 * 2 * NS], f16)
        tok_b = tok_b.rearrange("p c (a b) -> p c a b", a=2)
        ranki = sb("ranki", [P, 3, NT], i32)
        rankh, at = over(adj_m, at, [P, 2, NT], f16)
        ahead = sb("ahead", [P, 4, NT])
        n_later = sb("n_later", [P, NT])
        rank = sb("rank", [P, NT])
        iota_b = sb("iota_b", [P, 2 * NS], f16)
        stok = sb("stok", [P, 2, 2 * NS])
        sidf = sb("sidf", [P, 2 * NS])
        sid = sb("sid", [P, 2 * NS], i32)
        gx2, _ = over(acc_m, 0, [P, 2 * NS, 2 * D])
        x2t, at = over(e_m, 0, [P, DK, 2 * P])
        gt, at = over(e_m, at, [P, 2, HK * 2 * P])
        gt = gt.rearrange("p u (m t) -> p u m t", m=HK)
        DUOS = HK // 2

        def duo(g):
            q, d = g // DUOS, g % DUOS
            return gt[:, q % 2, 2 * d:2 * d + 2, :].rearrange("p m t -> p (m t)")

        def part_of(g, j, u):
            return g % 2 * 4 + 2 * j + u

        yo, at = over(hid_m, 0, [P, 2, D])
        f1, at = over(xn_m, 0, [P, DK, H])
        f2, at = over(xn_m, at, [P, HK, D])
        ws = sb("ws", [P, 2, 2])
        wt1 = sb("wt1", [ET1, P])
        wt2 = sb("wt2", [NT - ET1, P])

        bank = [ctx.enter_context(nc.psum_tensor(f"bank{i}", [P, 512], f32)) for i in range(8)]
        pT, pKV, pQ, pAcc = bank[0:2], bank[2:4], bank[4:6], bank[6:8]
        pW, pG, pX, pN, pH, pY = bank[0:2], bank[2], bank[3], bank[4], bank[5:7], bank[7]
        pS, pK = (bank[0], bank[1], bank[4]), (bank[2], bank[3], bank[5])
        pF, pR = bank[0:2] + bank[5:7], (bank[7], bank[2])

        names = """const rows_in cols_in wkv_in wq_in w_in dst_in pad vset eset epass cnt idx gat
            var rstd xs_ready xn_ready x16 x16c xT xTc KV kvb kc kmin kexp kphi Q qb qmin qexp
            qphi acc kvm cov flag etr tot blkc oh win Aev agg num att atc aggr T1 T1c OG
            og ogc ve1 r1 x1c x1p x1 gxb T2 T2c W1 rel W2 y1 ln2c ve2 r2 z1 x2c x2 ve3 r3 ln3c
            xn2 wsum w base wt wtc wd wrow beats beaten rank sids sidc wsc ybj ranked picked T3 T3c F1 gel yoc yo f_in rint ohb scop rows2_in hhi hlo w2s w2c w2_in xnb x1b atm f2c f2s ghi glo F2c
            sx ssrc sdst sg soh smm sc sacc""".split()
        s = {n: sem("s_" + n) for n in names}
        s_x = [sem(f"s_xload{i}") for i in range(4)]
        s_st = [sem(f"s_xtstore{i}") for i in range(2)]
        s_sq = [sem(f"s_qstore{i}") for i in range(2)]
        s_q = [sem(f"s_qload{i}") for i in range(2)]
        s_xt = [sem(f"s_xtload{i}") for i in range(2)]
        s_xi = [sem(f"s_xiload{i}") for i in range(2)]
        s_bs = [sem(f"s_xbstore{i}") for i in range(2)]
        s_os = [sem(f"s_outstore{i}") for i in range(2)]
        s_gx = [sem(f"s_gather{i}") for i in range(NS)]
        s_sc = [sem(f"s_scatter{i}") for i in range(2)]
        CH = NT // 4

        x_t = x[0:(NT - 1) * P, :].rearrange("(c p) f -> p c f", p=P)
        dst_r = dst.rearrange("(t e) -> t e", e=ER)
        src_r = src.rearrange("(t e) -> t e", e=ER)
        src_c = src.rearrange("(n a) -> n a", a=1)
        dst_c = dst.rearrange("(n a) -> n a", a=1)
        NCONST = 28
        VSET = 15

        def edge_columns(cols_, banks, b):
            n = min(2, WG - 2 * b)
            part = cols_[:, b * 2 * GW * TPW:(b * 2 + n) * GW * TPW]
            return (part.rearrange("p (g w j) -> p g j w", g=n, j=TPW),
                    banks[b][:, 0:n * GW * TPW].rearrange("p (g j w) -> p g j w", g=n, j=TPW))

        block = ctx.enter_context(nc.Block())

        @block.sync
        def _(sp):
            sp.dma_start(dlast[:, :, :], dst.rearrange("(p k e) -> p k e", p=EP, e=ER)).then_inc(s["dst_in"], 16)
            for i in range(4):
                n = min(CH * (i + 1), NT - 1)
                sp.dma_start(xn[:, CH * i:n, :], x_t[:, CH * i:n, :]).then_inc(s_x[i], 16)
            sp.wait_ge(s["pad"], 1)
            sp.dma_start(xn[0:LAST, NT - 1, :], x[N - LAST:N, :]).then_inc(s_x[3], 16)

            weights = {2: (wo, w_o), 3: (wl, w_l), 4: (wrr, w_r), NT - 1: (w1, w_1)}

            def store(st):
                t = st.back(1)
                if t.real():
                    sp.wait_ge(s["xTc"], t.done())
                    sp.dma_start(xq_d[t.i, :, 0:D], xt_s[:, t.par, :]).then_inc(s_st[t.par], 16)
                t = st.back(3)
                if t.real():
                    sp.wait_ge(s["qphi"], t.done())
                    sp.dma_start(xq_d[t.i, :, D:2 * D], qp_s[:, t.par, :]).then_inc(s_sq[t.par], 16)
                if st.j is None and st.n == 1:
                    sp.dma_start(rowt[:, 2 * D:], rows[2 * D:NR * D + 1].partition_broadcast(P)).then_inc(s["rows2_in"], 16)
                if st.j is None and st.n in weights:
                    w_sb, w_in = weights[st.n]
                    sp.dma_start(w_sb[:, :, :], w_in.rearrange("(k p) n -> p k n", p=P)).then_inc(s["w_in"], 16)
            steps(sp, NT + 3, store)
            for u in range(2):
                sp.wait_ge(s_st[u], 16 * NT // 2)
                sp.wait_ge(s_sq[u], 16 * NT // 2)

            sp.wait_ge(s["etr"], 3)
            sp.dma_start(w2, w_2.rearrange("(k p) n -> p k n", p=P)).then_inc(s["w2_in"], 16)

            sp.wait_ge(s["flag"], 1)
            fast = sp.value_load(flag[0:1, 0:1], min_val=0, max_val=1)
            with sp.If(fast == 0):
                sp.wait_ge(s["x16"], NT)
                sp.dma_start(xg_d.rearrange("(c p) f -> p c f", p=P), xn16[:, :, :]).then_inc(s["sx"], 16)
                with sp.Fori(0, ET) as e:
                    wait_apart(sp, s["sacc"], e + 1, (s["flag"], 1))
                    sp.dma_start(sidx[:, :], src_c[bass.ds(e * P, P), :]).then_inc(s["ssrc"], 16)
                    sp.dma_start(didx[:, :], dst_c[bass.ds(e * P, P), :]).then_inc(s["sdst"], 16)

            def weights_row(lot):
                lo, hi, w_t = ((0, EN, wt1), (EN, NT * P, wt2))[lot]
                sp.wait_ge(s["wtc"], lot + 1)
                sp.dma_start(w_d[lo:hi].rearrange("(c p) -> c p", p=P), w_t[:, :]).then_inc(s["wd"], 16)
                sp.wait_ge(s["wd"], 16 * (lot + 1))
                hi = min(hi, N)
                sp.dma_start(wrow[:, lo:hi], w_d[lo:hi].partition_broadcast(P)).then_inc(s["wrow"], 16)

            def load_store(st):
                if st.j is None and st.n == NT:
                    weights_row(0)
                if st.j is None and st.n == NT + 1:
                    sp.wait_ge(s["ve1"], NT)
                    sp.dma_start(f1, f_1.rearrange("(k p) n -> p k n", p=P)).then_inc(s["f_in"], 16)
                    sp.dma_start(f2, f_2.rearrange("(k p) n -> p k n", p=P)).then_inc(s["f_in"], 16)
                t = st.back(-1)

                def q_of(t):
                    if t.real():
                        wait(sp, s["num"], t.back(2).done())
                        sp.dma_start(qs[:, t.par, :], xq_d[t.i, :, D:2 * D]).then_inc(s_q[t.par], 16)
                if st.j is None and st.n == 0:
                    q_of(st)
                q_of(t)
                if st.real():
                    if st.back(2).real():
                        wait_apart(sp, s["OG"], st.back(2).done(), (s["flag"], 1))
                        wait_apart(sp, s["og"], st.back(2).done(), (s["flag"], 1))
                    sp.dma_start(xts[:, st.par, :], xq_d[st.i, :, 0:D]).then_inc(s_xt[st.par], 16)
                    if st.j is None and st.n == NT - 1:
                        sp.dma_start(xin[0:LAST, st.par, :], x[N - LAST:N, :]).then_inc(s_xi[st.par], 16)
                    else:
                        sp.dma_start(xin[:, st.par, :], x[bass.ds(st.i * P, P), :]).then_inc(s_xi[st.par], 16)
                t3 = st.back(3)
                if t3.real():
                    pair = (xb[:, t3.par, :], xb[:, t3.par, D:2 * D])
                    wait_apart(sp, s["base"], t3.done(), (s["flag"], 1))
                    sp.dma_start(xb_d[bass.ds(t3.i * P, P), :], pair[0]).then_inc(s_bs[t3.par], 16)
                    if t3.j is None and t3.n == NT - 1:
                        sp.dma_start(out[N - LAST:N, :], pair[1][0:LAST, :]).then_inc(s_os[t3.par], 16)
                    else:
                        sp.dma_start(out[bass.ds(t3.i * P, P), :], pair[1]).then_inc(s_os[t3.par], 16)
            steps(sp, NT + 3, load_store)

            weights_row(1)
            for u in range(2):
                sp.wait_ge(s_bs[u], 16 * NT // 2)
                sp.wait_ge(s_os[u], 16 * NT // 2)
                sp.wait_ge(s_sc[u], 16 * NS)

        @block.gpsimd
        def _(pool):
            link = Chain(pool, s["const"], NCONST)
            G.iota(win0[:, :], pattern=[[W, NW]], base=0, channel_multiplier=0,
                   allow_small_or_imprecise_dtypes=True).then_inc(s["eset"], 1)
            G.iota(key0[:, :], pattern=[[-KEYS * GW, WG]], base=0, channel_multiplier=-KEYS,
                   allow_small_or_imprecise_dtypes=True).then_inc(s["eset"], 1)
            G.memset(one16[:, :], 1.0).then_inc(s["eset"], 1)
            link(G.memset(minus_half[:, :], -0.5))
            link(G.memset(ident[:, :], 0.0))
            link(G.affine_select(out=ident[:, :], in_=ident[:, :], compare_op=ALU.not_equal, fill=1.0, base=0,
                                 pattern=[[-1, P]], channel_multiplier=1))
            for u in range(2):
                link(G.memset(vv[:, u, :, P:P + 1], 1.0))
            pool.wait_ge(s["var"], 1)
            G.tensor_tensor(rstd[:, 0:CH], ve[:, 0:CH], minus_half[:, 0:CH], ALU.pow).then_inc(s["rstd"], 1)
            pool.wait_ge(s["idx"], 1)
            for g in range(WG):
                for buf, tab in ((e_a, src_r), (e_b, dst_r)):
                    G.indirect_dma_start(buf[:, g, :], None, tab[:, :],
                                         bass.IndirectOffsetOnAxis(ap=gidx[:, g:g + 1], axis=0)).then_inc(s["gat"], 16)
            pool.wait_ge(s["var"], 2)
            G.tensor_tensor(rstd[:, CH:NT], ve[:, CH:NT], minus_half[:, CH:NT], ALU.pow).then_inc(s["rstd"], 1)
            link(G.memset(ones[:, :], 1.0))
            link(G.memset(scale_lo[:, :], LO))
            link(G.iota(iota[:, :, :], pattern=[[1, P], [0, TPH]], base=0, channel_multiplier=0,
                        allow_small_or_imprecise_dtypes=True))
            link(G.memset(same_head[:, :], 0.0))
            link(G.memset(head_of[:, :], 0.0))
            link(G.memset(later[:, :], 1.0))
            link(G.affine_select(out=later[:, :], in_=later[:, :], compare_op=ALU.is_gt, fill=0.0, base=0,
                                 pattern=[[1, P]], channel_multiplier=-1))
            link(G.iota(tok[:, :, 0], pattern=[[0, NT]], base=0, channel_multiplier=1,
                        allow_small_or_imprecise_dtypes=True))
            link(G.iota(tok[:, :, 1], pattern=[[1, NT]], base=0, channel_multiplier=0,
                        allow_small_or_imprecise_dtypes=True))
            link(G.iota(n_later[:, :], pattern=[[-P, NT]], base=N - 1, channel_multiplier=-1,
                        allow_small_or_imprecise_dtypes=True))
            link(G.memset(ahead[:, :, :], 0.0))
            link(G.iota(iota_b[:, :], pattern=[[1, 2 * NS]], base=0, channel_multiplier=0,
                        allow_small_or_imprecise_dtypes=True))
            for h in range(HPC):
                r = slice(h * DH, (h + 1) * DH)
                link(G.memset(same_head[r, r], 1.0))
                link(G.memset(head_of[r, h:h + 1], 1.0))
            link(G.memset(acc[:, :, :], 0.0))
            link(G.memset(dacc[:, :], 0.0))
            pool.wait_ge(s["rows2_in"], 16)
            link(G.tensor_tensor(cgb[:, :], row["bg"], row["c2"], ALU.add))
            assert link.n == link.per

            with pool.Fori(0, NT) as t:
                c16 = Chain(pool, s["x16c"], 2, t)
                wait_apart(pool, s["xn_ready"], t + 1, (s["var"], 1))
                xt = xn[:, bass.ds(t, 1), :].rearrange("p a f -> p (a f)")
                hi = xn16[:, bass.ds(t, 1), 0:D].rearrange("p a f -> p (a f)")
                lo = xn16[:, bass.ds(t, 1), D:2 * D].rearrange("p a f -> p (a f)")
                c16(G.tensor_copy(hi, xt), met=(s["var"], 1))
                c16(G.tensor_tensor(lo32[:, :], xt, hi, ALU.subtract), met=(s["var"], 1))
                G.tensor_tensor(lo, lo32[:, :], scale_lo[:, :].broadcast_to([P, D]), ALU.mult).then_inc(s["x16"], 1)

            pool.wait_ge(s["flag"], 1)
            fast = pool.value_load(flag[0:1, 0:1], min_val=0, max_val=1)
            with pool.If(fast == 0):
                pool.wait_ge(s["sx"], 16)
                with pool.Fori(0, ET) as e:
                    wait_apart(pool, s["ssrc"], (e + 1) * 16, (s["flag"], 1))
                    G.indirect_dma_start(msg[:, :], None, xg_d[:, :],
                                         bass.IndirectOffsetOnAxis(ap=sidx[:, 0:1], axis=0)).then_inc(s["sg"], 16)

            pool.wait_ge(s["w2_in"], 16)
            G.tensor_copy(w2_hi[:, :, :], w2).then_inc(s["w2c"], 1)
            pool.wait_ge(s["w2c"], 1)
            G.tensor_tensor(w2_lo[:, :, :], w2, w2_hi[:, :, :].bitcast(f32), ALU.subtract).then_inc(s["w2s"], 1)

            def norm_tail(st):
                t1, t2, t3 = st.back(1), st.back(2), st.back(3)
                if t3.real():
                    pool.wait_ge(s["ve3"], t3.done())
                    G.tensor_tensor(rs[:, 2:3], ves[:, 2:3], minus_half[:, 0:1], ALU.pow).then_inc(s["r3"], 1)
                    wait_apart(pool, s["xn2"], t3.done(), (s["flag"], 1))
                    G.tensor_tensor(xb[:, t3.par, D:2 * D], x2[:, :], xb[:, t3.par, 0:D], ALU.add).then_inc(s["base"], 1)
                if t2.real():
                    pool.wait_ge(s["hhi"], t2.done())
                    wait(pool, s["W2"], t2.back(1).done())
                    G.tensor_tensor(ht_lo[:, :, :], ht, ht_hi[:, :, :].bitcast(f32), ALU.subtract).then_inc(s["hlo"], 1)
                if st.real():
                    pool.wait_ge(s["x16"], NT)
                    pool.wait_ge(s["xs_ready"], NT)
                    pool.wait_ge(s["kvm"], 1)
                    xt = xn[:, bass.ds(st.i, 1), :].rearrange("p a f -> p (a f)")
                    G.tensor_tensor(xt, xt, row["bo"], ALU.add).then_inc(s["xnb"], 1)
                if t1.real():
                    pool.wait_ge(s["ve1"], t1.done())
                    G.tensor_tensor(rs[:, 0:1], ves[:, 0:1], minus_half[:, 0:1], ALU.pow).then_inc(s["r1"], 1)
                    pool.wait_ge(s["og"], t1.done())
                    wait(pool, s["x2"], t1.back(2).done())
                    G.tensor_tensor(gxb[:, t1.par, :], gx[:, :], cgb[:, :], ALU.add).then_inc(s["gxb"], 1)
                    pool.wait_ge(s["x1c"], t1.done())
                    G.tensor_tensor(x1a[:, :], x1a[:, :], row["g1"], ALU.mult).then_inc(s["x1p"], 1)
                    pool.wait_ge(s["x1p"], t1.done())
                    wait(pool, s["T2"], t1.back(2).done())
                    wait(pool, s["ve2"], t1.back(2).done())
                    G.tensor_tensor(x1[:, t1.par, :], x1a[:, :], row["c1"], ALU.add).then_inc(s["x1"], 1)
                if t2.real():
                    pool.wait_ge(s["ve2"], t2.done())
                    G.tensor_tensor(rs[:, 1:2], ves[:, 1:2], minus_half[:, 0:1], ALU.pow).then_inc(s["r2"], 1)
                if t1.real():
                    pool.wait_ge(s["x1"], t1.done())
                    wait(pool, s["y1"], t1.back(1).done())
                    G.tensor_tensor(x1b[:, :], x1[:, t1.par, :], row["b2"], ALU.add).then_inc(s["x1b"], 1)
                if t2.real():
                    pool.wait_ge(s["z1"], t2.done())
                    G.tensor_tensor(z1[:, :], z1[:, :], row["g2"], ALU.mult).then_inc(s["x2c"], 1)
                    pool.wait_ge(s["x2c"], t2.done())
                    wait(pool, s["w"], t2.back(1).done())
                    wait(pool, s["base"], t2.back(1).done())
                    G.tensor_tensor(x2[:, :], z1[:, :], gxb[:, t2.par, :], ALU.add).then_inc(s["x2"], 1)
            pool.wait_ge(s["const"], NCONST)
            steps(pool, NT + 3, norm_tail)

            pool.wait_ge(s["f_in"], 16 * 2)
            pool.wait_ge(s["W2"], NT)
            G.tensor_copy(w2_hi[:, :, :], f2).then_inc(s["f2c"], 1)
            pool.wait_ge(s["f2c"], 1)
            G.tensor_tensor(w2_lo[:, :, :], f2, w2_hi[:, :, :].bitcast(f32), ALU.subtract).then_inc(s["f2s"], 1)

            pool.wait_ge(s["sids"], 1)
            pool.wait_ge(s["aggr"], NT)
            for u in range(2):
                pool.wait_ge(s_bs[u], 16 * NT // 2)
            for c in range(2 * NS):
                G.indirect_dma_start(gx2[:, c, :], None, xb_d[:, :],
                                     bass.IndirectOffsetOnAxis(ap=sid[:, c:c + 1], axis=0)).then_inc(s_gx[c // 2], 16)
            for u in range(2):
                pool.wait_ge(s_os[u], 16 * NT // 2)
            for c in range(2 * NS):
                r = min(P, KEEP - c * P)
                pool.wait_ge(s["yo"], c + 1)
                G.indirect_dma_start(out[:, :], bass.IndirectOffsetOnAxis(ap=sid[0:r, c:c + 1], axis=0),
                                     yo[0:r, c % 2, :], None).then_inc(s_sc[c % 2], 16)

        @block.scalar
        def _(act):
            act.dma_start(wkv[:, :, 0:D], w_k.rearrange("(k p) n -> p k n", p=P)).then_inc(s["wkv_in"], 16)
            act.dma_start(wkv[:, :, D:2 * D], w_v.rearrange("(k p) n -> p k n", p=P)).then_inc(s["wkv_in"], 16)
            act.dma_start(wq[:, :, :], w_q.rearrange("(k p) n -> p k n", p=P)).then_inc(s["wq_in"], 16)
            act.dma_start(colt[:, :], cols).then_inc(s["cols_in"], 16)
            act.dma_start(rowt[:, 0:2 * D], rows[0:2 * D].partition_broadcast(P)).then_inc(s["rows_in"], 16)
            act.wait_ge(s["cols_in"], 16)

            def qkv(st):
                t = st.back(1)
                if t.real():
                    act.wait_ge(s["xT"], t.done())
                    wait(act, s["Q"], t.back(2).done())
                    if t.j is not None or t.n >= 2:
                        act.wait_ge(s_st[t.par], t.half * 16)
                    A.activation(xt_s[:, t.par, :], pT[t.par][:, 0:D], ACT.Copy).then_inc(s["xTc"], 1)
                t = st.back(2)
                if t.real():
                    act.wait_ge(s["Q"], t.done())
                    wait(act, s["qphi"], t.back(1).done())
                    for m in range(DK):
                        i = A.activation(qb[:, m * P:(m + 1) * P], pQ[t.par][:, m * P:(m + 1) * P], ACT.Identity,
                                         bias=bq[:, m:m + 1])
                    i.then_inc(s["qb"], 1)
                    act.wait_ge(s["kmin"], t.done())
                    wait(act, s["kphi"], t.back(1).done())
                    A.activation(kexp[:, :], kmin[:, :], ACT.Exp).then_inc(s["kexp"], 1)
                    act.wait_ge(s["qmin"], t.done())
                    A.activation(qexp[:, :], qmin[:, :], ACT.Exp).then_inc(s["qexp"], 1)
            steps(act, NT + 2, qkv)

            for b in range(3):
                act.wait_ge(s["etr"], b + 1)
                out_, in_ = edge_columns(scol, pS, b)
                A.activation(out_, in_, ACT.Copy).then_inc(s["scop"], 1)

            def sum_beats(lot, c):
                n = lot * ET1 + c
                act.wait_ge(s["beats"], n + 1)
                wait(act, s["beaten"], n - 1)
                held = beats1[:, c % 2, c * P:EN] if lot == 0 else beats2[:, c % 4, 0:N - EN]
                width = EN - c * P if lot == 0 else N - EN
                A.activation(scrap[:, n % 2, 0:width], held, ACT.Copy, accum_out=ahead[:, lot, c:c + 1]).then_inc(s["beaten"], 1)

            def adj_out(a, w):
                act.wait_ge(s["win"], a.i * UPB + w + 1)
                if w == 0:
                    wait(act, s["num"], a.back(2).done())
                A.activation(adj[:, a.par, :, w * WPU * W:(w + 1) * WPU * W],
                             pW[w % 2][:, 0:WPU * KEYS].rearrange("p (d c) -> p c d", c=NT), ACT.Copy).then_inc(s["Aev"], 1)

            def mix(st):
                a, t1, t2 = st, st.back(1), st.back(2)
                if t2.real():
                    act.wait_ge(s["T2"], t2.done())
                    wait(act, s["W1"], t2.back(1).done(2))
                    A.activation(x1t[:, :, :].rearrange("p k q -> p (k q)"), pX[:, 0:D], ACT.Copy).then_inc(s["T2c"], 1)
                if st.j is None and st.n == NT + 1:
                    sum_beats(0, 0)
                if a.real():
                    adj_out(a, 0)
                    adj_out(a, 1)
                def relu(half):
                    act.wait_ge(s["W1"], t2.i * 2 + half + 1)
                    for m in range(half * HK // 2, (half + 1) * HK // 2):
                        i = A.activation(ht[:, m, :], pH[half][:, (m % 4) * P:(m % 4 + 1) * P], ACT.Relu,
                                         bias=b1c[:, m:m + 1])
                    i.then_inc(s["rel"], 1)
                if t1.real():
                    act.wait_ge(s["aggr"], t1.done())
                    A.activation(at_in[:, 0:2, :].rearrange("p k f -> p (k f)"), agg1[:, :], ACT.Copy,
                                 scale=deg[:, 2:3]).then_inc(s["atm"], 1)
                if t2.real():
                    wait(act, s["hlo"], t2.back(1).done())
                    wait(act, s["W2"], t2.back(1).done())
                    relu(0)
                if t1.real():
                    act.wait_ge(s["T1"], t1.done())
                    wait(act, s["OG"], t1.back(1).done())
                    A.activation(at_t[:, :, :].rearrange("p k q -> p (k q)"), pX[:, :], ACT.Copy).then_inc(s["T1c"], 1)
                if t2.real():
                    relu(1)
                    act.wait_ge(s["rel"], t2.done(2))
                    A.activation(ht_hi[:, :, :], ht, ACT.Copy).then_inc(s["hhi"], 1)
                if a.real():
                    adj_out(a, 2)
                if a.real():
                    for w in range(3, UPB):
                        adj_out(a, w)
            steps(act, NT + 2, mix)

            for c in range(1, ET1):
                sum_beats(0, c)
            for c in range(BY_ACT):
                sum_beats(1, c)

            def gathered(q):
                act.wait_ge(s["T3"], q + 1)
                A.activation(x2t[:, :, :].rearrange("p k q -> p (k q)"), pX[:, :], ACT.Copy).then_inc(s["T3c"], 1)

            def gelu(q, d):
                act.wait_ge(s["F1"], q * DUOS + d + 1)
                if d == 0:
                    wait(act, s["glo"], (q - 1) * DUOS)
                for m in range(2 * d, 2 * d + 2):
                    i = A.activation(gt[:, q % 2, m, :], pF[d][:, m % 2 * 2 * P:(m % 2 + 1) * 2 * P],
                                     ACT.Gelu_apprx_tanh, bias=fb1c[:, m:m + 1])
                i.then_inc(s["gel"], 1)

            def high_part(g):
                act.wait_ge(s["gel"], g + 1)
                if g < 2:
                    act.wait_ge(s["W2"], NT)
                    act.wait_ge(s["hlo"], NT)
                wait(act, s["F2c"], g - 1)
                A.activation(ht_hi[:, g % 2 * 4:g % 2 * 4 + 4, :].rearrange("p c f -> p (c f)"), duo(g),
                             ACT.Copy).then_inc(s["ghi"], 1)

            gathered(0)
            for q in range(NS):
                for d in range(DUOS):
                    if d == DUOS - 1 and q + 1 < NS:
                        gathered(q + 1)
                    gelu(q, d)
                    if q or d >= 2:
                        high_part(q * DUOS + d - 2)
            high_part(NS * DUOS - 2)
            high_part(NS * DUOS - 1)

        @block.vector
        def _(dve):
            link = Chain(dve, s["vset"], 40)
            V.memset(xn[LAST // 32 * 32:P, NT - 1, :], 0.0).then_inc(s["pad"], 1)
            dve.wait_ge(s["dst_in"], 16)
            link(V.tensor_copy(dlastf[:, :], dlast[:, :, ER - 1]))
            dve.wait_ge(s["eset"], 3)
            for k in range(EK):
                i = V.tensor_scalar(passed[:, k, :], win0[:, :], dlastf[:, k:k + 1], None, ALU.is_gt)
            i.then_inc(s["epass"], 1)

            def statistics_of(q):
                dve.wait_ge(s_x[q], 16 if q < 3 else 32)
                for c in range(CH * q, CH * (q + 1)):
                    i = V.bn_stats(stats[:, c, :], xn[:, c, :])
                if q in (0, 3):
                    lot = slice(0, CH) if q == 0 else slice(CH, NT)
                    link(i)
                    for c in range(lot.start, lot.stop):
                        i = V.bn_aggr(mv[:, c, :], stats[:, c, :])
                    link(i)
                    V.tensor_scalar(ve[:, lot], mv[:, lot, 1], EPS, None, ALU.add).then_inc(s["var"], 1)

            statistics_of(0)
            dve.wait_ge(s["cnt"], 1)
            V.tensor_scalar(gidx[:, :], pT[0][0:GW, 0:WG], float((E - RUN) // ER), None, ALU.min).then_inc(s["idx"], 1)
            dve.wait_ge(s["rstd"], 1)

            e_f = [e[:, :, :].bitcast(f32) for e in (e_a, e_b, e_c, e_d)]

            def sources():
                dve.wait_ge(s["gat"], 16 * 2 * WG)
                link(V.tensor_scalar(e_c[:, :, :], e_a[:, :, :], 7, None, ALU.logical_shift_right))
                link(V.tensor_scalar(e_d[:, :, :], e_a[:, :, :], P - 1, None, ALU.bitwise_and))

            def edge_keys():
                link(V.tensor_copy(e_f[0], e_d[:, :, :]))
                for g in range(WG):
                    i = V.tensor_scalar(e_f[3][:, g, :], e_b[:, g, :], float(NT), key0[:, g:g + 1], ALU.mult, ALU.add)
                link(i)

            def count_found():
                link(V.tensor_tensor(e_f[3], e_f[3], e_c[:, :, :], ALU.add))
                link(V.tensor_scalar(e_f[1], e_f[3], 0.0, None, ALU.is_ge))
                V.scalar_tensor_tensor(out=e_f[2].rearrange("p a b -> p (a b)"),
                                       in0=e_f[3].rearrange("p a b -> p (a b)"), scalar=float(KEYS),
                                       in1=e_f[1].rearrange("p a b -> p (a b)"),
                                       op0=ALU.is_lt, op1=ALU.mult, accum_out=cov[:, :]).then_inc(s["cov"], 1)
            def rest_of_statistics():
                statistics_of(2)
                statistics_of(3)
            between = {1: lambda: statistics_of(1), 2: rest_of_statistics, 3: sources, 4: edge_keys,
                       NT - 1: count_found}

            def qkv(st):
                if st.real():
                    t = st
                    xt = xn[:, bass.ds(t.i, 1), :].rearrange("p a f -> p (a f)")
                    m = mv[:, bass.ds(t.i, 1), 0:1].rearrange("p a f -> p (a f)")
                    r = rstd[:, bass.ds(t.i, 1)]
                    wait(dve, s["xT"], t.back(2).done())
                    V.tensor_scalar(xs[:, t.par, :], xt, m, r, ALU.subtract, ALU.mult).then_inc(s["xs_ready"], 1)
                    V.tensor_scalar(xt, xt, m, r, ALU.subtract, ALU.mult).then_inc(s["xn_ready"], 1)
                    if t.j is None and t.n == 4:
                        dve.wait_ge(s["rstd"], 2)
                t = st.back(3)
                if t.real():
                    dve.wait_ge(s["kexp"], t.done())
                    wait(dve, s["acc"], t.back(2).done())
                    V.scalar_tensor_tensor(out=kphi[:, t.par, :], in0=kb[:, :], scalar=0.0, in1=kexp[:, :],
                                           op0=ALU.max, op1=ALU.add).then_inc(s["kphi"], 1)
                    dve.wait_ge(s["qexp"], t.done())
                    if t.j is not None or t.n >= 2:
                        dve.wait_ge(s_sq[t.par], t.half * 16)
                    V.scalar_tensor_tensor(out=qp_s[:, t.par, :], in0=qb[:, :], scalar=0.0, in1=qexp[:, :],
                                           op0=ALU.max, op1=ALU.add).then_inc(s["qphi"], 1)
                t = st.back(2)
                if t.real():
                    if t.j is None and t.n == 0:
                        dve.wait_ge(s["rows_in"], 16)
                    dve.wait_ge(s["KV"], t.done())
                    wait(dve, s["kphi"], t.back(1).done())
                    V.tensor_tensor(kb[:, :], pKV[t.par][:, 0:D], row["bk"], ALU.add).then_inc(s["kc"], 1)
                    wait(dve, s["acc"], t.back(2).done())
                    V.tensor_tensor(vv[:, t.par, :, 0:P], pKV[t.par][:, D:2 * D].rearrange("p (k f) -> p k f", k=DK),
                                    row["bv"].rearrange("p (k f) -> p k f", k=DK), ALU.add).then_inc(s["kvb"], 1)
                    dve.wait_ge(s["kc"], t.done())
                    wait(dve, s["kexp"], t.back(1).done())
                    V.tensor_scalar(kmin[:, :], kb[:, :], 0.0, None, ALU.min).then_inc(s["kmin"], 1)
                    dve.wait_ge(s["qb"], t.done())
                    wait(dve, s["qexp"], t.back(1).done())
                    V.tensor_scalar(qmin[:, :], qb[:, :], 0.0, None, ALU.min).then_inc(s["qmin"], 1)
                if st.j is None and st.n in between:
                    between[st.n]()
            steps(dve, NT + 3, qkv)

            dve.wait_ge(s["acc"], NT)
            dve.wait_ge(s["const"], NCONST)
            for k in range(DK):
                V.tensor_tensor(kvm[:, k, 0:P], pAcc[k][:, 0:P], same_head[:, :], ALU.mult)
                i = V.tensor_copy(ksum[:, k:k + 1], pAcc[k][:, P:P + 1])
            link(i)
            for k in range(DK):
                i = V.tensor_scalar(kvm[:, k, P:CW], head_of[:, :], ksum[:, k:k + 1], None, ALU.mult)
            i.then_inc(s["kvm"], 1)

            dve.wait_ge(s["tot"], 1)
            link(V.tensor_scalar(covered[:, :], pQ[0][:, 0:1], float(E), None, ALU.is_equal))
            link(V.tensor_scalar(covered_m1[:, :], covered[:, :], -1.0, None, ALU.add))
            V.tensor_copy(flag[:, :], covered[:, :]).then_inc(s["flag"], 1)
            for b in range(3):
                dve.wait_ge(s["etr"], b + 1)
                out_, in_ = edge_columns(kcol, pK, b)
                i = V.tensor_scalar(out_, in_, covered[:, :], covered_m1[:, :], ALU.mult, ALU.add)
            link(i)
            assert link.n == VSET, link.n

            dve.wait_ge(s["flag"], 1)
            fast = dve.value_load(flag[0:1, 0:1], min_val=0, max_val=1)
            with dve.If(fast == 0):
                V.memset(dcol[:, :], 0.0).then_inc(s["sacc"], 1)
                dve.wait_ge(s["sacc"], 1)
                with dve.Fori(0, ET) as e:
                    dve.wait_ge(s["sdst"], (e + 1) * 16)
                    V.tensor_copy(dcol[:, :], didx[:, :]).then_inc(s["sc"], 1)
                    with dve.Fori(0, NT) as b:
                        n = e * (4 * NT + 1) + b * 4 + 1
                        dve.wait_ge(s["sc"], n)
                        V.tensor_scalar(oh_e[:, :], iota[:, 0:P, 0], dcol[:, :], None, ALU.is_equal).then_inc(s["soh"], 1)
                        dve.wait_ge(s["smm"], e * NT + b + 1)
                        ab = acc[:, bass.ds(b, 1), :].rearrange("p a f -> p (a f)")
                        db = dacc[:, bass.ds(b, 1)]
                        V.tensor_tensor(ab, pG[:, 0:D], ab, ALU.add).then_inc(s["sc"], 1)
                        dve.wait_ge(s["sc"], n + 1)
                        V.scalar_tensor_tensor(out=ab, in0=pG[:, D:2 * D], scalar=1 / LO, in1=ab, op0=ALU.mult,
                                               op1=ALU.add).then_inc(s["sc"], 1)
                        V.tensor_tensor(db, pN[:, 0:1], db, ALU.add).then_inc(s["sc"], 1)
                        V.tensor_scalar(dcol[:, :], dcol[:, :], -float(P), None, ALU.add).then_inc(s["sc"], 1)
                    dve.wait_ge(s["sc"], (e + 1) * (4 * NT + 1))
                    V.tensor_copy(dcol[:, :], didx[:, :]).then_inc(s["sacc"], 1)

            def one_hots(a, w):
                if w == 0:
                    bc = Chain(dve, s["blkc"], 1, a.i)
                    for n, c in enumerate((scol, kcol)):
                        i = V.tensor_copy(blk[:, a.par, n, :], c[:, bass.ds(a.i * (WPB * TPW), WPB * TPW)])
                    bc(i)
                if w >= OH or a.j is not None or a.n > 0:
                    dve.wait_ge(s["win"], a.i * UPB + w + 1 - OH)
                for c, (oh, n) in enumerate(((oh_s, P), (oh_k, KEYS))):
                    of_unit = blk[:, a.par, c, w * TPU:(w + 1) * TPU].rearrange("p (h j) -> p h j", h=2)
                    i = V.tensor_tensor(oh[:, w % OH, :, :, :],
                                        iota[:, 0:n, :].unsqueeze(1).broadcast_to([P, 2, n, TPH]),
                                        of_unit.unsqueeze(2).broadcast_to([P, 2, n, TPH]), ALU.is_equal)
                i.then_inc(s["oh"], 1)

            def heads_and_mean(t):
                lk = Chain(dve, s["atc"], 4, t.i)
                wait(dve, s["atm"], t.back(1).done())
                dve.wait_ge(s["num"], t.done())
                state = pN[:, 0:DK * CW].rearrange("p (k c) -> p k c", k=DK)
                V.tensor_tensor(deg[:, 0:1], pN[:, DK * CW:DK * CW + 1], dacc[:, bass.ds(t.i, 1)], ALU.add)
                lk(V.tensor_scalar(den[:, 0, :].rearrange("p (k h) -> p k h", k=DK), state[:, :, P:CW], 1e-6, None,
                                   ALU.add))
                V.tensor_scalar(deg[:, 1:2], deg[:, 0:1], 1.0, None, ALU.max)
                lk(V.reciprocal(den[:, 1, :], den[:, 0, :]))
                lk(V.reciprocal(deg[:, 2:3], deg[:, 1:2]))
                wait(dve, s["T1"], t.back(1).done())
                V.tensor_tensor(at_in[:, 2:4, :].rearrange("p k (h f) -> p k h f", h=HPC),
                                state[:, :, 0:P].rearrange("p k (h f) -> p k h f", h=HPC),
                                den[:, 1, :].rearrange("p (k h) -> p k h", k=DK).unsqueeze(3).broadcast_to(
                                    [P, DK, HPC, DH]), ALU.mult).then_inc(s["att"], 1)
                dve.wait_ge(s["agg"], t.done())
                lk(V.tensor_tensor(agg1[:, :], pG[:, 0:D], acc[:, bass.ds(t.i, 1), :].rearrange("p a f -> p (a f)"),
                                   ALU.add))
                V.scalar_tensor_tensor(out=agg1[:, :], in0=pG[:, D:2 * D], scalar=1 / LO, in1=agg1[:, :],
                                       op0=ALU.mult, op1=ALU.add).then_inc(s["aggr"], 1)

            def statistics(lk, n, r, out_sem):
                lk(V.bn_stats(bn[:, n, :], r), met=(s["kvm"], 1))
                lk(V.bn_aggr(mvs[:, n, :], bn[:, n, :]))
                V.tensor_scalar(ves[:, n:n + 1], mvs[:, n, 1:2], EPS, None, ALU.add).then_inc(out_sem, 1)

            def after_attention(t):
                lk = Chain(dve, s["ogc"], 3, t.i)
                dve.wait_ge(s["OG"], t.done())
                dve.wait_ge(s["xnb"], t.done())
                V.tensor_tensor(r1[:, :], pN[:, 0:D], xn[:, bass.ds(t.i, 1), :].rearrange("p a f -> p (a f)"),
                                ALU.add).then_inc(s["ogc"], 1)
                dve.wait_ge(s_xi[t.par], (t.half + 1) * 16)
                wait(dve, s["gxb"], t.back(1).done())
                V.tensor_tensor(gx[:, :], pN[:, D:2 * D], xin[:, t.par, :], ALU.add).then_inc(s["og"], 1)
                lk.n = 1
                dve.wait_ge(s["ogc"], lk.base + 1)
                statistics(lk, 0, r1[:, :], s["ve1"])

            def norm1(t):
                dve.wait_ge(s["r1"], t.done())
                wait(dve, s["x1"], t.back(1).done())
                V.tensor_scalar(x1a[:, :], r1[:, :], mvs[:, 0, 0:1], rs[:, 0:1], ALU.subtract, ALU.mult).then_inc(s["x1c"], 1)

            def after_ff(t):
                lk = Chain(dve, s["ln2c"], 2, t.i)
                dve.wait_ge(s["W2"], t.done())
                dve.wait_ge(s["x1b"], t.done())
                V.tensor_tensor(r2[:, :], pY[:, 0:D], x1b[:, :], ALU.add).then_inc(s["y1"], 1)
                dve.wait_ge(s["y1"], t.done())
                lk(V.bn_stats(bn[:, 1, :], r2[:, :]), met=(s["kvm"], 1))
                lk(V.bn_aggr(mvs[:, 1, :], bn[:, 1, :]))
                V.tensor_scalar(ves[:, 1:2], mvs[:, 1, 1:2], EPS, None, ALU.add).then_inc(s["ve2"], 1)

            def norm2(t):
                dve.wait_ge(s["r2"], t.done())
                wait(dve, s["x2"], t.back(1).done())
                V.tensor_scalar(z1[:, :], r2[:, :], mvs[:, 1, 0:1], rs[:, 1:2], ALU.subtract, ALU.mult).then_inc(s["z1"], 1)

            def stats3(t):
                lk = Chain(dve, s["ln3c"], 2, t.i)
                dve.wait_ge(s["x2"], t.done())
                statistics(lk, 2, x2[:, :], s["ve3"])

            def norm3(t):
                dve.wait_ge(s["r3"], t.done())
                wait(dve, s["base"], t.back(2).done())
                if t.j is not None or t.n >= 2:
                    dve.wait_ge(s_bs[t.par], t.half * 16)
                    dve.wait_ge(s_os[t.par], t.half * 16)
                V.tensor_scalar(xb[:, t.par, 0:D], x2[:, :], mvs[:, 2, 0:1], rs[:, 2:3], ALU.subtract, ALU.mult).then_inc(s["xn2"], 1)
                dve.wait_ge(s["xn2"], t.done())
                V.tensor_tensor_reduce(out=yb[:, :], in0=xb[:, t.par, 0:D], in1=row["wr"], scale=1.0, scalar=0.0,
                                       op0=ALU.mult, op1=ALU.add, accum_out=wraw[:, :]).then_inc(s["wsum"], 1)
                dve.wait_ge(s["wsum"], t.done())
                V.tensor_tensor(wall[:, bass.ds(t.i, 1)], wraw[:, :], br, ALU.add).then_inc(s["w"], 1)

            def compare(c):
                lo, hi = c * P, c * P + P
                if c == 0:
                    dve.wait_ge(s["wrow"], 16)
                wait(dve, s["beaten"], c - 1)
                wait(dve, s["ranked"], c - 1)
                me = wall[:, c:c + 1]
                i = V.scalar_tensor_tensor(out=beats1[:, c % 2, lo:hi], in0=wrow[:, lo:hi], scalar=me,
                                           in1=later[:, :], op0=ALU.is_le, op1=ALU.mult)
                if hi < EN:
                    i = V.tensor_scalar(beats1[:, c % 2, hi:EN], wrow[:, hi:EN], me, None, ALU.is_le)
                i.then_inc(s["beats"], 1)

            def compare_last(c):
                r = min(P, N - c * P)
                wait(dve, s["beaten"], min(ET1 + c - 3, ET1 + BY_ACT))
                wait(dve, s["ranked"], ET1 + c - 3)
                me = wall[0:r, c:c + 1]
                lo = max(c * P, EN)
                if c >= ET1:
                    i = V.scalar_tensor_tensor(out=beats2[0:r, c % 4, lo - EN:lo - EN + r], in0=wrow[0:r, lo:lo + r],
                                               scalar=me, in1=later[0:r, 0:r], op0=ALU.is_le, op1=ALU.mult,
                                               accum_out=ahead[0:r, 2, c:c + 1])
                    lo += r
                if c < BY_ACT:
                    i = V.tensor_scalar(beats2[:, c % 4, lo - EN:N - EN], wrow[:, lo:N], me, None, ALU.is_le)
                elif lo < N:
                    i = V.tensor_scalar(beats2[:, c % 4, lo - EN:N - EN], wrow[:, lo:N], me, None, ALU.is_le, ALU.add,
                                        accum_out=ahead[:, 1, c:c + 1])
                i.then_inc(s["beats"], 1)

            def mix(st):
                a, t1, t2, t3 = st, st.back(1), st.back(2), st.back(3)
                step = st.n if st.j is None else None
                if step == NT:
                    dve.wait_ge(s["wt"], 1)
                    V.tensor_copy(wt1[:, :], bank[1][0:ET1, 0:P]).then_inc(s["wtc"], 1)
                if t1.real():
                    heads_and_mean(t1)
                if a.real():
                    one_hots(a, 3)
                if t3.real():
                    stats3(t3)
                if a.real():
                    one_hots(a, 4)
                if t3.real():
                    norm3(t3)
                if a.real():
                    for w in range(5, UPB):
                        one_hots(a, w)
                if t1.real():
                    after_attention(t1)
                    norm1(t1)
                if step == NT:
                    compare(0)
                    compare(1)
                if step == NT + 1:
                    compare(3)
                if t2.real():
                    after_ff(t2)
                b = st.back(-1)
                if b.real():
                    one_hots(b, 0)
                if t2.real():
                    norm2(t2)
                if b.real():
                    one_hots(b, 1)
                    one_hots(b, 2)
                if step == NT:
                    compare(2)
                if step == NT + 1:
                    compare(4)
            dve.wait_ge(s["scop"], 3)
            dve.wait_ge(s["rows2_in"], 16)
            first_block = Tile(0)
            for w in range(3):
                one_hots(first_block, w)
            steps(dve, NT + 3, mix)

            dve.wait_ge(s["wt"], 2)
            V.tensor_copy(wt2[:, :], bank[1][0:NT - ET1, P:2 * P]).then_inc(s["wtc"], 1)
            for c in range(5, ET1):
                compare(c)
            V.memset(beats2[:, :, N - EN:NT * P - EN], 0.0)
            dve.wait_ge(s["wrow"], 32)
            for c in range(NT):
                compare_last(c)
            rl = Chain(dve, s["rank"], 4)
            dve.wait_ge(s["beaten"], ET1 + BY_ACT)
            dve.wait_ge(s["beats"], ET1 + NT)
            rl(V.tensor_tensor(ahead[:, 3, :], ahead[:, 0, :], ahead[:, 1, :], ALU.add))
            rl(V.tensor_tensor(ahead[:, 3, :], ahead[:, 3, :], ahead[:, 2, :], ALU.add))
            rl(V.tensor_tensor(rank[:, :], n_later[:, :], ahead[:, 3, :], ALU.subtract))
            dve.wait_ge(s["ranked"], ET1 + NT)
            rl(V.tensor_tensor(rank[:, :], rank[:, :], bank[0][:, 0:NT], ALU.add))
            dve.wait_ge(s["num"], NT)
            ri = Chain(dve, s["rint"], 4)
            ri(V.tensor_scalar(ranki[:, 0, :], rank[:, :], 0.0, None, ALU.max))
            V.tensor_scalar(ranki[:, 1, :], ranki[:, 0, :], P - 1, None, ALU.bitwise_and)
            ri(V.tensor_scalar(ranki[:, 2, :], ranki[:, 0, :], 7, None, ALU.logical_shift_right))
            ri(V.tensor_copy(rankh[:, :, :], ranki[:, 1:3, :]))
            V.tensor_tensor(oh_r[:, :, :, :], iota[:, :, :].unsqueeze(1).broadcast_to([P, NT // TPH, P, TPH]),
                            rankh[:, 0, :].rearrange("p (g j) -> p g j", j=TPH).unsqueeze(2).broadcast_to(
                                [P, NT // TPH, P, TPH]), ALU.is_equal)
            ri(V.tensor_tensor(oh_b[:, :, :], iota_b[:, :].unsqueeze(1).broadcast_to([P, NT, 2 * NS]),
                               rankh[:, 1, :].unsqueeze(2).broadcast_to([P, NT, 2 * NS]), ALU.is_equal))
            V.tensor_tensor(tok_b[:, :, :, :], oh_b[:, :, :].unsqueeze(2).broadcast_to([P, NT, 2, 2 * NS]),
                            tok[:, :, :].unsqueeze(3).broadcast_to([P, NT, 2, 2 * NS]), ALU.mult).then_inc(s["ohb"], 1)
            dve.wait_ge(s["picked"], 1)
            sl = Chain(dve, s["sidc"], 2)
            sl(V.tensor_copy(stok[:, :, :].rearrange("p a b -> p (a b)"), pY[:, 0:4 * NS]))
            sl(V.scalar_tensor_tensor(out=sidf[:, :], in0=stok[:, 1, :], scalar=float(P), in1=stok[:, 0, :],
                                      op0=ALU.mult, op1=ALU.add))
            V.tensor_scalar(sid[:, :], sidf[:, :], float(N - 1), None, ALU.min).then_inc(s["sids"], 1)

            def low_part(g):
                dve.wait_ge(s["ghi"], g + 1)
                slot = slice(g % 2 * 4, g % 2 * 4 + 4)
                V.tensor_tensor(ht_lo[:, slot, :].rearrange("p c f -> p (c f)"), duo(g),
                                ht_hi[:, slot, :].bitcast(f32).rearrange("p c f -> p (c f)"),
                                ALU.subtract).then_inc(s["glo"], 1)

            def routing_weights(q):
                wk = Chain(dve, s["wsc"], 1, q)
                dve.wait_ge(s_gx[q], 32)
                wait(dve, s["yo"], 2 * q)
                for u in range(2):
                    if u:
                        dve.wait_ge(s["ybj"], 2 * q + 1)
                    i = V.tensor_tensor_reduce(out=yb[:, :], in0=gx2[:, 2 * q + u, 0:D], in1=row["wr"], scale=1.0,
                                               scalar=0.0, op0=ALU.mult, op1=ALU.add, accum_out=ws[:, 0, u:u + 1])
                    i.then_inc(s["ybj"], 1)
                dve.wait_ge(s["ybj"], 2 * q + 2)
                wk(V.tensor_scalar(ws[:, 1, :], ws[:, 0, :], br, None, ALU.add))

            def out_bias(q):
                dve.wait_ge(s["F2c"], (q + 1) * DUOS)
                for u in range(2):
                    wait(dve, s_sc[u], 16 * q)
                    V.tensor_tensor(yo[:, u, :], pR[u][:, 0:D], row["fb2"], ALU.add).then_inc(s["yoc"], 1)

            def routed_out(q):
                for u in range(2):
                    c = 2 * q + u
                    dve.wait_ge(s["yoc"], c + 1)
                    V.scalar_tensor_tensor(out=yo[:, u, :], in0=yo[:, u, :], scalar=ws[:, 1, u:u + 1],
                                           in1=gx2[:, c, D:2 * D], op0=ALU.mult, op1=ALU.add).then_inc(s["yo"], 1)

            for q in range(NS + 1):
                if q < NS:
                    low_part(q * DUOS)
                if q:
                    out_bias(q - 1)
                if q < NS:
                    low_part(q * DUOS + 1)
                if q:
                    routed_out(q - 1)
                if q < NS:
                    low_part(q * DUOS + 2)
                    routing_weights(q)
                    low_part(q * DUOS + 3)

        @block.tensor
        def _(pe):
            pe.wait_ge(s["epass"], 1)
            for g in range(WG):
                for k in range(EK):
                    i = T.matmul(pT[0][0:GW, g:g + 1], passed[:, k, g * GW:(g + 1) * GW], one16[0:EP, :],
                                 start=(k == 0), stop=(k == EK - 1))
            i.then_inc(s["cnt"], 1)
            pe.wait_ge(s["idx"], 1)
            pe.wait_ge(s["const"], 5)
            pe.wait_ge(s["wkv_in"], 32)
            pe.wait_ge(s["wq_in"], 16)

            def transpose_edges(b):
                for g in range(2 * b, min(2 * b + 2, WG)):
                    for j in range(TPW):
                        for bk, e in ((pS[b], e_a), (pK[b], e_d)):
                            col = (g % 2 * TPW + j) * GW
                            i = T.transpose(bk[:, col:col + GW], e[:, g, j * P:(j + 1) * P].bitcast(f32),
                                            ident[0:GW, 0:GW])
                i.then_inc(s["etr"], 1)

            def edges_found():
                pe.wait_ge(s["cov"], 1)
                pe.wait_ge(s["const"], NCONST)
                pe.wait_ge(s["qb"], NT)
                pe.wait_ge(s["kvb"], NT)
                T.matmul(pQ[0][:, 0:1], ones[0:GW, :], cov[:, :], start=True, stop=True).then_inc(s["tot"], 1)
                transpose_edges(0)
                transpose_edges(1)

            def qkv(st):
                if st.j is None and st.n == NT + 2:
                    edges_found()
                t = st.back(1)
                if t.real():
                    pe.wait_ge(s["xs_ready"], t.done())
                    wait(pe, s["xTc"], t.back(2).done())
                    for k in range(DK):
                        i = T.transpose(pT[t.par][:, k * P:(k + 1) * P], xs[:, t.par, k * P:(k + 1) * P], ident[:, :])
                    i.then_inc(s["xT"], 1)
                t = st.back(2)
                if t.real():
                    pe.wait_ge(s["xTc"], t.done())
                    wait(pe, s["kvb"], t.back(2).done())
                    for k in range(DK):
                        i = T.matmul(pKV[t.par][:, :], xt_s[:, t.par, k * P:(k + 1) * P], wkv[:, k, :],
                                     start=(k == 0), stop=(k == DK - 1))
                    i.then_inc(s["KV"], 1)
                    wait(pe, s["qb"], t.back(2).done())
                    for m in range(DK):
                        for k in range(DK):
                            i = T.matmul(pQ[t.par][:, m * P:(m + 1) * P], wq[:, k, m * P:(m + 1) * P],
                                         xt_s[:, t.par, k * P:(k + 1) * P], start=(k == 0), stop=(k == DK - 1))
                    i.then_inc(s["Q"], 1)
                t = st.back(3)
                if t.real():
                    r = LAST if t.j is None and t.n == NT - 1 else P
                    pe.wait_ge(s["kphi"], t.done())
                    for k in range(DK):
                        i = T.matmul(pAcc[k][:, 0:P + 1], kphi[0:r, t.par, k * P:(k + 1) * P], vv[0:r, t.par, k, :],
                                     start=(t.j is None and t.n == 0), stop=(t.j is None and t.n == NT - 1))
                    i.then_inc(s["acc"], 1)
            steps(pe, NT + 3, qkv)
            pe.wait_ge(s["flag"], 1)
            transpose_edges(2)

            pe.wait_ge(s["scop"], 3)
            pe.wait_ge(s["vset"], VSET)
            pe.wait_ge(s["flag"], 1)
            fast = pe.value_load(flag[0:1, 0:1], min_val=0, max_val=1)
            with pe.If(fast == 0):
                with pe.Fori(0, ET) as e:
                    wait_apart(pe, s["sg"], (e + 1) * 16, (s["flag"], 1))
                    with pe.Fori(0, NT) as b:
                        pe.wait_ge(s["soh"], e * NT + b + 1)
                        T.matmul(pG[:, :], oh_e[:, :], msg[:, :], start=True, stop=True)
                        T.matmul(pN[:, 0:1], oh_e[:, :], one16[:, :], start=True, stop=True).then_inc(s["smm"], 1)

            pe.wait_ge(s["w_in"], 16 * 4)
            pe.wait_ge(s["kvm"], 1)
            pe.wait_ge(s["x16"], NT)

            def window(a, w):
                pe.wait_ge(s["oh"], a.i * UPB + w + 1)
                if w >= 2 or a.j is not None or a.n > 0:
                    pe.wait_ge(s["Aev"], a.i * UPB + w - 1)
                for v in range(WPU):
                    for j in range(TPW):
                        h, e = divmod(v * TPW + j, TPH)
                        i = T.matmul(pW[w % 2][:, v * KEYS:(v + 1) * KEYS], oh_s[:, w % OH, h, :, e],
                                     oh_k[:, w % OH, h, :, e], start=(j == 0), stop=(j == TPW - 1))
                i.then_inc(s["win"], 1)

            def add_beats(lot, c):
                r = min(P, N - c * P)
                pe.wait_ge(s["beats"], lot * ET1 + c + 1)
                for b in range(max(c, ET1 * lot), (ET1, NT)[lot]):
                    lhs = beats2[0:r, c % 4, (b - ET1) * P:(b - ET1 + 1) * P] if lot else beats1[:, c % 2, b * P:(b + 1) * P]
                    i = T.matmul(bank[0][:, b:b + 1], lhs, one16[0:r, :], start=(lot == 0 and c == 0 and b == 0),
                                 stop=(lot == 1 and c == NT - 1))
                i.then_inc(s["ranked"], 1)

            def to_hidden(w_sb, xt, out_sem):
                for m in range(HK):
                    for k in range(DK):
                        i = T.matmul(pH[m // 4][:, (m % 4) * P:(m % 4 + 1) * P], w_sb[:, k, m * P:(m + 1) * P],
                                     xt[:, k, :], start=(k == 0), stop=(k == DK - 1))
                    if m % 4 == 3:
                        i.then_inc(out_sem, 1)

            def from_hidden_high(t):
                pe.wait_ge(s["w2s"], 1)
                pe.wait_ge(s["hhi"], t.done())
                for m in range(HK):
                    T.matmul(pY[:, 0:D], ht_hi[:, m, :], w2_hi[:, m, :], start=(m == 0), stop=False)
                    T.matmul(pY[:, 0:D], ht_hi[:, m, :], w2_lo[:, m, :], start=False, stop=False)

            def from_hidden_low(t):
                pe.wait_ge(s["hlo"], t.done())
                for m in range(HK):
                    i = T.matmul(pY[:, 0:D], ht_lo[:, m, :], w2_hi[:, m, :], start=False, stop=(m == HK - 1))
                i.then_inc(s["W2"], 1)

            def mix(st):
                a, t1, t2 = st, st.back(1), st.back(2)
                if t2.real():
                    pe.wait_ge(s["x1"], t2.done())
                    wait(pe, s["T1c"], t2.done())
                    for k in range(DK):
                        i = T.transpose(pX[:, k * P:(k + 1) * P], x1[:, t2.par, k * P:(k + 1) * P], ident[:, :])
                    i.then_inc(s["T2"], 1)
                if a.real():
                    window(a, 0)
                    window(a, 1)
                if t2.real():
                    pe.wait_ge(s["T2c"], t2.done())
                    wait(pe, s["rel"], t2.back(1).done(2))
                    to_hidden(w1, x1t, s["W1"])
                if st.j is None and st.n == NT + 1:
                    add_beats(0, 0)
                    add_beats(0, 1)
                if t1.real():
                    pe.wait_ge(s["att"], t1.done())
                    pe.wait_ge(s["atm"], t1.done())
                    wait(pe, s["T2c"], t1.back(1).done())
                    for k in range(4):
                        i = T.transpose(pX[:, k * P:(k + 1) * P], at_in[:, k, :], ident[:, :])
                    i.then_inc(s["T1"], 1)
                if a.real():
                    window(a, 2)
                    window(a, 3)
                if t1.real():
                    pe.wait_ge(s_xt[t1.par], (t1.half + 1) * 16)
                    for k in range(DK):
                        T.matmul(pN[:, D:2 * D], xts[:, t1.par, k * P:(k + 1) * P], wrr[:, k, :], start=(k == 0),
                                 stop=False)
                    pe.wait_ge(s["T1c"], t1.done())
                    for k in range(DK):
                        T.matmul(pN[:, D:2 * D], at_t[:, k, :], wl[:, k, :], start=False, stop=(k == DK - 1))
                    for k in range(DK):
                        i = T.matmul(pN[:, 0:D], at_t[:, 2 + k, :], wo[:, k, :], start=(k == 0), stop=(k == DK - 1))
                    i.then_inc(s["OG"], 1)
                if a.real():
                    window(a, 4)
                    window(a, 5)
                if t2.real():
                    wait(pe, s["y1"], t2.back(1).done())
                    from_hidden_high(t2)
                if a.real():
                    window(a, 6)
                    window(a, 7)
                    wait(pe, s["og"], a.back(1).done())
                    pe.wait_ge(s_q[a.par], (a.half + 1) * 16)
                    for k in range(DK):
                        T.matmul(pN[:, k * CW:(k + 1) * CW], qs[:, a.par, k * P:(k + 1) * P], kvm[:, k, :],
                                 start=True, stop=True)
                if t2.real():
                    from_hidden_low(t2)
                if a.real():
                    pe.wait_ge(s["Aev"], a.i * UPB + UPB)
                    if a.j is None and a.n == NT - 1:
                        pe.wait_ge(s["w"], ET1)
                        T.transpose(bank[1][0:ET1, 0:P], wall[:, 0:ET1], ident[:, :]).then_inc(s["wt"], 1)
                    wait(pe, s["aggr"], a.back(1).done())
                    for c in range(NT):
                        i = T.matmul(pG[:, :], adj[:, a.par, c, :], xn16[:, c, :], start=(c == 0), stop=(c == NT - 1))
                    i.then_inc(s["agg"], 1)
                    for c in range(NT):
                        i = T.matmul(pN[:, DK * CW:DK * CW + 1], adj[:, a.par, c, :], one16[:, :], start=(c == 0),
                                     stop=(c == NT - 1))
                    i.then_inc(s["num"], 1)
            steps(pe, NT + 2, mix)
            for c in range(2, 5):
                add_beats(0, c)
            pe.wait_ge(s["w"], NT)
            pe.wait_ge(s["wtc"], 1)
            T.transpose(bank[1][0:NT - ET1, P:2 * P], wall[:, ET1:NT], ident[:, :]).then_inc(s["wt"], 1)
            for c in range(5, ET1):
                add_beats(0, c)
            for c in range(NT):
                add_beats(1, c)
            pe.wait_ge(s["y1"], NT)
            pe.wait_ge(s["ohb"], 1)
            for c in range(NT):
                r = min(P, N - c * P)
                i = T.matmul(pY[:, 0:4 * NS], oh_r[0:r, c // TPH, :, c % TPH],
                             tok_b[0:r, c, :, :].rearrange("p a b -> p (a b)"), start=(c == 0), stop=(c == NT - 1))
            i.then_inc(s["picked"], 1)

            pe.wait_ge(s["wtc"], 2)
            pe.wait_ge(s["rank"], 4)
            pe.wait_ge(s["T1c"], NT)
            pe.wait_ge(s["T2c"], NT)
            pe.wait_ge(s["sidc"], 1)
            pe.wait_ge(s["Aev"], NT * UPB)
            pe.wait_ge(s["rel"], NT * 2)
            pe.wait_ge(s["aggr"], NT)
            pe.wait_ge(s["f_in"], 16 * 2)

            def gathered(q):
                pe.wait_ge(s_gx[q], 32)
                wait(pe, s["T3c"], q)
                for k in range(DK):
                    for u in range(2):
                        i = T.transpose(pX[:, (k * 2 + u) * P:(k * 2 + u + 1) * P],
                                        gx2[:, 2 * q + u, k * P:(k + 1) * P], ident[:, :])
                i.then_inc(s["T3"], 1)

            def first_layer(q, d):
                if d == 0:
                    pe.wait_ge(s["T3c"], q + 1)
                wait(pe, s["gel"], (q - 1) * DUOS + d + 1)
                for m in range(2 * d, 2 * d + 2):
                    for k in range(DK):
                        i = T.matmul(pF[d][:, m % 2 * 2 * P:(m % 2 + 1) * 2 * P], f1[:, k, m * P:(m + 1) * P],
                                     x2t[:, k, :], start=(k == 0), stop=(k == DK - 1))
                i.then_inc(s["F1"], 1)

            def second_layer(q, d):
                g = q * DUOS + d
                pe.wait_ge(s["ghi"], g + 1)
                for u in range(2):
                    if d == 0:
                        wait(pe, s["yoc"], 2 * (q - 1) + u + 1)
                    for j in range(2):
                        high = ht_hi[:, part_of(g, j, u), :]
                        T.matmul(pR[u][:, 0:D], high, w2_hi[:, 2 * d + j, :], start=(d == 0 and j == 0), stop=False)
                        T.matmul(pR[u][:, 0:D], high, w2_lo[:, 2 * d + j, :], start=False, stop=False)
                pe.wait_ge(s["glo"], g + 1)
                for u in range(2):
                    for j in range(2):
                        i = T.matmul(pR[u][:, 0:D], ht_lo[:, part_of(g, j, u), :], w2_hi[:, 2 * d + j, :],
                                     start=False, stop=(d == DUOS - 1 and j == 1))
                i.then_inc(s["F2c"], 1)

            gathered(0)
            for q in range(NS):
                for d in range(DUOS):
                    first_layer(q, d)
                    if d == DUOS - 1 and q + 1 < NS:
                        gathered(q + 1)
                    if q == 0 and d == 0:
                        pe.wait_ge(s["f2s"], 1)
                    if q:
                        second_layer(q - 1, d)
            for d in range(DUOS):
                second_layer(NS - 1, d)


def kernel(**inputs):
    import numpy as np
    import concourse.bacc as bacc
    from concourse.bass_utils import run_bass_kernel_spmd

    a = {k: np.asarray(v) for k, v in inputs.items()}
    m = {k[7:]: v for k, v in a.items() if k.startswith("L0_mix_")}
    g = {k[7:]: v for k, v in a.items() if k.startswith("L0_gnn_")}
    f = {k[7:]: v for k, v in a.items() if k.startswith("L0_ffn_")}
    rows = [m["bk"], m["bv"], m["bo"], m["ln1_g"], m["ln1_b"], m["b2"], m["ln2_g"], m["ln2_b"], g["b_r"],
            f["wr"].reshape(-1), f["b2"], f["br"].reshape(-1)]
    cols = [m["bq"].reshape(-1, P).T, m["b1"].reshape(-1, P).T, f["b1"].reshape(-1, P).T]
    given = [
        ("x", a["x"]), ("src", a["src"]), ("dst", a["dst"]), ("w_l", g["W_l"].T), ("w_r", g["W_r"].T),
        ("w_q", m["Wq"]), ("w_k", m["Wk"]), ("w_v", m["Wv"]), ("w_o", m["Wo"]), ("w_1", m["W1"]), ("w_2", m["W2"]),
        ("f_1", f["w1"]), ("f_2", f["w2"]), ("rows", np.concatenate(rows)), ("cols", np.concatenate(cols, axis=1)),
    ]
    nc = bacc.Bacc("TRN2", target_bir_lowering=False, num_devices=1)
    arrays, args = {}, []
    for name, v in given:
        v = np.ascontiguousarray(v)
        arrays["in_" + name] = v
        args.append(nc.dram_tensor("in_" + name, v.shape, mybir.dt.from_np(v.dtype), kind="ExternalInput").ap())
    args.append(nc.dram_tensor("out_0", (N, D), mybir.dt.float32, kind="ExternalOutput").ap())
    args.append(nc.dram_tensor("xq_d", (NT, P, 2 * D), mybir.dt.float32, kind="Internal").ap())
    args.append(nc.dram_tensor("xg_d", (NT * P, 2 * D), mybir.dt.float16, kind="Internal").ap())
    args.append(nc.dram_tensor("w_d", (NT * P,), mybir.dt.float32, kind="Internal").ap())
    args.append(nc.dram_tensor("xb_d", (NT * P, 2 * D), mybir.dt.float32, kind="Internal").ap())
    gps_layer(nc, *args)
    r = run_bass_kernel_spmd(nc, [arrays], core_ids=[0])
    return r.results[0]["out_0"]
```
